# Optimizing a Trainium2 kernel written in Bass

```python
import numpy as np
import jax
import jax.numpy as jnp

def _softmax(x, axis=-1):
    return jax.nn.softmax(x, axis=axis)

def _gelu(x):
    return jax.nn.gelu(x, approximate=True)

def _silu(x):
    return jax.nn.silu(x)

def _sigmoid(x):
    return jax.nn.sigmoid(x)

def _layernorm(x, axis=-1, eps=1e-05):
    m = jnp.mean(x, axis=axis, keepdims=True)
    v = jnp.var(x, axis=axis, keepdims=True)
    return (x - m) / jnp.sqrt(v + eps)

def _scatter_add(tgt, idx, src, axis=0):
    return tgt.at[idx].add(src)

def _segment_sum(src, seg, n):
    return jax.ops.segment_sum(src, seg, n)
kernel_name = 'mk_gnn_resnorm_d4_gnn_r8_ad32a9'

def setup_inputs(seed: int=0):
    np.random.seed(seed)
    _w = jnp.asarray

    def _rec_inputs():
        import jax
        import jax.numpy as jnp
        _gk = jax.random.key(seed)
        x = -0.0003713 + 1 * jax.random.normal(jax.random.fold_in(_gk, 1), (6250, 256), jnp.float32)
        src = jax.random.randint(jax.random.fold_in(_gk, 2), (100000,), 0, 6250, jnp.int32)
        dst = jnp.minimum((6250 * jax.random.uniform(jax.random.fold_in(_gk, 3), (100000,)) ** 2.0).astype(jnp.int32), 49999)
        _o = jnp.argsort(dst, stable=True)
        src = src[_o]
        dst = dst[_o]
        edge_type_8 = jax.random.randint(jax.random.fold_in(_gk, 13), (100000,), 0, 8, jnp.int32)
        return (x, src, dst, edge_type_8)
    x, src, dst, edge_type_8 = _rec_inputs()

    def _L0_gnn_setup():
        import jax, jax.numpy as jnp
        import numpy as np
        N_NODES = 6250
        N_EDGES = 100000
        IN_FEAT = 256
        OUT_FEAT = 256
        NUM_RELS = 8
        ALPHA = 0.5
        key = jax.random.key(seed)
        k1, k2, k3, k4, k5, k6 = jax.random.split(key, 6)
        x = jax.random.normal(k1, (N_NODES, IN_FEAT), dtype=jnp.float32)
        edge_index = jax.random.randint(k2, (2, N_EDGES), 0, N_NODES, dtype=jnp.int64)
        edge_type = jax.random.randint(k3, (N_EDGES,), 0, NUM_RELS, dtype=jnp.int64)
        gain = float(np.sqrt(2.0))
        lim_w = gain * float(np.sqrt(6.0 / (IN_FEAT + OUT_FEAT)))
        weight = jax.random.uniform(k4, (NUM_RELS, IN_FEAT, OUT_FEAT), dtype=jnp.float32, minval=-lim_w, maxval=lim_w)
        loop_weight = jax.random.uniform(k5, (IN_FEAT, OUT_FEAT), dtype=jnp.float32, minval=-lim_w, maxval=lim_w)
        h_bias = jnp.zeros((OUT_FEAT,), dtype=jnp.float32)
        return {'edge_index': edge_index, 'x': x, 'edge_type': edge_type, 'weight': weight, 'h_bias': h_bias, 'loop_weight': loop_weight}
    _L0_gnn_all = _L0_gnn_setup()
    _L0_gnn_in = {k: v for k, v in _L0_gnn_all.items() if k in ('weight', 'h_bias', 'loop_weight')}
    del _L0_gnn_all

    def _L1_gnn_setup():
        import jax, jax.numpy as jnp
        import numpy as np
        N_NODES = 6250
        N_EDGES = 100000
        D_IN = 256
        D_OUT = 256
        BN_EPS = 1e-05
        L2_EPS = 1e-12
        key = jax.random.key(seed)
        ks = jax.random.split(key, 8)
        x = jax.random.normal(ks[0], (N_NODES, D_IN), dtype=jnp.float32)
        edge_index = jax.random.randint(ks[1], (2, N_EDGES), 0, N_NODES, dtype=jnp.int64)
        s = 1.0 / np.sqrt(D_IN)
        W_l = jax.random.uniform(ks[2], (D_OUT, D_IN), jnp.float32, -s, s)
        b_l = jax.random.uniform(ks[3], (D_OUT,), jnp.float32, -s, s)
        W_r = jax.random.uniform(ks[4], (D_OUT, D_IN), jnp.float32, -s, s)
        gamma = jnp.ones((D_OUT,), jnp.float32)
        beta = jnp.zeros((D_OUT,), jnp.float32)
        return {'x': x, 'edge_index': edge_index, 'W_l': W_l, 'b_l': b_l, 'W_r': W_r, 'gamma': gamma, 'beta': beta}
    _L1_gnn_all = _L1_gnn_setup()
    _L1_gnn_in = {k: v for k, v in _L1_gnn_all.items() if k in ('W_l', 'b_l', 'W_r', 'gamma', 'beta')}
    del _L1_gnn_all

    def _L2_gnn_setup():
        import jax, jax.numpy as jnp
        import numpy as np
        N_NODES = 6250
        NEG_SLOPE = 0.2

        def _gat_layer(h, W, al, ar, src, dst, residual):
            N = h.shape[0]
            H, D = al.shape
            feat = (h @ W).reshape(N, H, D)
            el = jnp.sum(feat * al[None], axis=-1)
            er = jnp.sum(feat * ar[None], axis=-1)
            e = jax.nn.leaky_relu(el[src] + er[dst], NEG_SLOPE)
            m = jax.ops.segment_max(e, dst, num_segments=N)
            m = jnp.where(jnp.isfinite(m), m, jnp.zeros_like(m))
            ex = jnp.exp(e - m[dst])
            den = jax.ops.segment_sum(ex, dst, num_segments=N)
            a = ex / jnp.maximum(den[dst], jnp.asarray(1e-09, ex.dtype))
            msg = a[:, :, None] * feat[src]
            out = jax.ops.segment_sum(msg, dst, num_segments=N)
            if residual:
                out = out + h.reshape(N, H, D)
            out = jax.nn.relu(out)
            return out.reshape(N, H * D)
        key = jax.random.key(seed)
        ks = jax.random.split(key, 12)
        N, E, F_IN, H, D = (N_NODES, 50000, 256, 4, 64)
        s = 1.0 / np.sqrt(F_IN)
        inp = {'x': jax.random.normal(ks[0], (N, F_IN), dtype=jnp.float32), 'src': jax.random.randint(ks[1], (E,), 0, N, dtype=jnp.int32), 'dst': jax.random.randint(ks[2], (E,), 0, N, dtype=jnp.int32)}
        for i in range(3):
            inp[f'W{i}'] = jax.random.normal(ks[3 + 3 * i], (F_IN, H * D), dtype=jnp.float32) * s
            inp[f'al{i}'] = jax.random.normal(ks[4 + 3 * i], (H, D), dtype=jnp.float32) * s
            inp[f'ar{i}'] = jax.random.normal(ks[5 + 3 * i], (H, D), dtype=jnp.float32) * s
        return inp
    _L2_gnn_all = _L2_gnn_setup()
    _L2_gnn_in = {k: v for k, v in _L2_gnn_all.items() if k in ('W0', 'al0', 'ar0', 'W1', 'al1', 'ar1', 'W2', 'al2', 'ar2')}
    del _L2_gnn_all

    def _L3_gnn_setup():
        import jax, jax.numpy as jnp
        import numpy as np
        N_NODES = 6250
        key = jax.random.key(seed)
        k1, k2, k3 = jax.random.split(key, 3)
        x = jax.random.normal(k1, (N_NODES, 256), dtype=jnp.float32)
        W = jax.random.normal(k2, (256, 256), dtype=jnp.float32) * (1.0 / np.sqrt(256))
        edge_index = jax.random.randint(k3, (2, 200000), 0, N_NODES, dtype=jnp.int64)
        return {'x': x, 'W': W, 'edge_index': edge_index}
    _L3_gnn_all = _L3_gnn_setup()
    _L3_gnn_in = {k: v for k, v in _L3_gnn_all.items() if k in ('W',)}
    del _L3_gnn_all
    return {'x': x, 'src': src, 'dst': dst, 'edge_type_8': edge_type_8, 'L0_gnn_weight': _L0_gnn_in['weight'], 'L0_gnn_h_bias': _L0_gnn_in['h_bias'], 'L0_gnn_loop_weight': _L0_gnn_in['loop_weight'], 'L1_gnn_W_l': _L1_gnn_in['W_l'], 'L1_gnn_b_l': _L1_gnn_in['b_l'], 'L1_gnn_W_r': _L1_gnn_in['W_r'], 'L1_gnn_gamma': _L1_gnn_in['gamma'], 'L1_gnn_beta': _L1_gnn_in['beta'], 'L2_gnn_W0': _L2_gnn_in['W0'], 'L2_gnn_al0': _L2_gnn_in['al0'], 'L2_gnn_ar0': _L2_gnn_in['ar0'], 'L2_gnn_W1': _L2_gnn_in['W1'], 'L2_gnn_al1': _L2_gnn_in['al1'], 'L2_gnn_ar1': _L2_gnn_in['ar1'], 'L2_gnn_W2': _L2_gnn_in['W2'], 'L2_gnn_al2': _L2_gnn_in['al2'], 'L2_gnn_ar2': _L2_gnn_in['ar2'], 'L3_gnn_W': _L3_gnn_in['W']}

def reference(x, src, dst, edge_type_8, L0_gnn_weight, L0_gnn_h_bias, L0_gnn_loop_weight, L1_gnn_W_l, L1_gnn_b_l, L1_gnn_W_r, L1_gnn_gamma, L1_gnn_beta, L2_gnn_W0, L2_gnn_al0, L2_gnn_ar0, L2_gnn_W1, L2_gnn_al1, L2_gnn_ar1, L2_gnn_W2, L2_gnn_al2, L2_gnn_ar2, L3_gnn_W):
    import jax
    import jax.numpy as jnp

    def _L0_gnn_ref(edge_index, x, edge_type, weight, h_bias, loop_weight):
        import jax, jax.numpy as jnp
        import numpy as np
        N_NODES = 6250
        N_EDGES = 100000
        IN_FEAT = 256
        OUT_FEAT = 256
        NUM_RELS = 8
        ALPHA = 0.5
        num_nodes = x.shape[0]
        src, dst = (edge_index[0], edge_index[1])
        hx = jnp.einsum('ni,rio->rno', x, weight)
        msg = hx[edge_type, src]
        agg = jax.ops.segment_sum(msg, dst, num_segments=num_nodes)
        node_repr = agg * jnp.asarray(ALPHA, x.dtype) ** 0.5
        node_repr = node_repr + h_bias
        loop_message = x @ loop_weight
        node_repr = node_repr + loop_message * jnp.asarray(1.0 - ALPHA, x.dtype) ** 0.5
        return node_repr

    def _L1_gnn_ref(x, edge_index, W_l, b_l, W_r, gamma, beta):
        import jax, jax.numpy as jnp
        import numpy as np
        N_NODES = 6250
        N_EDGES = 100000
        D_IN = 256
        D_OUT = 256
        BN_EPS = 1e-05
        L2_EPS = 1e-12
        N = x.shape[0]
        src = edge_index[0]
        dst = edge_index[1]
        agg = jax.ops.segment_sum(x[src], dst, num_segments=N)
        deg = jax.ops.segment_sum(jnp.ones_like(src, dtype=x.dtype), dst, num_segments=N)
        mean = agg / jnp.maximum(deg, 1.0)[:, None]
        out = mean @ W_l.T + b_l + x @ W_r.T
        nrm = jnp.sqrt(jnp.sum(out * out, axis=-1, keepdims=True))
        out = out / jnp.maximum(nrm, L2_EPS)
        mu = jnp.mean(out, axis=0)
        var = jnp.mean((out - mu) ** 2, axis=0)
        out = (out - mu) / jnp.sqrt(var + BN_EPS) * gamma + beta
        return jax.nn.relu(out)

    def _L2_gnn_ref(x, src, dst, W0, al0, ar0, W1, al1, ar1, W2, al2, ar2):
        import jax, jax.numpy as jnp
        import numpy as np
        N_NODES = 6250
        NEG_SLOPE = 0.2

        def _gat_layer(h, W, al, ar, src, dst, residual):
            N = h.shape[0]
            H, D = al.shape
            feat = (h @ W).reshape(N, H, D)
            el = jnp.sum(feat * al[None], axis=-1)
            er = jnp.sum(feat * ar[None], axis=-1)
            e = jax.nn.leaky_relu(el[src] + er[dst], NEG_SLOPE)
            m = jax.ops.segment_max(e, dst, num_segments=N)
            m = jnp.where(jnp.isfinite(m), m, jnp.zeros_like(m))
            ex = jnp.exp(e - m[dst])
            den = jax.ops.segment_sum(ex, dst, num_segments=N)
            a = ex / jnp.maximum(den[dst], jnp.asarray(1e-09, ex.dtype))
            msg = a[:, :, None] * feat[src]
            out = jax.ops.segment_sum(msg, dst, num_segments=N)
            if residual:
                out = out + h.reshape(N, H, D)
            out = jax.nn.relu(out)
            return out.reshape(N, H * D)
        h = _gat_layer(x, W0, al0, ar0, src, dst, residual=True)
        h = _gat_layer(h, W1, al1, ar1, src, dst, residual=True)
        h = _gat_layer(h, W2, al2, ar2, src, dst, residual=False)
        return h

    def _L3_gnn_ref(x, W, edge_index):
        import jax, jax.numpy as jnp
        import numpy as np
        N_NODES = 6250
        N = x.shape[0]
        src, dst = (edge_index[0], edge_index[1])
        h = x @ W
        deg = jax.ops.segment_sum(jnp.ones_like(dst, dtype=h.dtype), dst, num_segments=N)
        deg_inv_sqrt = jnp.where(deg > 0, jax.lax.rsqrt(jnp.maximum(deg, 1)), 0.0)
        norm = deg_inv_sqrt[src] * deg_inv_sqrt[dst]
        msgs = h[src] * norm[:, None]
        out = jax.ops.segment_sum(msgs, dst, num_segments=N)
        return out
    edge_index = jnp.stack([src, dst])
    x = _layernorm(x + _L0_gnn_ref(edge_index, x, edge_type_8, L0_gnn_weight, L0_gnn_h_bias, L0_gnn_loop_weight), axis=-1)
    x = _layernorm(x + _L1_gnn_ref(x, edge_index, L1_gnn_W_l, L1_gnn_b_l, L1_gnn_W_r, L1_gnn_gamma, L1_gnn_beta), axis=-1)
    x = _layernorm(x + _L2_gnn_ref(x, src, dst, L2_gnn_W0, L2_gnn_al0, L2_gnn_ar0, L2_gnn_W1, L2_gnn_al1, L2_gnn_ar1, L2_gnn_W2, L2_gnn_al2, L2_gnn_ar2), axis=-1)
    x = _layernorm(x + _L3_gnn_ref(x, L3_gnn_W, edge_index), axis=-1)
    return x

_drawn_inputs = setup_inputs


def setup_inputs(seed=0):
    import zlib

    import numpy as np

    out = dict(_drawn_inputs(seed))
    spreads = {'L0_gnn_h_bias': (0.0, 0.1), 'L1_gnn_gamma': (1.0, 0.2), 'L1_gnn_beta': (0.0, 0.1)}
    factors = {'L1_gnn_b_l': 28.845,
     'L2_gnn_ar0': 57.599,
     'L2_gnn_al1': 4.57,
     'L2_gnn_ar1': 30.187,
     'L2_gnn_ar2': 31.431}
    for name, (base, spread) in spreads.items():
        noise = np.random.default_rng([zlib.crc32(name.encode()), seed]).standard_normal(out[name].shape)
        drawn = base * np.exp(spread * noise) if base else spread * noise
        out[name] = jnp.asarray(drawn.astype(out[name].dtype))
    for name, factor in factors.items():
        out[name] = (out[name] * factor).astype(out[name].dtype)
    return out
```

```python
import concourse.bass as bass
from concourse import mybir
from contextlib import ExitStack

FP = mybir.dt.float32
BF = mybir.dt.bfloat16
I32 = mybir.dt.int32
ALU = mybir.AluOpType
ACT = mybir.ActivationFunctionType
AX = mybir.AxisListType

P = 128
N = 6250
E = 100000
D = 256
H = 4
DH = D // H
R = 8
NB = -(-N // P)
NBA = NB + 1
NP = NBA * P
LAST = N - (NB - 1) * P
T = -(-E // P)
TAIL = E - (T - 1) * P
CH = -(-T // P)
U = 8
NBUF = 3
S = -(-(T + NB - 1 + NB) // (2 * U)) * 2 * U
K = S // U
SC = -(-(S + U) // P)
SP_ = SC * P
RT = SC * P
NODST = 7000
NF = 5
BIG = 3.0e38
W4 = D + H
LN_EPS = 1e-5
BN_EPS = 1e-5
L2_EPS = 1e-12
HALF = 0.5 ** 0.5


class Chain:

    def __init__(self, eng, sem, at=0, passed=None):
        self.eng, self.sem, self.at, self.n, self.passed = eng, sem, at, 0, passed

    def link(self, ins, plain=False):
        self.n += 1
        ins.then_inc(self.sem, 1)
        if plain:
            wait_apart(self.eng, self.sem, self.at + self.n, self.passed)
        else:
            self.eng.wait_ge(self.sem, self.at + self.n)


def wait_apart(eng, sem, value, passed):
    eng.wait_ge(sem, value)
    eng.sem_inc(passed, 1)


def build(nc, x, src, dst, etype, w_rel, h_bias, w_loop, w_l, b_l, w_r, gamma, beta,
          gat_w, gat_al, gat_ar, w3, out):
    ctx = ExitStack()
    sems = {}

    def sb(name, shape, dt, c=None):
        return (c or ctx).enter_context(nc.sbuf_tensor(name, shape, dt))

    def sem(name):
        if name not in sems:
            sems[name] = nc.alloc_semaphore(name=name)
        return sems[name]

    tiles_gathered = nc.alloc_semaphore(name="tiles_gathered")
    waits_met = nc.alloc_semaphore(name="waits_met")

    def clear_sems():
        numbers = sorted(s.num for s in sems.values())
        with nc.Block() as block:
            @block.gpsimd
            def _(pool):
                while numbers:
                    lo = hi = numbers.pop(0)
                    while numbers and numbers[0] == hi + 1:
                        hi = numbers.pop(0)
                    pool.sem_clear(range(lo, hi + 1))
        for s in sems.values():
            nc.release_semaphore(s)
        sems.clear()

    cur = sb("cur", [P, NBA, D], FP)
    agg = sb("agg", [P, NBA, W4], FP)
    row0 = sb("row0", [P, SP_], I32)
    rows_src = sb("rows_src", [P, SP_], I32)
    dloc = sb("dloc", [P, SP_], FP)
    mneg = sb("mneg", [P, SP_], FP)
    cont = sb("cont", [1, SP_], FP)
    packed = sb("packed", [1, K], I32)
    deg = sb("deg", [P, NBA], FP)
    rdeg = sb("rdeg", [P, NBA], FP)
    dinv = sb("dinv", [P, NBA], FP)
    ident = sb("ident", [P, P], FP)
    iota_f = sb("iota_f", [P, P], FP)
    iota_p = sb("iota_p", [P, 1], FP)
    ones = sb("ones", [P, P], FP)
    eps = sb("eps", [P, 1], FP)
    ps = [ctx.enter_context(nc.psum_tensor(f"ps{i}", [P, 512], FP)) for i in range(8)]

    table0 = nc.dram_tensor("table0", (R * NP, D), FP, kind="Internal").ap()
    tables = [nc.dram_tensor(f"table{i}", (NP, W4 if i in (2, 3, 4) else D), FP, kind="Internal").ap()
              for i in range(1, 6)]
    tiles_dram = nc.dram_tensor("tiles_dram", (RT, NF * P), FP, kind="Internal").ap()
    dloc_dram = nc.dram_tensor("dloc_dram", (SP_, P), BF, kind="Internal").ap()
    starts_dram = nc.dram_tensor("starts_dram", (SP_, P), BF, kind="Internal").ap()
    ends_dram = nc.dram_tensor("ends_dram", (SP_, P), BF, kind="Internal").ap()
    x2_dram = nc.dram_tensor("x2_dram", (NBA * P, D), FP, kind="Internal").ap()

    def raw_edges(c):
        dst_i = sb("dst_i", [P, SC, P], I32, c)
        prev_i = sb("prev_i", [P, SC, P], I32, c)
        next_i = sb("next_i", [P, SC, P], I32, c)
        src_i = sb("src_i", [P, SC, P], I32, c)
        typ_i = sb("typ_i", [P, SC, P], I32, c)
        f = sb("fields", [P, SC, NF, P], FP, c)
        m, ld, st, ch_sem = sem("raw_memset"), sem("raw_loaded"), sem("raw_stored"), sem("raw_chain")
        full = CH - 1
        rest = T - 1 - full * P
        e0 = full * P * P

        with nc.Block() as block:
            @block.gpsimd
            def _(pool):
                nc.gpsimd.memset(dst_i[:, full, :], NODST)
                nc.gpsimd.memset(prev_i[:, full, :], NODST)
                nc.gpsimd.memset(prev_i[0:1, 0, 0:1], -1)
                nc.gpsimd.memset(next_i[:, full, :], NODST)
                nc.gpsimd.memset(src_i[:, full, :], 0)
                nc.gpsimd.memset(typ_i[:, full, :], 0)
                nc.gpsimd.memset(ident[:], 0.0)
                nc.gpsimd.memset(ones[:], 1.0)
                nc.gpsimd.memset(eps[:], LN_EPS).then_inc(m, 1)
                pool.wait_ge(m, 1)
                nc.gpsimd.affine_select(out=ident[:], in_=ident[:], compare_op=ALU.not_equal, fill=1.0,
                                        base=0, pattern=[[-1, P]], channel_multiplier=1)
                nc.gpsimd.iota(iota_f[:], [[1, P]], base=0, channel_multiplier=0,
                               allow_small_or_imprecise_dtypes=True)
                nc.gpsimd.iota(iota_p[:], [[0, 1]], base=0, channel_multiplier=1,
                               allow_small_or_imprecise_dtypes=True)

            @block.sync
            def _(sp):
                sp.wait_ge(m, 1)
                n = 0
                for tile, a in ((dst_i, dst), (src_i, src), (typ_i, etype)):
                    sp.dma_start(tile[:, 0:full, :], a[0:e0].rearrange("(c p e) -> p c e", p=P, e=P)).then_inc(ld, 16)
                    sp.dma_start(tile[0:rest, full, :], a[e0:e0 + rest * P].rearrange("(p e) -> p e", e=P)).then_inc(ld, 16)
                    sp.dma_start(tile[rest:rest + 1, full, 0:TAIL],
                                 a[E - TAIL:E].rearrange("(p e) -> p e", p=1)).then_inc(ld, 16)
                    n += 48
                sp.dma_start(prev_i[:, 1:full, :], dst[P * P - 1:e0 - 1].rearrange("(c p e) -> p c e", p=P, e=P)).then_inc(ld, 16)
                sp.dma_start(prev_i[1:P, 0, :], dst[P - 1:P * P - 1].rearrange("(p e) -> p e", e=P)).then_inc(ld, 16)
                sp.dma_start(prev_i[0:1, 0, 1:P], dst[0:P - 1].rearrange("(p e) -> p e", p=1)).then_inc(ld, 16)
                sp.dma_start(prev_i[0:rest, full, :], dst[e0 - 1:e0 - 1 + rest * P].rearrange("(p e) -> p e", e=P)).then_inc(ld, 16)
                sp.dma_start(prev_i[rest:rest + 1, full, 0:TAIL],
                             dst[E - TAIL - 1:E - 1].rearrange("(p e) -> p e", p=1)).then_inc(ld, 16)
                sp.dma_start(next_i[:, 0:full, :], dst[1:e0 + 1].rearrange("(c p e) -> p c e", p=P, e=P)).then_inc(ld, 16)
                sp.dma_start(next_i[0:rest, full, :], dst[e0 + 1:e0 + 1 + rest * P].rearrange("(p e) -> p e", e=P)).then_inc(ld, 16)
                sp.dma_start(next_i[rest:rest + 1, full, 0:TAIL - 1],
                             dst[E - TAIL + 1:E].rearrange("(p e) -> p e", p=1)).then_inc(ld, 16)
                n += 16 * 8
                sp.wait_ge(ld, n)

        assert SC == CH
        with nc.Block() as block:
            @block.vector
            def _(dve):
                ch = Chain(dve, ch_sem)
                nc.vector.tensor_copy(f[:, :, 0, :], dst_i[:])
                nc.vector.tensor_copy(f[:, :, 1, :], src_i[:])
                ch.link(nc.vector.tensor_copy(f[:, :, 2, :], typ_i[:]))
                ch.link(nc.vector.scalar_tensor_tensor(out=f[:, :, 2, :], in0=f[:, :, 2, :], scalar=float(NP),
                                                       in1=f[:, :, 1, :], op0=ALU.mult, op1=ALU.add))
                nc.vector.tensor_tensor(f[:, :, 3, :], dst_i[:], prev_i[:], ALU.not_equal)
                ch.link(nc.vector.tensor_tensor(f[:, :, 4, :], dst_i[:], next_i[:], ALU.not_equal))

        with nc.Block() as block:
            @block.sync
            def _(sp):
                sp.dma_start(tiles_dram.rearrange("(c p) w -> p c w", p=P),
                             f[:].rearrange("p c f e -> p c (f e)")).then_inc(st, 16)
                sp.wait_ge(st, 16)
        return f

    def make_steps(c, f):
        thr = sb("thr", [P, NB], FP, c)
        cmp_lo = sb("cmp_lo", [P, NB, CH], FP, c)
        cmp_hi = sb("cmp_hi", [P, NB, CH], FP, c)
        cnt = sb("cnt", [P, 2 * NB], FP, c)
        first = sb("first", [P, NB], FP, c)
        num = sb("num", [P, NB], FP, c)
        odd_i = sb("odd_i", [P, NB], I32, c)
        odd = sb("odd", [P, NB], FP, c)
        zero = sb("zero", [P, NB], FP, c)
        cum = sb("cum", [P, NB], FP, c)
        cum0 = sb("cum0", [P, NB], FP, c)
        shift = sb("shift", [P, NB], FP, c)
        step = sb("step", [P, SC], FP, c)
        ind = sb("ind", [P, SC, NB], FP, c)
        ind0 = sb("ind0", [P, SC, NB], FP, c)
        blk = sb("blk", [P, SC], FP, c)
        til = sb("til", [P, SC], FP, c)
        til_i = sb("til_i", [P, SC], I32, c)
        blk128 = sb("blk128", [P, SC], FP, c)
        brow = sb("brow", [1, SP_], FP, c)
        pk = sb("pk", [1, 4, K], FP, c)
        a_s, b_s, g_s, t_s = sem("steps_thr"), sem("steps_cmp"), sem("steps_sum"), sem("steps_tiles")
        ch_sem = sem("steps_chain")

        with nc.Block() as block:
            @block.gpsimd
            def _(pool):
                nc.gpsimd.iota(thr[:], [[P, NB]], base=0, channel_multiplier=0,
                               allow_small_or_imprecise_dtypes=True)
                nc.gpsimd.iota(step[:], [[P, SC]], base=0, channel_multiplier=1,
                               allow_small_or_imprecise_dtypes=True)
                nc.gpsimd.memset(zero[:], 0.0).then_inc(a_s, 1)

            @block.vector
            def _(dve):
                ch = Chain(dve, ch_sem)
                dve.wait_ge(a_s, 1)
                nc.vector.tensor_tensor(cmp_hi[:], f[:, 0:CH, 0, P - 1:P].rearrange("p c o -> p o c").to_broadcast([P, NB, CH]),
                                        thr[:].unsqueeze(2).to_broadcast([P, NB, CH]), ALU.is_lt)
                ch.link(nc.vector.tensor_scalar(num[:], thr[:], float(P), None, ALU.add))
                ch.link(nc.vector.tensor_tensor(cmp_lo[:], f[:, 0:CH, 0, 0:1].rearrange("p c o -> p o c").to_broadcast([P, NB, CH]),
                                                num[:].unsqueeze(2).to_broadcast([P, NB, CH]), ALU.is_lt))
                nc.vector.tensor_reduce(cnt[:, 0:NB], cmp_hi[:], op=ALU.add, axis=AX.X)
                ch.link(nc.vector.tensor_reduce(cnt[:, NB:2 * NB], cmp_lo[:], op=ALU.add, axis=AX.X))
                nc.vector.tensor_copy(first[:], zero[:]).then_inc(b_s, 1)
                dve.wait_ge(g_s, 1)
                ch.link(nc.vector.tensor_copy(cnt[:], ps[0][:, 0:2 * NB]))
                ch.link(nc.vector.tensor_copy(first[:], cnt[:, 0:NB]))
                ch.link(nc.vector.tensor_tensor(num[:], cnt[:, NB:2 * NB], first[:], ALU.subtract))
                ch.link(nc.vector.tensor_scalar(num[:], num[:], 1.0, None, ALU.max))
                ch.link(nc.vector.tensor_copy(odd_i[:], num[:]))
                ch.link(nc.vector.tensor_scalar(odd_i[:], odd_i[:], 1, None, ALU.bitwise_and))
                ch.link(nc.vector.tensor_copy(odd[:], odd_i[:]))
                ch.link(nc.vector.tensor_tensor(num[:], num[:], odd[:], ALU.add))
                ch.link(nc.vector.tensor_tensor_scan(cum[:], num[:], zero[:], 0.0, ALU.add, ALU.add))
                ch.link(nc.vector.tensor_tensor(cum0[:], cum[:], num[:], ALU.subtract))
                ch.link(nc.vector.tensor_tensor(shift[:], first[:], cum0[:], ALU.subtract))
                nc.vector.tensor_tensor(ind[:], cum[:].unsqueeze(1).to_broadcast([P, SC, NB]),
                                        step[:].unsqueeze(2).to_broadcast([P, SC, NB]), ALU.is_le)
                ch.link(nc.vector.tensor_tensor(ind0[:], cum0[:].unsqueeze(1).to_broadcast([P, SC, NB]),
                                                step[:].unsqueeze(2).to_broadcast([P, SC, NB]), ALU.is_le))
                nc.vector.tensor_reduce(blk[:], ind[:], op=ALU.add, axis=AX.X)
                ch.link(nc.vector.tensor_tensor(ind0[:], ind0[:], ind[:], ALU.subtract))
                ch.link(nc.vector.tensor_tensor(ind0[:], ind0[:], shift[:].unsqueeze(1).to_broadcast([P, SC, NB]), ALU.mult))
                ch.link(nc.vector.tensor_reduce(til[:], ind0[:], op=ALU.add, axis=AX.X))
                ch.link(nc.vector.tensor_tensor(til[:], til[:], step[:], ALU.add))
                nc.vector.tensor_scalar(blk128[:], blk[:], float(P), None, ALU.mult)
                nc.vector.tensor_copy(til_i[:], til[:]).then_inc(t_s, 1)

            @block.tensor
            def _(pe):
                pe.wait_ge(b_s, 1)
                nc.tensor.matmul(ps[0][:, 0:2 * NB], ones[:], cnt[:], start=True, stop=True).then_inc(g_s, 1)

        sf = f
        ok = sb("ok", [P, SC, P], FP, c)
        d16 = sb("d16", [P, SC, P], BF, c)
        mrow = sb("mrow", [P, SC, P], FP, c)
        starts16 = sb("starts16", [P, SC, P], BF, c)
        ends16 = sb("ends16", [P, SC, P], BF, c)
        gth, cal, st = tiles_gathered, sem("steps_rows"), sem("steps_stored")
        with nc.Block() as block:
            @block.gpsimd
            def _(pool):
                for k in range(SC):
                    nc.gpsimd.indirect_dma_start(
                        out=sf[:, k, :, :].rearrange("p f e -> p (f e)"), out_offset=None, in_=tiles_dram,
                        in_offset=bass.IndirectOffsetOnAxis(ap=til_i[:, k:k + 1], axis=0)).then_inc(gth, 16)
                pool.wait_ge(gth, 16 * SC)
        ch2 = sem("rows_chain")
        with nc.Block() as block:
            @block.vector
            def _(dve):
                ch = Chain(dve, ch2)
                d = sf[:, :, 0, :]
                ch.link(nc.vector.tensor_tensor(d, d, blk128[:].unsqueeze(2).to_broadcast([P, SC, P]), ALU.subtract))
                ch.link(nc.vector.tensor_scalar(ok[:], d, 0.0, None, ALU.is_ge))
                ch.link(nc.vector.scalar_tensor_tensor(out=ok[:], in0=d, scalar=float(P), in1=ok[:],
                                                       op0=ALU.is_lt, op1=ALU.mult))
                ch.link(nc.vector.scalar_tensor_tensor(out=d, in0=d, scalar=1.0, in1=ok[:], op0=ALU.add, op1=ALU.mult))
                ch.link(nc.vector.tensor_scalar(d, d, -1.0, None, ALU.add))
                nc.vector.tensor_copy(d16[:], d)
                nc.vector.tensor_scalar(mrow[:], ok[:], BIG, -BIG, ALU.mult, ALU.add)
                ch.link(nc.vector.tensor_tensor(sf[:, :, 3, :], sf[:, :, 3, :], ok[:], ALU.mult))
                nc.vector.tensor_tensor(sf[:, :, 4, :], sf[:, :, 4, :], ok[:], ALU.mult)
                ch.link(nc.vector.tensor_tensor(ok[:], ok[:], sf[:, :, 3, :], ALU.subtract))
                ch.link(nc.vector.tensor_scalar(starts16[:], sf[:, :, 3, :], -BIG, None, ALU.mult))
                nc.vector.tensor_scalar(ends16[:], sf[:, :, 4, :], -BIG, None, ALU.mult).then_inc(cal, 1)

            @block.sync
            def _(sp):
                sp.wait_ge(cal, 1)
                sp.dma_start(dloc_dram.rearrange("(c p) e -> p c e", p=P), d16[:]).then_inc(st, 16)
                sp.dma_start(starts_dram.rearrange("(c p) e -> p c e", p=P), starts16[:]).then_inc(st, 16)
                sp.dma_start(ends_dram.rearrange("(c p) e -> p c e", p=P), ends16[:]).then_inc(st, 16)
                sp.wait_ge(st, 48)

        tr, cp = sem("turned"), sem("turned_copied")
        with nc.Block() as block:
            @block.tensor
            def _(pe):
                for k in range(SC):
                    if k:
                        pe.wait_ge(cp, 2 * k)
                    for j, a in enumerate((sf[:, k, 0, :], mrow[:, k, :], sf[:, k, 1, :], sf[:, k, 2, :])):
                        nc.tensor.transpose(ps[j][:, 0:P], a, ident[:]).then_inc(tr, 1)
                    nc.tensor.transpose(ps[4][:, 0:P], ok[:, k, :], ident[:])
                    nc.tensor.transpose(ps[5][0:1, 0:P], blk[:, k:k + 1], ident[:]).then_inc(tr, 1)

            @block.vector
            def _(dve):
                for k in range(SC):
                    col = slice(k * P, (k + 1) * P)
                    dve.wait_ge(tr, 5 * k + 5)
                    nc.vector.tensor_copy(dloc[:, col], ps[0][:, 0:P])
                    nc.vector.tensor_copy(mneg[:, col], ps[1][:, 0:P])
                    nc.vector.tensor_copy(rows_src[:, col], ps[2][:, 0:P])
                    nc.vector.tensor_copy(row0[:, col], ps[3][:, 0:P])
                    nc.vector.tensor_copy(cont[:, col], ps[4][0:1, 0:P])
                    nc.vector.tensor_copy(brow[:, col], ps[5][0:1, 0:P]).then_inc(cp, 2)
        ch3 = sem("pack_chain")
        with nc.Block() as block:
            @block.vector
            def _(dve):
                ch = Chain(dve, ch3)
                b = brow[:, 0:S].rearrange("o (k j u) -> o u j k", j=U // 2, u=2)[:, 0]
                for j in range(1, 4):
                    ch.link(nc.vector.tensor_tensor(pk[:, j, :], b[:, j, :], b[:, j - 1, :], ALU.subtract))
                ch.link(nc.vector.tensor_copy(pk[:, 0, :], b[:, 0, :]))
                for j in range(1, 4):
                    ch.link(nc.vector.scalar_tensor_tensor(out=pk[:, 0, :], in0=pk[:, j, :], scalar=float(64 << (j - 1)),
                                                           in1=pk[:, 0, :], op0=ALU.mult, op1=ALU.add))
                ch.link(nc.vector.tensor_copy(packed[:], pk[:, 0, :]))

    def pair_blocks(eng, k):
        r = eng.value_load(packed[0:1, bass.ds(k, 1)], min_val=0, max_val=511)
        why = "make_steps numbers the blocks from 0 to NB"
        b = [r & 63]
        for j in range(1, 4):
            b.append(b[-1] + ((r >> (5 + j)) & 1))
        b = [nc.s_assert_within(v, 0, NB, skip_runtime_bounds_check_because=why) for v in b]
        return b


    full_iters, left = K // NBUF, K % NBUF
    slot_full = [nc.alloc_semaphore(name=f"slot_full{j}") for j in range(NBUF * U)]
    used = [0] * NBUF

    def nxt(i, u):
        return (i, u + 1) if u + 1 < NBUF else (i + 1, 0)

    def each_batch(eng, body):
        with eng.Fori(0, full_iters) as i:
            for u in range(NBUF):
                body(i, u)
        for u in range(left):
            body(full_iters, u)

    def ahead(eng, early, late):
        early(0, 0)
        with eng.Fori(0, full_iters) as i:
            for u in range(NBUF):
                early(*nxt(i, u))
                late(i, u)
        for u in range(left):
            if u + 1 < left:
                early(full_iters, u + 1)
            late(full_iters, u)

    def gather_batches(pool, rows, width, table, stage, staged, pair_done, base):
        def batch(i, u):
            k = i * NBUF + u
            pool.wait_ge(staged[u], i * 16 + 16)
            for j in range(U):
                if j % 2 == 0:
                    wait_apart(pool, pair_done, k * (U // 2) + (j // 2 + 1), waits_met)
                nc.gpsimd.indirect_dma_start(
                    out=rows[:, u, j, 0:width], out_offset=None, in_=table,
                    in_offset=bass.IndirectOffsetOnAxis(ap=stage[:, u, j:j + 1], axis=0),
                ).then_inc(slot_full[u * U + j], 16)
        each_batch(pool, batch)

    def stage_indices(sp, index, stage, staged, base):
        def batch(i, u, reused=True):
            k = i * NBUF + u
            if reused:
                for j in range(U):
                    sp.wait_ge(slot_full[u * U + j], i * 16 + 16 * base[u])
            sp.dma_start(stage[:, u, :], index[:, bass.ds(k * U, U)]).then_inc(staged[u], 16)
        for u in range(NBUF):
            batch(0, u, reused=False)
        with sp.Fori(1, full_iters) as i:
            for u in range(NBUF):
                batch(i, u)
        for u in range(left):
            batch(full_iters, u)

    def aggregate(name, table, index, with_deg):
        c = ExitStack()
        width = D + 1 if with_deg else D
        rows = sb(f"rows_{name}", [P, NBUF, U, width], FP, c)
        hot = sb(f"hot_{name}", [P, NBUF, U, P], FP, c)
        stage = sb(f"stage_{name}", [P, NBUF, U], I32, c)
        hot_ready, pair_done, added = sem(f"hot_{name}"), sem(f"pair_{name}"), sem(f"added_{name}")
        staged, ones_set = [sem(f"staged_{name}{u}") for u in range(NBUF)], sem(f"ones_{name}")
        base = list(used)
        for u in range(NBUF):
            used[u] += full_iters + (u < left)
        credit = NBUF * U // 2
        with nc.Block() as block:
            @block.gpsimd
            def _(pool):
                if with_deg:
                    nc.gpsimd.memset(rows[:, :, :, D:D + 1], 1.0).then_inc(ones_set, 1)
                nc.gpsimd.memset(hot[:], 0.0).then_inc(pair_done, credit)
                gather_batches(pool, rows, D, table, stage, staged, pair_done, base)

            @block.sync
            def _(sp):
                stage_indices(sp, index, stage, staged, base)

            @block.vector
            def _(dve):
                nc.vector.memset(agg[:], 0.0).then_inc(added, U // 2)
                dve.wait_ge(pair_done, credit)

                def early(i, u):
                    k = i * NBUF + u
                    dve.wait_ge(pair_done, (k + 1) * (U // 2))
                    nc.vector.tensor_tensor(
                        hot[:, u, :, :], iota_f[:].unsqueeze(1).to_broadcast([P, U, P]),
                        dloc[:, bass.ds(k * U, U)].unsqueeze(2).to_broadcast([P, U, P]),
                        ALU.is_equal).then_inc(hot_ready, 1)

                def late(i, u):
                    k = i * NBUF + u
                    blocks = pair_blocks(dve, k)
                    for j in range(U // 2):
                        dve.wait_ge(pair_done, k * (U // 2) + (credit + j + 1))
                        dve.wait_ge(added, k * (U // 2) + (U // 2 + j))
                        acc = agg[:, bass.ds(blocks[j], 1), 0:width].rearrange("p o w -> p (o w)")
                        nc.vector.tensor_tensor(acc, acc, ps[j][:, 0:width], ALU.add).then_inc(added, 1)
                ahead(dve, early, late)

            @block.tensor
            def _(pe):
                if with_deg:
                    pe.wait_ge(ones_set, 1)
                def batch(i, u):
                    k = i * NBUF + u
                    pe.wait_ge(hot_ready, k + 1)
                    for j in range(U // 2):
                        pe.wait_ge(added, k * (U // 2) + (j + 1))
                        for s in (2 * j, 2 * j + 1):
                            pe.wait_ge(slot_full[u * U + s], i * 16 + 16 * (base[u] + 1))
                            mm = nc.tensor.matmul(ps[j][:, 0:width], hot[:, u, s, :], rows[:, u, s, :],
                                                  start=s % 2 == 0, stop=s % 2 == 1)
                        mm.then_inc(pair_done, 1)
                each_batch(pe, batch)
        c.close()

    G = 5

    def load(name, pairs, gp=()):
        s = sem(f"load_{name}")
        with nc.Block() as block:
            @block.sync
            def _(sp):
                for out_, in_ in pairs:
                    sp.dma_start(out_, in_).then_inc(s, 16)
                sp.wait_ge(s, 16 * len(pairs))

    def two_ahead(eng, early, late):
        early(0, 0)
        with eng.Fori(0, NBA // 2 - 1) as i:
            early(i * 2 + 1, 1)
            late(i * 2, 0)
            early(i * 2 + 2, 0)
            late(i * 2 + 1, 1)
        early(NBA - 1, 1)
        late(NBA - 2, 0)
        late(NBA - 1, 1)

    def project(name, weights, widths, fill, fill_links, on_act, on_dve, dve_links=0, ob=None, table=None, keep=False):
        c = ExitStack()
        nb = sb(f"nb_{name}", [P, 2, D], FP, c)
        xt = sb(f"xt_{name}", [P, 2, 2, P], FP, c)
        filled, turned, xt_ready, mm_done = (sem(f"{q}_{name}") for q in ("filled", "turned", "xt", "mm"))
        taken_a, taken_d, kept, ob_free = (sem(f"{q}_{name}") for q in ("takena", "takend", "kept", "obfree"))
        fch, dch = sem(f"fillchain_{name}"), sem(f"takechain_{name}")
        stored = [sem(f"stored_{name}{u}") for u in range(2)]
        nt, la, ld = len(widths), len(on_act), len(on_dve)
        sets = 2 if nt <= 3 else 1
        pst = [ps[6], ps[7]]
        start = [sum(widths[:n]) for n in range(nt)]

        def bank(u, n):
            return ps[(u % sets) * nt + n]

        def take(eng, i, u, tiles, taken, links=0):
            if not tiles:
                return
            if ob is not None:
                eng.wait_ge(ob_free, i + 1)
            ch = Chain(eng, dch, i * links)
            for n, f in tiles.items():
                eng.wait_ge(mm_done, i * nt + (2 * nt + n + 1))
                f(ch, i, u, bank(u, n)[:, 0:widths[n]]).then_inc(taken, 1)
            assert ch.n == links

        with nc.Block() as block:
            @block.vector
            def _(dve):
                def early(i, u):
                    dve.wait_ge(turned, i + 1)
                    if keep:
                        dve.wait_ge(kept, i + 1)
                    ch = Chain(dve, fch, i * fill_links)
                    fill(ch, i, nb[:, u, :]).then_inc(filled, 1)
                    assert ch.n == fill_links
                two_ahead(dve, early, lambda i, u: take(dve, i, u, on_dve, taken_d, dve_links))

            @block.scalar
            def _(act):
                act.sem_inc(turned, 2)
                act.sem_inc(xt_ready, 2)
                act.sem_inc(mm_done, 2 * nt)
                if keep:
                    act.sem_inc(kept, 2)
                if la:
                    act.sem_inc(taken_a, sets * la)
                if ld:
                    act.sem_inc(taken_d, sets * ld)
                if ob is not None:
                    act.sem_inc(ob_free, 2)

                def early(i, u):
                    act.wait_ge(turned, i + 3)
                    act.wait_ge(mm_done, i * nt + nt)
                    nc.scalar.copy(xt[:, u, :, :].rearrange("p h e -> p (h e)"),
                                   pst[u][:, 0:2 * P]).then_inc(xt_ready, 1)
                    if keep:
                        nc.scalar.copy(cur[:, bass.ds(i, 1), :].rearrange("p o w -> p (o w)"),
                                       nb[:, u, :]).then_inc(kept, 1)
                two_ahead(act, early, lambda i, u: take(act, i, u, on_act, taken_a))

            @block.tensor
            def _(pe):
                def early(i, u):
                    pe.wait_ge(filled, i + 1)
                    pe.wait_ge(xt_ready, i + 1)
                    nc.tensor.transpose(pst[u][:, 0:P], nb[:, u, 0:P], ident[:])
                    nc.tensor.transpose(pst[u][:, P:2 * P], nb[:, u, P:D], ident[:]).then_inc(turned, 1)

                def late(i, u):
                    pe.wait_ge(xt_ready, i + 3)
                    for n in range(nt):
                        if n in on_act:
                            pe.wait_ge(taken_a, i * la + (list(on_act).index(n) + 1))
                        else:
                            pe.wait_ge(taken_d, i * ld + (list(on_dve).index(n) + 1))
                        for h in range(2):
                            mm = nc.tensor.matmul(bank(u, n)[:, 0:widths[n]], xt[:, u, h, :],
                                                  weights[:, h, start[n]:start[n] + widths[n]],
                                                  start=h == 0, stop=h == 1)
                        mm.then_inc(mm_done, 1)
                two_ahead(pe, early, late)

            @block.sync
            def _(sp):
                if ob is None:
                    return
                with sp.Fori(0, NBA // 2) as it:
                    for u in range(2):
                        i = it * 2 + u
                        if la:
                            sp.wait_ge(taken_a, i * la + (sets + 1) * la)
                        if ld:
                            sp.wait_ge(taken_d, i * ld + (sets + 1) * ld)
                        sp.dma_start(table(i), ob[:, u]).then_inc(stored[u], 16)
                        sp.wait_ge(stored[u], it * 16 + 16)
                        sp.sem_inc(ob_free, 1)
        c.close()

    def blk1(a, i):
        return a[:, bass.ds(i, 1), 0:D].rearrange("p o w -> p (o w)")

    def grp(a, g):
        return a[:, bass.ds(g * G, G), 0:D]

    def each_group(name, links, body, per=1):
        s = sem(f"groups_{name}")
        with nc.Block() as block:
            @block.vector
            def _(dve):
                with dve.Fori(0, NBA // G) as g:
                    ch = Chain(dve, s, g * links, waits_met)
                    body(ch, g)
                    assert ch.n == links, (name, ch.n)

    mv = sb("mv", [P, NBA, 2], FP)
    rstd = sb("rstd", [P, NBA], FP)

    def row_stats(name, combine, links):
        c = ExitStack()
        st6 = sb(f"st6_{name}", [P, G, 6], FP, c)
        mv5 = sb(f"mv5_{name}", [P, G, 2], FP, c)

        def body(ch, g):
            combine(ch, g)
            for j in range(G):
                ins = nc.vector.bn_stats(st6[:, j, :], blk1(cur, g * G + j))
            ch.link(ins, plain=True)
            for j in range(G):
                ins = nc.vector.bn_aggr(mv5[:, j, :], st6[:, j, :])
            ch.link(ins)
            ch.link(nc.vector.tensor_copy(mv[:, bass.ds(g * G, G), :], mv5[:]))
        each_group(name, links + 3, body)
        root, done = sem(f"root_{name}"), sem(f"rstd_{name}")
        with nc.Block() as block:
            @block.scalar
            def _(act):
                nc.scalar.activation(rstd[:], mv[:, :, 1:2].rearrange("p b o -> p (b o)"), ACT.Sqrt, bias=eps[:]).then_inc(root, 1)

            @block.vector
            def _(dve):
                dve.wait_ge(root, 1)
                nc.vector.reciprocal(rstd[:], rstd[:]).then_inc(done, 1)
        c.close()

    def normalised(ch, i, nb):
        return nc.vector.tensor_scalar(nb, blk1(cur, i), mv[:, bass.ds(i, 1), 0:1].rearrange("p o w -> p (o w)"),
                                       rstd[:, bass.ds(i, 1)], ALU.subtract, ALU.mult)

    def copied(ch, i, nb):
        return nc.vector.tensor_copy(nb, blk1(cur, i))

    def w_view(w):
        return w.rearrange("(h p) n -> p h n", p=P)

    def rows_of(t):
        return lambda i: t[bass.ds(i * P, P), :]

    def layer0():
        c = ExitStack()
        w = sb("w0", [P, 2, (R + 1) * D], FP, c)
        bias = sb("bias0", [P, D], FP, c)
        ob = sb("ob0", [P, 2, R * D], FP, c)
        zero = sem("cur_cleared")
        with nc.Block() as block:
            @block.gpsimd
            def _(pool):
                nc.gpsimd.memset(cur[:, NB - 1:NBA, :], 0.0).then_inc(zero, 1)
        load("x", [(cur[:, 0:NB - 1, :], x[0:(NB - 1) * P, :].rearrange("(b p) d -> p b d", p=P)),
                   (cur[0:LAST, NB - 1, :], x[(NB - 1) * P:N, :]),
                   (bias[:], h_bias.partition_broadcast(P)),
                   (w[:, :, R * D:], w_view(w_loop))] +
             [(w[:, :, r * D:(r + 1) * D], w_view(w_rel[r])) for r in range(R)])

        def to_ob(eng_copy, n):
            return lambda ch, i, u, b: eng_copy(ob[:, u, n * 512:(n + 1) * 512], b)

        def self_part(ch, i, u, b):
            ch.link(nc.vector.scalar_tensor_tensor(out=blk1(cur, i), in0=b, scalar=HALF, in1=blk1(cur, i),
                                                   op0=ALU.mult, op1=ALU.add))
            return nc.vector.tensor_tensor(blk1(cur, i), blk1(cur, i), bias[:], ALU.add)
        t0 = table0.rearrange("(r n) d -> n r d", r=R)
        project("l0", w, [512] * 4 + [D], copied, 0,
                {0: to_ob(nc.scalar.copy, 0), 1: to_ob(nc.scalar.copy, 1), 2: to_ob(nc.scalar.copy, 2)},
                {3: to_ob(nc.vector.tensor_copy, 3), 4: self_part}, dve_links=1,
                ob=ob, table=lambda i: t0[bass.ds(i * P, P), :, :])
        c.close()

    def degrees():
        s = sem("degrees")
        c = ExitStack()
        root = sb("deg_root", [P, NBA], FP, c)
        has = sb("deg_has", [P, NBA], FP, c)
        r = sem("deg_rooted")
        with nc.Block() as block:
            @block.vector
            def _(dve):
                ch = Chain(dve, s)
                ch.link(nc.vector.tensor_copy(deg[:], agg[:, :, D:D + 1].rearrange("p b o -> p (b o)")))
                nc.vector.tensor_scalar(has[:], deg[:], 0.0, None, ALU.is_gt)
                ch.link(nc.vector.tensor_scalar(deg[:], deg[:], 1.0, None, ALU.max))
                ch.link(nc.vector.reciprocal(rdeg[:], deg[:]))
                dve.wait_ge(r, 1)
                ch.link(nc.vector.reciprocal(dinv[:], root[:]))
                ch.link(nc.vector.tensor_tensor(dinv[:], dinv[:], has[:], ALU.mult))

            @block.scalar
            def _(act):
                act.wait_ge(s, 2)
                nc.scalar.sqrt(root[:], deg[:]).then_inc(r, 1)
        c.close()

    def layer1_table():
        c = ExitStack()
        w = sb("wl", [P, 2, D], FP, c)
        ob = sb("ob1", [P, 2, D], FP, c)
        load("wl", [(w[:], w_view(w_l))])

        def combine(ch, g):
            ch.link(nc.vector.scalar_tensor_tensor(out=grp(cur, g), in0=grp(agg, g), scalar=HALF, in1=grp(cur, g),
                                                   op0=ALU.mult, op1=ALU.add), plain=True)
        row_stats("x1", combine, 1)
        project("l1", w, [D], normalised, 0, {0: lambda ch, i, u, b: nc.scalar.copy(ob[:, u, :], b)}, {},
                ob=ob, table=rows_of(tables[0]), keep=True)
        c.close()

    def layer1_end():
        c = ExitStack()
        w = sb("wr", [P, 2, D], FP, c)
        bl = sb("bl", [P, D], FP, c)
        gam = sb("gam", [P, D], FP, c)
        bet = sb("bet", [P, D], FP, c)
        tmp = sb("tmp1", [P, 2, G, D], FP, c)
        ss = sb("ss", [P, NBA], FP, c)
        mask = sb("row_mask", [P, P], FP, c)
        mu = sb("mu", [P, D], FP, c)
        load("wr", [(w[:], w_view(w_r)), (bl[:], b_l.partition_broadcast(P)), (gam[:], gamma.partition_broadcast(P)),
                    (bet[:], beta.partition_broadcast(P))])

        def mean_part(ch, i, u, b):
            a = blk1(agg, i)
            ch.link(nc.vector.scalar_tensor_tensor(out=a, in0=a, scalar=rdeg[:, bass.ds(i, 1)], in1=b,
                                                   op0=ALU.mult, op1=ALU.add))
            return nc.vector.tensor_tensor(a, a, bl[:], ALU.add)
        project("l1r", w, [D], copied, 0, {}, {0: mean_part}, dve_links=1)

        def squares(ch, g):
            ch.link(nc.vector.tensor_tensor(tmp[:, 0], grp(agg, g), grp(agg, g), ALU.mult))
            ch.link(nc.vector.tensor_reduce(ss[:, bass.ds(g * G, G)], tmp[:, 0], op=ALU.add, axis=AX.X))
        each_group("squares", 2, squares)
        root, s, mk = sem("len_root"), sem("len_chain"), sem("mask_made")
        with nc.Block() as block:
            @block.scalar
            def _(act):
                nc.scalar.sqrt(ss[:], ss[:]).then_inc(root, 1)

            @block.gpsimd
            def _(pool):
                nc.gpsimd.affine_select(out=mask[:], in_=ones[:], compare_op=ALU.is_gt, fill=0.0, base=LAST,
                                        pattern=[[0, P]], channel_multiplier=-1).then_inc(mk, 1)

            @block.vector
            def _(dve):
                ch = Chain(dve, s)
                dve.wait_ge(root, 1)
                ch.link(nc.vector.tensor_scalar(ss[:], ss[:], L2_EPS, None, ALU.max))
                ch.link(nc.vector.reciprocal(ss[:], ss[:]))
                dve.wait_ge(mk, 1)
                ch.link(nc.vector.tensor_tensor(ss[:, NB - 1:NB], ss[:, NB - 1:NB], mask[:, 0:1], ALU.mult))
                ch.link(nc.vector.memset(ss[:, NB:NBA], 0.0))

        ngr = NBA // G
        scaled, summed, mean_s = sem("rows_scaled"), sem("mean_summed"), sem("mean_chain")
        with nc.Block() as block:
            @block.vector
            def _(dve):
                with dve.Fori(0, ngr) as g:
                    nc.vector.tensor_tensor(grp(agg, g), grp(agg, g),
                                            ss[:, bass.ds(g * G, G)].unsqueeze(2).to_broadcast([P, G, D]),
                                            ALU.mult).then_inc(scaled, 1)
                dve.wait_ge(summed, 1)
                nc.vector.tensor_scalar(mu[:], ps[0][:, 0:D], 1.0 / N, None, ALU.mult).then_inc(mean_s, 1)

            @block.tensor
            def _(pe):
                def one(i, first, last):
                    return nc.tensor.matmul(ps[0][:, 0:D], ones[:], blk1(agg, i), start=first, stop=last)
                pe.wait_ge(scaled, 1)
                for j in range(G):
                    one(j, j == 0, False)
                with pe.Fori(1, ngr - 1) as g:
                    pe.wait_ge(scaled, g + 1)
                    for j in range(G):
                        one(g * G + j, False, False)
                pe.wait_ge(scaled, ngr)
                for j in range(G):
                    mm = one((ngr - 1) * G + j, False, j == G - 1)
                mm.then_inc(summed, 1)

        cent, sq, sqd, var_s, rt, vch = (sem(q) for q in ("centred", "squared", "sq_summed", "var_summed", "var_root", "var_chain"))
        with nc.Block() as block:
            @block.vector
            def _(dve):
                with dve.Fori(0, ngr) as g:
                    nc.vector.tensor_tensor(grp(agg, g), grp(agg, g), mu[:].unsqueeze(1).to_broadcast([P, G, D]),
                                            ALU.subtract).then_inc(cent, 1)
                ch = Chain(dve, vch)
                dve.wait_ge(var_s, 1)
                ch.link(nc.vector.tensor_scalar(mu[:], ps[0][:, 0:D], 1.0 / N, None, ALU.mult))
                dve.wait_ge(rt, 1)
                ch.link(nc.vector.reciprocal(mu[:], mu[:]))
                ch.link(nc.vector.tensor_tensor(gam[:], gam[:], mu[:], ALU.mult))

            @block.scalar
            def _(act):
                act.sem_inc(sqd, 2)
                with act.Fori(0, ngr // 2) as gg:
                    for u in range(2):
                        g = gg * 2 + u
                        act.wait_ge(cent, g + 1)
                        act.wait_ge(sqd, g + 1)
                        nc.scalar.square(tmp[:, u], grp(agg, g)).then_inc(sq, 1)
                act.wait_ge(vch, 1)
                nc.scalar.activation(mu[:], mu[:], ACT.Sqrt, bias=eps[:]).then_inc(rt, 1)

            @block.tensor
            def _(pe):
                def group(g, u, first=False, final=False):
                    pe.wait_ge(sq, g + 1)
                    for j in range(G - final):
                        last = final and j == G - 2
                        mm = nc.tensor.matmul(ps[0][:, 0:D], mask[:] if last else ones[:], tmp[:, u, j, :],
                                              start=first and j == 0, stop=last)
                    mm.then_inc(sqd, 1)
                    return mm
                group(0, 0, first=True)
                group(1, 1)
                with pe.Fori(1, ngr // 2 - 1) as gg:
                    group(gg * 2, 0)
                    group(gg * 2 + 1, 1)
                group(ngr - 2, 0)
                group(ngr - 1, 1, final=True)
                pe.wait_ge(sqd, 2 + ngr)
                pe.sem_inc(var_s, 1)

        def combine(ch, g):
            t = tmp[:, 0]
            ch.link(nc.vector.tensor_tensor(t, grp(agg, g), gam[:].unsqueeze(1).to_broadcast([P, G, D]), ALU.mult))
            ch.link(nc.vector.tensor_tensor(t, t, bet[:].unsqueeze(1).to_broadcast([P, G, D]), ALU.add))
            ch.link(nc.vector.scalar_tensor_tensor(out=grp(cur, g), in0=t, scalar=0.0, in1=grp(cur, g),
                                                   op0=ALU.max, op1=ALU.add), plain=True)
        row_stats("x2", combine, 3)
        c.close()

    er_all = sb("er_all", [P, NBA, H], FP)
    er3 = sb("er3", [P, NBA, H, 3], BF)
    rden = sb("rden", [P, NBA, H], FP)

    def heads(a):
        return a.rearrange("p (h w) -> p h w", h=H)

    def gat_weights(c, n):
        w = sb(f"wg{n}", [P, 2, D + 2 * H], FP, c)
        av = sb(f"av{n}", [P, 2, D], FP, c)
        t = sb(f"avt{n}", [P, 2, D], FP, c)
        load(f"wg{n}", [(w[:, :, 0:D], w_view(gat_w[n])),
                        (av[:, 0, :], gat_al[n].rearrange("h d -> (h d)").partition_broadcast(P)),
                        (av[:, 1, :], gat_ar[n].rearrange("h d -> (h d)").partition_broadcast(P))])
        s = sem(f"wgchain{n}")
        with nc.Block() as block:
            @block.vector
            def _(dve):
                ch = Chain(dve, s)
                for q in range(2):
                    ch.link(nc.vector.tensor_tensor(t[:], w[:, :, 0:D], av[:, q:q + 1, :].to_broadcast([P, 2, D]), ALU.mult))
                    for k in range(2):
                        ch.link(nc.vector.tensor_reduce(w[:, k, D + q * H:D + (q + 1) * H], heads(t[:, k, :]),
                                                        op=ALU.add, axis=AX.X))
        return w

    def gat_table(c, n, fill, fill_links, table):
        w = gat_weights(c, n)
        ob = sb(f"obg{n}", [P, 2, W4], FP, c)

        def head_rows(ch, i, u, b):
            nc.scalar.copy(heads(ob[:, u, :])[:, :, 0:DH], heads(b[:, 0:D]))
            nc.scalar.copy(heads(ob[:, u, :])[:, :, DH:DH + 1].rearrange("p h o -> p (h o)"), b[:, D:D + H])
            return nc.scalar.copy(er_all[:, bass.ds(i, 1), :].rearrange("p o h -> p (o h)"), b[:, D + H:D + 2 * H])
        project(f"g{n}", w, [D + 2 * H], fill, fill_links, {0: head_rows}, {}, ob=ob, table=rows_of(table), keep=True)
        r = sb(f"er_rest{n}", [P, NBA, H], FP, c)
        s = sem(f"er_chain{n}")
        with nc.Block() as block:
            @block.vector
            def _(dve):
                ch = Chain(dve, s)
                part = lambda q: er3[:, :, :, q:q + 1].rearrange("p b h o -> p b (h o)")
                ch.link(nc.vector.tensor_copy(part(0), er_all[:]))
                ch.link(nc.vector.tensor_tensor(r[:], er_all[:], part(0), ALU.subtract))
                ch.link(nc.vector.tensor_copy(part(1), r[:]))
                ch.link(nc.vector.tensor_tensor(r[:], r[:], part(1), ALU.subtract))
                ch.link(nc.vector.tensor_copy(part(2), r[:]))

    def aggregate_gat(name, table):
        c = ExitStack()
        rows = sb(f"rows_{name}", [P, NBUF, U, W4], FP, c)
        hot = sb(f"hot_{name}", [P, NBUF, U, P], FP, c)
        hot_t = sb(f"hott_{name}", [P, NBUF, U * P], BF, c)
        dst_t = sb(f"dstt_{name}", [P, NBUF, U * P], BF, c)
        starts = sb(f"starts_{name}", [H, NBUF, U * P], BF, c)
        ends = sb(f"ends_{name}", [H, NBUF, U * P], BF, c)
        fwd = sb(f"fwd_{name}", [H, NBUF, U * P], FP, c)
        back = sb(f"back_{name}", [H, U * P], FP, c)
        el = sb(f"el_{name}", [P, U, H], FP, c)
        er = sb(f"er_{name}", [P, U + 1, H], FP, c)
        z = sb(f"z_{name}", [P, 2, U + 1, H], FP, c)
        ex = sb(f"ex_{name}", [P, NBUF, U + 1, H], FP, c)
        am = sb(f"am_{name}", [1, H], FP, c)
        fac = sb(f"fac_{name}", [P, H], FP, c)
        stage = sb(f"stage_{name}", [P, NBUF, U], I32, c)
        names = ("pair", "added", "hot", "hott", "el", "elt", "er", "fwd", "back", "backt", "zr", "ex", "am", "fac",
                 "rescaled", "scaled", "erread", "zchain", "half")
        (pair_done, added, hot_ready, hott_ready, el_ready, elt_done, er_done, fwd_done, back_done, backt_done, z_ready,
         ex_ready, am_ready, fac_done, rescaled, scaled, er_read, zch, half) = (sem(f"{q}_{name}") for q in names)
        staged = [sem(f"staged_{name}{u}") for u in range(NBUF)]
        flags = [sem(f"flags_{name}{u}") for u in range(NBUF)]
        base = list(used)
        for u in range(NBUF):
            used[u] += full_iters + (u < left)
        credit = NBUF * U // 2
        el_t = [ps[4], ps[5]]
        er_bank, misc = ps[6], ps[7]
        HU = U // 2
        back_t = misc[:, 0:(U + 1) * H].rearrange("p (s h) -> p s h", h=H)
        fac_bank = misc[:, 64:64 + H]

        def both_ends(eng, step):
            step((0, 0), None)
            with eng.Fori(0, full_iters) as i:
                for u in range(NBUF):
                    step(nxt(i, u), (i, u))
            for u in range(left):
                step((full_iters, u + 1) if u + 1 < left else None, (full_iters, u))

        with nc.Block() as block:
            @block.gpsimd
            def _(pool):
                nc.gpsimd.memset(hot[:], 0.0).then_inc(pair_done, credit)
                gather_batches(pool, rows, W4, table, stage, staged, pair_done, base)

            @block.sync
            def _(sp):
                sp.sem_inc(back_done, NBUF)
                sp.sem_inc(hott_ready, NBUF)

                def batch(i, u, reused=True):
                    k = i * NBUF + u
                    if reused:
                        for j in range(U):
                            sp.wait_ge(slot_full[u * U + j], i * 16 + 16 * base[u])
                    sp.dma_start(stage[:, u, :], rows_src[:, bass.ds(k * U, U)]).then_inc(staged[u], 16)
                    sp.wait_ge(hott_ready, k + 1)
                    sp.wait_ge(back_done, k + 1)
                    for to, of, n in ((dst_t, dloc_dram, P), (starts, starts_dram, H), (ends, ends_dram, H)):
                        sp.dma_start(to[:, u, :], of[bass.ds(k * U, U), :].rearrange("s e -> (s e)")
                                     .partition_broadcast(n)).then_inc(flags[u], 16)
                for u in range(NBUF):
                    batch(0, u, reused=False)
                with sp.Fori(1, full_iters) as i:
                    for u in range(NBUF):
                        batch(i, u)
                for u in range(left):
                    batch(full_iters, u)

            @block.vector
            def _(dve):
                nc.vector.memset(agg[:], 0.0).then_inc(added, U // 2)
                nc.vector.memset(fwd[:], -BIG).then_inc(fwd_done, 1)
                dve.wait_ge(pair_done, credit)
                dve.sem_inc(elt_done, 1)
                dve.sem_inc(er_done, NBUF)
                dve.sem_inc(backt_done, 2)
                dve.sem_inc(ex_ready, 1)
                dve.sem_inc(fac_done, 1)

                def one_hots(i, u):
                    k = i * NBUF + u
                    for j in range(U):
                        dve.wait_ge(slot_full[u * U + j], i * 16 + 16 * (base[u] + 1))
                    dve.wait_ge(elt_done, k + 1)
                    nc.vector.tensor_tensor(
                        el[:], rows[:, u, :, :].rearrange("p s (h w) -> p s h w", h=H)[:, :, :, DH:DH + 1]
                        .rearrange("p s h o -> p s (h o)"),
                        mneg[:, bass.ds(k * U, U)].unsqueeze(2).to_broadcast([P, U, H]), ALU.add).then_inc(el_ready, 1)
                    dve.wait_ge(flags[u], i * 48 + 48)
                    dve.wait_ge(er_done, k + 1)
                    nc.vector.tensor_scalar(hot_t[:, u, :], dst_t[:, u, :], iota_p[:], None,
                                            ALU.is_equal).then_inc(hott_ready, 1)
                    dve.wait_ge(pair_done, (k + 1) * HU)
                    nc.vector.tensor_tensor(
                        hot[:, u, :, :], iota_f[:].unsqueeze(1).to_broadcast([P, U, P]),
                        dloc[:, bass.ds(k * U, U)].unsqueeze(2).to_broadcast([P, U, P]),
                        ALU.is_equal).then_inc(hot_ready, 1)

                def forward(i, u):
                    k = i * NBUF + u
                    prev = fwd[:, (u - 1) % NBUF, U * P - 1:U * P]
                    dve.wait_ge(elt_done, k + 2)
                    dve.wait_ge(fwd_done, k + 1)
                    dve.wait_ge(backt_done, k + 1)
                    nc.vector.tensor_tensor_scan(fwd[:, u, 0:HU * P], starts[:, u, 0:HU * P], el_t[0][0:H, 0:HU * P],
                                                 prev, ALU.add, ALU.max).then_inc(half, 1)
                    dve.wait_ge(half, k + 1)
                    nc.vector.tensor_tensor_scan(fwd[:, u, HU * P:], starts[:, u, HU * P:], el_t[1][0:H, 0:HU * P],
                                                 fwd[:, u, HU * P - 1:HU * P], ALU.add, ALU.max).then_inc(fwd_done, 1)

                def backward(i, u):
                    k = i * NBUF + u
                    dve.wait_ge(fwd_done, k + 2)
                    dve.wait_ge(backt_done, k + 2)
                    nc.vector.tensor_tensor_scan(back[:, ::-1], ends[:, u, ::-1], fwd[:, u, ::-1], -BIG,
                                                 ALU.add, ALU.max).then_inc(back_done, 1)

                def logits(i, u):
                    k = i * NBUF + u
                    ch = Chain(dve, zch, k * 6)
                    dve.wait_ge(er_done, k + (NBUF + 1))
                    ch.link(nc.vector.tensor_reduce(er[:, 0:U, :], er_bank[:, 0:U * H * 3]
                                                    .rearrange("p (s h q) -> p s h q", h=H, q=3), op=ALU.add, axis=AX.X))
                    ch.link(nc.vector.tensor_copy(er[:, U, :], er[:, 0, :]))
                    dve.wait_ge(ex_ready, k + 1)
                    nc.vector.tensor_tensor(z[:, 0, 0:U, :], el[:], er[:, 0:U, :], ALU.add).then_inc(er_read, 1)
                    dve.wait_ge(backt_done, k + 3)
                    nc.vector.tensor_tensor(z[:, 0, U, :], back_t[:, U, :], er[:, U, :], ALU.add)
                    nc.vector.tensor_tensor(z[:, 1, 0:U, :], back_t[:, 0:U, :], er[:, 0:U, :], ALU.add)
                    ch.link(nc.vector.tensor_tensor(z[:, 1, U, :], back_t[:, 0, :], er[:, U, :], ALU.add))
                    flat = z[:].rearrange("p a s h -> p (a s h)")
                    ch.link(nc.vector.scalar_tensor_tensor(out=flat, in0=flat, scalar=0.2, in1=flat, op0=ALU.mult, op1=ALU.max))
                    ch.link(nc.vector.tensor_tensor(z[:, 0], z[:, 0], z[:, 1], ALU.subtract))
                    ch.link(nc.vector.tensor_scalar(z[:, 0], z[:, 0], 0.0, None, ALU.min))
                    dve.sem_inc(z_ready, 1)

                def rescale(i, u, blocks):
                    k = i * NBUF + u
                    dve.wait_ge(ex_ready, k + 2)
                    dve.wait_ge(fac_done, k + 1)
                    nc.vector.tensor_scalar(am[:], ex[0:1, u, U, :], -1.0, cont[:, bass.ds(k * U, 1)],
                                            ALU.add, ALU.mult).then_inc(am_ready, 1)
                    dve.wait_ge(fac_done, k + 2)
                    dve.wait_ge(added, k * HU + HU)
                    nc.vector.tensor_scalar(fac[:], fac_bank, 1.0, None, ALU.add).then_inc(rescaled, 1)
                    dve.wait_ge(rescaled, k * 2 + 2)
                    acc = agg[:, bass.ds(blocks[0], 1), :].rearrange("p o (h w) -> p (o h) w", h=H)
                    nc.vector.tensor_tensor(acc, acc, fac[:].unsqueeze(2).to_broadcast([P, H, W4 // H]),
                                            ALU.mult).then_inc(rescaled, 1)

                def accumulate(i, u, blocks, pairs):
                    k = i * NBUF + u
                    for j in pairs:
                        if j == 0:
                            dve.wait_ge(rescaled, k * 2 + 3)
                        dve.wait_ge(pair_done, k * HU + (credit + j + 1))
                        dve.wait_ge(added, k * HU + (HU + j))
                        acc = agg[:, bass.ds(blocks[j], 1), :].rearrange("p o w -> p (o w)")
                        nc.vector.tensor_tensor(acc, acc, ps[j][:, 0:W4], ALU.add).then_inc(added, 1)

                def step(nx, this):
                    if this:
                        blocks = pair_blocks(dve, this[0] * NBUF + this[1])
                    if nx:
                        one_hots(*nx)
                        forward(*nx)
                    if this:
                        rescale(*this, blocks)
                        accumulate(*this, blocks, (0, 1))
                    if nx:
                        backward(*nx)
                    if this:
                        accumulate(*this, blocks, (2, 3))
                    if nx:
                        logits(*nx)
                dve.sem_inc(rescaled, 1)
                both_ends(dve, step)

            @block.scalar
            def _(act):
                act.sem_inc(er_read, 1)
                act.sem_inc(z_ready, 1)
                act.sem_inc(am_ready, NBUF)

                def batch(i, u):
                    k = i * NBUF + u
                    act.wait_ge(z_ready, k + 2)
                    act.wait_ge(am_ready, k + 1)
                    nc.scalar.activation(ex[:, u], z[:, 0], ACT.Exp).then_inc(ex_ready, 1)
                    act.wait_ge(ex_ready, k + 2)
                    by_head = rows[:, u, :, :].rearrange("p s (h w) -> p s h w", h=H)
                    nc.scalar.copy(by_head[:, :, :, DH:DH + 1].rearrange("p s h o -> p s (h o)"), ex[:, u, 0:U, :])
                    for s in range(U):
                        for h in range(H):
                            a = by_head[:, s, h, 0:DH]
                            ins = nc.scalar.mul(a, a, ex[:, u, s, h:h + 1])
                        if s % 2:
                            ins.then_inc(scaled, 1)
                each_batch(act, batch)

            @block.tensor
            def _(pe):
                def turn(i, u):
                    k = i * NBUF + u
                    pe.wait_ge(el_ready, k + 1)
                    pe.wait_ge(fwd_done, k + 1)
                    for s in range(U):
                        ins = nc.tensor.transpose(el_t[s // HU][0:H, (s % HU) * P:(s % HU + 1) * P], el[:, s, :], ident[:])
                    ins.then_inc(elt_done, 1)

                def er_of_edges(i, u, blocks):
                    k = i * NBUF + u
                    pe.wait_ge(hott_ready, k + (NBUF + 1))
                    pe.wait_ge(er_read, k + 1)
                    for s in range(U):
                        ins = nc.tensor.matmul(er_bank[:, s * 3 * H:(s + 1) * 3 * H], hot_t[:, u, s * P:(s + 1) * P],
                                               er3[:, bass.ds(blocks[s // 2], 1), :, :].rearrange("p o h q -> p (o h q)"),
                                               start=True, stop=True)
                    ins.then_inc(er_done, 1)

                def factor(i, u):
                    k = i * NBUF + u
                    pe.wait_ge(am_ready, k + (NBUF + 1))
                    pe.wait_ge(hot_ready, k + 1)
                    pe.wait_ge(rescaled, k * 2 + 1)
                    nc.tensor.matmul(fac_bank, hot[0:1, u, 0, :], am[:], start=True, stop=True).then_inc(fac_done, 1)

                def turn_back(i, u):
                    k = i * NBUF + u
                    pe.wait_ge(back_done, k + (NBUF + 1))
                    wait_apart(pe, z_ready, k + 1, waits_met)
                    for s in range(U):
                        nc.tensor.transpose(back_t[:, s, :], back[:, s * P:(s + 1) * P], ident[0:H, 0:H])
                    prev = fwd[:, (u - 1) % NBUF, U * P - 1:U * P]
                    nc.tensor.matmul(back_t[:, U, :], prev.to_broadcast([H, P]), ident[0:H, 0:H],
                                     start=True, stop=True).then_inc(backt_done, 1)

                def sums(i, u, pairs):
                    k = i * NBUF + u
                    for j in pairs:
                        pe.wait_ge(scaled, k * HU + (j + 1))
                        pe.wait_ge(added, k * HU + (j + 1))
                        for s in (2 * j, 2 * j + 1):
                            mm = nc.tensor.matmul(ps[j][:, 0:W4], hot[:, u, s, :], rows[:, u, s, :],
                                                  start=s % 2 == 0, stop=s % 2 == 1)
                        mm.then_inc(pair_done, 1)

                def step(nx, this):
                    if nx:
                        blocks = pair_blocks(pe, nx[0] * NBUF + nx[1])
                        turn(*nx)
                        er_of_edges(*nx, blocks)
                    if this:
                        factor(*this)
                        sums(*this, (0, 1))
                    if nx:
                        turn_back(*nx)
                    if this:
                        sums(*this, (2, 3))
                both_ends(pe, step)
        c.close()

    def gat_fill(ch, i, nb):
        a = agg[:, bass.ds(i, 1), :].rearrange("p o (h w) -> p (o h) w", h=H)[:, :, 0:DH]
        ch.link(nc.vector.tensor_tensor(heads(nb), a, rden[:, bass.ds(i, 1), :].rearrange("p o h -> p (o h)")
                                        .unsqueeze(2).to_broadcast([P, H, DH]), ALU.mult))
        ch.link(nc.vector.tensor_tensor(nb, nb, blk1(cur, i), ALU.add))
        return nc.vector.tensor_scalar(nb, nb, 0.0, None, ALU.max)

    def weight_sums(n):
        s = sem(f"rden{n}")
        with nc.Block() as block:
            @block.vector
            def _(dve):
                ch = Chain(dve, s)
                den = agg[:].rearrange("p b (h w) -> p b h w", h=H)[:, :, :, DH:DH + 1].rearrange("p b h o -> p b (h o)")
                ch.link(nc.vector.tensor_scalar(rden[:], den, 1e-9, None, ALU.max))
                ch.link(nc.vector.reciprocal(rden[:], rden[:]))

    def layer2():
        for n in range(3):
            c = ExitStack()
            if n:
                weight_sums(n)
                gat_table(c, n, gat_fill, 2, tables[1 + n])
            else:
                gat_table(c, n, normalised, 0, tables[1])
                load("keep_x2", [(x2_dram.rearrange("(b p) d -> p b d", p=P), cur[:])])
            c.close()
            clear_sems()
            aggregate_gat(f"a{2 + n}", tables[1 + n])
            clear_sems()
        weight_sums(3)
        load("x2_back", [(cur[:], x2_dram.rearrange("(b p) d -> p b d", p=P))])
        c = ExitStack()
        t = sb("h3", [P, D], FP, c)
        s = sem("h3_chain")

        def combine(ch, g):
            for j in range(G):
                i = g * G + j
                a = agg[:, bass.ds(i, 1), :].rearrange("p o (h w) -> p (o h) w", h=H)[:, :, 0:DH]
                ch.link(nc.vector.tensor_tensor(heads(t[:]), a, rden[:, bass.ds(i, 1), :].rearrange("p o h -> p (o h)")
                                                .unsqueeze(2).to_broadcast([P, H, DH]), ALU.mult))
                ch.link(nc.vector.scalar_tensor_tensor(out=blk1(cur, i), in0=t[:], scalar=0.0, in1=blk1(cur, i),
                                                       op0=ALU.max, op1=ALU.add), plain=True)
        row_stats("x3", combine, 2 * G)
        c.close()
        clear_sems()

    def layer3():
        c = ExitStack()
        w = sb("w3s", [P, 2, D], FP, c)
        ob = sb("ob5", [P, 2, D], FP, c)
        load("w3", [(w[:], w_view(w3))])
        project("l3", w, [D], normalised, 0,
                {0: lambda ch, i, u, b: nc.scalar.mul(ob[:, u, :], b, dinv[:, bass.ds(i, 1)])}, {},
                ob=ob, table=rows_of(tables[4]), keep=True)
        c.close()
        clear_sems()
        aggregate("a5", tables[4], rows_src, False)
        clear_sems()

        def combine(ch, g):
            ch.link(nc.vector.tensor_tensor(grp(agg, g), grp(agg, g), dinv[:, bass.ds(g * G, G)].unsqueeze(2)
                                            .to_broadcast([P, G, D]), ALU.mult))
            ch.link(nc.vector.tensor_tensor(grp(cur, g), grp(cur, g), grp(agg, g), ALU.add), plain=True)
        row_stats("x4", combine, 2)

    def store_out():
        ready, so = sem("out_ready"), sem("out_stored")
        with nc.Block() as block:
            @block.vector
            def _(dve):
                with dve.Fori(0, NB) as i:
                    normalised(None, i, blk1(cur, i)).then_inc(ready, 1)

            @block.sync
            def _(sp):
                with sp.Fori(0, NB - 1) as i:
                    sp.wait_ge(ready, i + 1)
                    sp.dma_start(out[bass.ds(i * P, P), :], blk1(cur, i)).then_inc(so, 16)
                sp.wait_ge(ready, NB)
                sp.dma_start(out[(NB - 1) * P:N, :], cur[0:LAST, NB - 1, :]).then_inc(so, 16)
                sp.wait_ge(so, 16 * NB)

    c = ExitStack()
    make_steps(c, raw_edges(c))
    c.close()
    clear_sems()
    layer0()
    clear_sems()
    aggregate("a0", table0, row0, True)
    clear_sems()
    degrees()
    layer1_table()
    clear_sems()
    aggregate("a1", tables[0], rows_src, False)
    clear_sems()
    layer1_end()
    clear_sems()
    layer2()
    layer3()
    store_out()
    ctx.close()


def kernel(x, src, dst, edge_type_8, L0_gnn_weight, L0_gnn_h_bias, L0_gnn_loop_weight, L1_gnn_W_l, L1_gnn_b_l,
           L1_gnn_W_r, L1_gnn_gamma, L1_gnn_beta, L2_gnn_W0, L2_gnn_al0, L2_gnn_ar0, L2_gnn_W1, L2_gnn_al1,
           L2_gnn_ar1, L2_gnn_W2, L2_gnn_al2, L2_gnn_ar2, L3_gnn_W):
    import numpy as np
    import concourse.bacc as bacc
    from concourse import mybir as mb
    from concourse.bass_utils import run_bass_kernel_spmd

    nc = bacc.Bacc("TRN2", target_bir_lowering=False, num_devices=1)
    arrays = {}

    def given(name, a):
        a = np.ascontiguousarray(a)
        arrays[name] = a
        return nc.dram_tensor(name, a.shape, mb.dt.from_np(a.dtype), kind="ExternalInput").ap()

    args = [given("in_x", x), given("in_src", src), given("in_dst", dst), given("in_type", edge_type_8),
            given("in_w_rel", L0_gnn_weight), given("in_h_bias", L0_gnn_h_bias), given("in_w_loop", L0_gnn_loop_weight),
            given("in_w_l", np.asarray(L1_gnn_W_l).T), given("in_b_l", L1_gnn_b_l), given("in_w_r", np.asarray(L1_gnn_W_r).T),
            given("in_gamma", L1_gnn_gamma), given("in_beta", L1_gnn_beta),
            [given(f"in_gat_w{i}", a) for i, a in enumerate((L2_gnn_W0, L2_gnn_W1, L2_gnn_W2))],
            [given(f"in_gat_al{i}", a) for i, a in enumerate((L2_gnn_al0, L2_gnn_al1, L2_gnn_al2))],
            [given(f"in_gat_ar{i}", a) for i, a in enumerate((L2_gnn_ar0, L2_gnn_ar1, L2_gnn_ar2))],
            given("in_w3", L3_gnn_W)]
    out = nc.dram_tensor("out_0_dram", (N, D), FP, kind="ExternalOutput").ap()
    build(nc, *args, out)
    r = run_bass_kernel_spmd(nc, [arrays], core_ids=[0])
    return r.results[0]["out_0_dram"]
```

```python
import concourse.bass as bass
from concourse import mybir
from contextlib import ExitStack

FP = mybir.dt.float32
BF = mybir.dt.bfloat16
I32 = mybir.dt.int32
ALU = mybir.AluOpType
ACT = mybir.ActivationFunctionType
AX = mybir.AxisListType

P = 128
N = 6250
E = 100000
D = 256
H = 4
DH = D // H
R = 8
NB = -(-N // P)
NBA = NB + 1
NP = NBA * P
LAST = N - (NB - 1) * P
T = -(-E // P)
TAIL = E - (T - 1) * P
CH = -(-T // P)
U = 8
NBUF = 4
S = -(-(T + NB - 1 + NB) // (2 * U)) * 2 * U
K = S // U
SC = -(-(S + U) // P)
SP_ = SC * P
RT = SC * P
NODST = 7000
NF = 5
BIG = 3.0e38
W4 = D + H
LN_EPS = 1e-5
BN_EPS = 1e-5
L2_EPS = 1e-12
HALF = 0.5 ** 0.5


class Chain:

    def __init__(self, eng, sem, at=0, passed=None):
        self.eng, self.sem, self.at, self.n, self.passed = eng, sem, at, 0, passed

    def link(self, ins, plain=False):
        self.n += 1
        ins.then_inc(self.sem, 1)
        if plain:
            wait_apart(self.eng, self.sem, self.at + self.n, self.passed)
        else:
            self.eng.wait_ge(self.sem, self.at + self.n)


def wait_apart(eng, sem, value, passed):
    eng.wait_ge(sem, value)
    eng.sem_inc(passed, 1)


def build(nc, x, src, dst, etype, w_rel, h_bias, w_loop, w_l, b_l, w_r, gamma, beta,
          gat_w, gat_al, gat_ar, w3, out):
    ctx = ExitStack()
    sems = {}

    def sb(name, shape, dt, c=None):
        return (c or ctx).enter_context(nc.sbuf_tensor(name, shape, dt))

    def sem(name):
        if name not in sems:
            sems[name] = nc.alloc_semaphore(name=name)
        return sems[name]

    tiles_gathered = nc.alloc_semaphore(name="tiles_gathered")
    waits_met = nc.alloc_semaphore(name="waits_met")

    def clear_sems():
        numbers = sorted(s.num for s in sems.values())
        with nc.Block() as block:
            @block.gpsimd
            def _(pool):
                while numbers:
                    lo = hi = numbers.pop(0)
                    while numbers and numbers[0] == hi + 1:
                        hi = numbers.pop(0)
                    pool.sem_clear(range(lo, hi + 1))
        for s in sems.values():
            nc.release_semaphore(s)
        sems.clear()

    cur = sb("cur", [P, NBA, D], FP)
    agg = sb("agg", [P, NBA, W4], FP)
    row0 = sb("row0", [P, SP_], I32)
    rows_src = sb("rows_src", [P, SP_], I32)
    dloc = sb("dloc", [P, SP_], FP)
    mneg = sb("mneg", [P, SP_], FP)
    cont = sb("cont", [1, SP_ // U], FP)
    packed = sb("packed", [1, K], I32)
    deg = sb("deg", [P, NBA], FP)
    rdeg = sb("rdeg", [P, NBA], FP)
    dinv = sb("dinv", [P, NBA], FP)
    ident = sb("ident", [P, P], FP)
    iota_f = sb("iota_f", [P, P], FP)
    iota_p = sb("iota_p", [P, 1], FP)
    ones = sb("ones", [P, P], FP)
    eps = sb("eps", [P, 1], FP)
    ps = [ctx.enter_context(nc.psum_tensor(f"ps{i}", [P, 512], FP)) for i in range(8)]

    table0 = nc.dram_tensor("table0", (R * NP, D), FP, kind="Internal").ap()
    tables = [nc.dram_tensor(f"table{i}", (NP, W4 if i in (2, 3, 4) else D), FP, kind="Internal").ap()
              for i in range(1, 6)]
    tiles_dram = nc.dram_tensor("tiles_dram", (RT, NF * P), FP, kind="Internal").ap()
    dloc_dram = nc.dram_tensor("dloc_dram", (SP_, P), BF, kind="Internal").ap()
    starts_dram = nc.dram_tensor("starts_dram", (SP_, P), BF, kind="Internal").ap()
    ends_dram = nc.dram_tensor("ends_dram", (SP_, P), BF, kind="Internal").ap()
    x2_dram = nc.dram_tensor("x2_dram", (NBA * P, D), FP, kind="Internal").ap()

    def raw_edges(c):
        dst_i = sb("dst_i", [P, SC, P], I32, c)
        prev_i = sb("prev_i", [P, SC, P], I32, c)
        next_i = sb("next_i", [P, SC, P], I32, c)
        src_i = sb("src_i", [P, SC, P], I32, c)
        typ_i = sb("typ_i", [P, SC, P], I32, c)
        f = sb("fields", [P, SC, NF, P], FP, c)
        m, ld, st, ch_sem = sem("raw_memset"), sem("raw_loaded"), sem("raw_stored"), sem("raw_chain")
        full = CH - 1
        rest = T - 1 - full * P
        e0 = full * P * P

        with nc.Block() as block:
            @block.gpsimd
            def _(pool):
                nc.gpsimd.memset(dst_i[:, full, :], NODST)
                nc.gpsimd.memset(prev_i[:, full, :], NODST)
                nc.gpsimd.memset(prev_i[0:1, 0, 0:1], -1)
                nc.gpsimd.memset(next_i[:, full, :], NODST)
                nc.gpsimd.memset(src_i[:, full, :], 0)
                nc.gpsimd.memset(typ_i[:, full, :], 0)
                nc.gpsimd.memset(ident[:], 0.0)
                nc.gpsimd.memset(ones[:], 1.0)
                nc.gpsimd.memset(eps[:], LN_EPS).then_inc(m, 1)
                pool.wait_ge(m, 1)
                nc.gpsimd.affine_select(out=ident[:], in_=ident[:], compare_op=ALU.not_equal, fill=1.0,
                                        base=0, pattern=[[-1, P]], channel_multiplier=1)
                nc.gpsimd.iota(iota_f[:], [[1, P]], base=0, channel_multiplier=0,
                               allow_small_or_imprecise_dtypes=True)
                nc.gpsimd.iota(iota_p[:], [[0, 1]], base=0, channel_multiplier=1,
                               allow_small_or_imprecise_dtypes=True)

            @block.sync
            def _(sp):
                sp.wait_ge(m, 1)
                n = 0
                for tile, a in ((dst_i, dst), (src_i, src), (typ_i, etype)):
                    sp.dma_start(tile[:, 0:full, :], a[0:e0].rearrange("(c p e) -> p c e", p=P, e=P)).then_inc(ld, 16)
                    sp.dma_start(tile[0:rest, full, :], a[e0:e0 + rest * P].rearrange("(p e) -> p e", e=P)).then_inc(ld, 16)
                    sp.dma_start(tile[rest:rest + 1, full, 0:TAIL],
                                 a[E - TAIL:E].rearrange("(p e) -> p e", p=1)).then_inc(ld, 16)
                    n += 48
                sp.dma_start(prev_i[:, 1:full, :], dst[P * P - 1:e0 - 1].rearrange("(c p e) -> p c e", p=P, e=P)).then_inc(ld, 16)
                sp.dma_start(prev_i[1:P, 0, :], dst[P - 1:P * P - 1].rearrange("(p e) -> p e", e=P)).then_inc(ld, 16)
                sp.dma_start(prev_i[0:1, 0, 1:P], dst[0:P - 1].rearrange("(p e) -> p e", p=1)).then_inc(ld, 16)
                sp.dma_start(prev_i[0:rest, full, :], dst[e0 - 1:e0 - 1 + rest * P].rearrange("(p e) -> p e", e=P)).then_inc(ld, 16)
                sp.dma_start(prev_i[rest:rest + 1, full, 0:TAIL],
                             dst[E - TAIL - 1:E - 1].rearrange("(p e) -> p e", p=1)).then_inc(ld, 16)
                sp.dma_start(next_i[:, 0:full, :], dst[1:e0 + 1].rearrange("(c p e) -> p c e", p=P, e=P)).then_inc(ld, 16)
                sp.dma_start(next_i[0:rest, full, :], dst[e0 + 1:e0 + 1 + rest * P].rearrange("(p e) -> p e", e=P)).then_inc(ld, 16)
                sp.dma_start(next_i[rest:rest + 1, full, 0:TAIL - 1],
                             dst[E - TAIL + 1:E].rearrange("(p e) -> p e", p=1)).then_inc(ld, 16)
                n += 16 * 8
                sp.wait_ge(ld, n)

        assert SC == CH
        with nc.Block() as block:
            @block.vector
            def _(dve):
                ch = Chain(dve, ch_sem)
                nc.vector.tensor_copy(f[:, :, 0, :], dst_i[:])
                nc.vector.tensor_copy(f[:, :, 1, :], src_i[:])
                ch.link(nc.vector.tensor_copy(f[:, :, 2, :], typ_i[:]))
                ch.link(nc.vector.scalar_tensor_tensor(out=f[:, :, 2, :], in0=f[:, :, 2, :], scalar=float(NP),
                                                       in1=f[:, :, 1, :], op0=ALU.mult, op1=ALU.add))
                nc.vector.tensor_tensor(f[:, :, 3, :], dst_i[:], prev_i[:], ALU.not_equal)
                ch.link(nc.vector.tensor_tensor(f[:, :, 4, :], dst_i[:], next_i[:], ALU.not_equal))

        with nc.Block() as block:
            @block.sync
            def _(sp):
                sp.dma_start(tiles_dram.rearrange("(c p) w -> p c w", p=P),
                             f[:].rearrange("p c f e -> p c (f e)")).then_inc(st, 16)
                sp.wait_ge(st, 16)
        return f

    def make_steps(c, f):
        thr = sb("thr", [P, NB], FP, c)
        cmp_lo = sb("cmp_lo", [P, NB, CH], FP, c)
        cmp_hi = sb("cmp_hi", [P, NB, CH], FP, c)
        cnt = sb("cnt", [P, 2 * NB], FP, c)
        first = sb("first", [P, NB], FP, c)
        num = sb("num", [P, NB], FP, c)
        odd_i = sb("odd_i", [P, NB], I32, c)
        odd = sb("odd", [P, NB], FP, c)
        zero = sb("zero", [P, NB], FP, c)
        cum = sb("cum", [P, NB], FP, c)
        cum0 = sb("cum0", [P, NB], FP, c)
        shift = sb("shift", [P, NB], FP, c)
        step = sb("step", [P, SC], FP, c)
        ind = sb("ind", [P, SC, NB], FP, c)
        ind0 = sb("ind0", [P, SC, NB], FP, c)
        blk = sb("blk", [P, SC], FP, c)
        til = sb("til", [P, SC], FP, c)
        til_i = sb("til_i", [P, SC], I32, c)
        blk128 = sb("blk128", [P, SC], FP, c)
        brow = sb("brow", [1, SP_], FP, c)
        crow = sb("crow", [1, SP_], FP, c)
        pk = sb("pk", [1, 4, K], FP, c)
        a_s, b_s, g_s, t_s = sem("steps_thr"), sem("steps_cmp"), sem("steps_sum"), sem("steps_tiles")
        ch_sem = sem("steps_chain")

        with nc.Block() as block:
            @block.gpsimd
            def _(pool):
                nc.gpsimd.iota(thr[:], [[P, NB]], base=0, channel_multiplier=0,
                               allow_small_or_imprecise_dtypes=True)
                nc.gpsimd.iota(step[:], [[P, SC]], base=0, channel_multiplier=1,
                               allow_small_or_imprecise_dtypes=True)
                nc.gpsimd.memset(zero[:], 0.0).then_inc(a_s, 1)

            @block.vector
            def _(dve):
                ch = Chain(dve, ch_sem)
                dve.wait_ge(a_s, 1)
                nc.vector.tensor_tensor(cmp_hi[:], f[:, 0:CH, 0, P - 1:P].rearrange("p c o -> p o c").to_broadcast([P, NB, CH]),
                                        thr[:].unsqueeze(2).to_broadcast([P, NB, CH]), ALU.is_lt)
                ch.link(nc.vector.tensor_scalar(num[:], thr[:], float(P), None, ALU.add))
                ch.link(nc.vector.tensor_tensor(cmp_lo[:], f[:, 0:CH, 0, 0:1].rearrange("p c o -> p o c").to_broadcast([P, NB, CH]),
                                                num[:].unsqueeze(2).to_broadcast([P, NB, CH]), ALU.is_lt))
                nc.vector.tensor_reduce(cnt[:, 0:NB], cmp_hi[:], op=ALU.add, axis=AX.X)
                ch.link(nc.vector.tensor_reduce(cnt[:, NB:2 * NB], cmp_lo[:], op=ALU.add, axis=AX.X))
                nc.vector.tensor_copy(first[:], zero[:]).then_inc(b_s, 1)
                dve.wait_ge(g_s, 1)
                ch.link(nc.vector.tensor_copy(cnt[:], ps[0][:, 0:2 * NB]))
                ch.link(nc.vector.tensor_copy(first[:], cnt[:, 0:NB]))
                ch.link(nc.vector.tensor_tensor(num[:], cnt[:, NB:2 * NB], first[:], ALU.subtract))
                ch.link(nc.vector.tensor_scalar(num[:], num[:], 1.0, None, ALU.max))
                ch.link(nc.vector.tensor_copy(odd_i[:], num[:]))
                ch.link(nc.vector.tensor_scalar(odd_i[:], odd_i[:], 1, None, ALU.bitwise_and))
                ch.link(nc.vector.tensor_copy(odd[:], odd_i[:]))
                ch.link(nc.vector.tensor_tensor(num[:], num[:], odd[:], ALU.add))
                ch.link(nc.vector.tensor_tensor_scan(cum[:], num[:], zero[:], 0.0, ALU.add, ALU.add))
                ch.link(nc.vector.tensor_tensor(cum0[:], cum[:], num[:], ALU.subtract))
                ch.link(nc.vector.tensor_tensor(shift[:], first[:], cum0[:], ALU.subtract))
                nc.vector.tensor_tensor(ind[:], cum[:].unsqueeze(1).to_broadcast([P, SC, NB]),
                                        step[:].unsqueeze(2).to_broadcast([P, SC, NB]), ALU.is_le)
                ch.link(nc.vector.tensor_tensor(ind0[:], cum0[:].unsqueeze(1).to_broadcast([P, SC, NB]),
                                                step[:].unsqueeze(2).to_broadcast([P, SC, NB]), ALU.is_le))
                nc.vector.tensor_reduce(blk[:], ind[:], op=ALU.add, axis=AX.X)
                ch.link(nc.vector.tensor_tensor(ind0[:], ind0[:], ind[:], ALU.subtract))
                ch.link(nc.vector.tensor_tensor(ind0[:], ind0[:], shift[:].unsqueeze(1).to_broadcast([P, SC, NB]), ALU.mult))
                ch.link(nc.vector.tensor_reduce(til[:], ind0[:], op=ALU.add, axis=AX.X))
                ch.link(nc.vector.tensor_tensor(til[:], til[:], step[:], ALU.add))
                nc.vector.tensor_scalar(blk128[:], blk[:], float(P), None, ALU.mult)
                nc.vector.tensor_copy(til_i[:], til[:]).then_inc(t_s, 1)

            @block.tensor
            def _(pe):
                pe.wait_ge(b_s, 1)
                nc.tensor.matmul(ps[0][:, 0:2 * NB], ones[:], cnt[:], start=True, stop=True).then_inc(g_s, 1)

        sf = f
        ok = sb("ok", [P, SC, P], FP, c)
        d16 = sb("d16", [P, SC, P], BF, c)
        mrow = sb("mrow", [P, SC, P], FP, c)
        starts16 = sb("starts16", [P, SC, P], BF, c)
        ends16 = sb("ends16", [P, SC, P], BF, c)
        gth, cal, st = tiles_gathered, sem("steps_rows"), sem("steps_stored")
        with nc.Block() as block:
            @block.gpsimd
            def _(pool):
                for k in range(SC):
                    nc.gpsimd.indirect_dma_start(
                        out=sf[:, k, :, :].rearrange("p f e -> p (f e)"), out_offset=None, in_=tiles_dram,
                        in_offset=bass.IndirectOffsetOnAxis(ap=til_i[:, k:k + 1], axis=0)).then_inc(gth, 16)
                pool.wait_ge(gth, 16 * SC)
        ch2 = sem("rows_chain")
        with nc.Block() as block:
            @block.vector
            def _(dve):
                ch = Chain(dve, ch2)
                d = sf[:, :, 0, :]
                ch.link(nc.vector.tensor_tensor(d, d, blk128[:].unsqueeze(2).to_broadcast([P, SC, P]), ALU.subtract))
                ch.link(nc.vector.tensor_scalar(ok[:], d, 0.0, None, ALU.is_ge))
                ch.link(nc.vector.scalar_tensor_tensor(out=ok[:], in0=d, scalar=float(P), in1=ok[:],
                                                       op0=ALU.is_lt, op1=ALU.mult))
                ch.link(nc.vector.scalar_tensor_tensor(out=d, in0=d, scalar=1.0, in1=ok[:], op0=ALU.add, op1=ALU.mult))
                ch.link(nc.vector.tensor_scalar(d, d, -1.0, None, ALU.add))
                nc.vector.tensor_copy(d16[:], d)
                nc.vector.tensor_scalar(mrow[:], ok[:], BIG, -BIG, ALU.mult, ALU.add)
                ch.link(nc.vector.tensor_tensor(sf[:, :, 3, :], sf[:, :, 3, :], ok[:], ALU.mult))
                nc.vector.tensor_tensor(sf[:, :, 4, :], sf[:, :, 4, :], ok[:], ALU.mult)
                ch.link(nc.vector.tensor_tensor(ok[:], ok[:], sf[:, :, 3, :], ALU.subtract))
                ch.link(nc.vector.tensor_scalar(starts16[:], sf[:, :, 3, :], -BIG, None, ALU.mult))
                nc.vector.tensor_scalar(ends16[:], sf[:, :, 4, :], -BIG, None, ALU.mult).then_inc(cal, 1)

            @block.sync
            def _(sp):
                sp.wait_ge(cal, 1)
                sp.dma_start(dloc_dram.rearrange("(c p) e -> p c e", p=P), d16[:]).then_inc(st, 16)
                sp.dma_start(starts_dram.rearrange("(c p) e -> p c e", p=P), starts16[:]).then_inc(st, 16)
                sp.dma_start(ends_dram.rearrange("(c p) e -> p c e", p=P), ends16[:]).then_inc(st, 16)
                sp.wait_ge(st, 48)

        tr, cp = sem("turned"), sem("turned_copied")
        with nc.Block() as block:
            @block.tensor
            def _(pe):
                for k in range(SC):
                    if k:
                        pe.wait_ge(cp, 2 * k)
                    for j, a in enumerate((sf[:, k, 0, :], mrow[:, k, :], sf[:, k, 1, :], sf[:, k, 2, :])):
                        nc.tensor.transpose(ps[j][:, 0:P], a, ident[:]).then_inc(tr, 1)
                    nc.tensor.transpose(ps[4][:, 0:P], ok[:, k, :], ident[:])
                    nc.tensor.transpose(ps[5][0:1, 0:P], blk[:, k:k + 1], ident[:]).then_inc(tr, 1)

            @block.vector
            def _(dve):
                for k in range(SC):
                    col = slice(k * P, (k + 1) * P)
                    dve.wait_ge(tr, 5 * k + 5)
                    nc.vector.tensor_copy(dloc[:, col], ps[0][:, 0:P])
                    nc.vector.tensor_copy(mneg[:, col], ps[1][:, 0:P])
                    nc.vector.tensor_copy(rows_src[:, col], ps[2][:, 0:P])
                    nc.vector.tensor_copy(row0[:, col], ps[3][:, 0:P])
                    nc.vector.tensor_copy(crow[:, col], ps[4][0:1, 0:P])
                    nc.vector.tensor_copy(brow[:, col], ps[5][0:1, 0:P]).then_inc(cp, 2)
        ch3 = sem("pack_chain")
        with nc.Block() as block:
            @block.vector
            def _(dve):
                ch = Chain(dve, ch3)
                nc.vector.tensor_copy(cont[:], crow[:].rearrange("o (k u) -> o u k", u=U)[:, 0])
                b = brow[:, 0:S].rearrange("o (k j u) -> o u j k", j=U // 2, u=2)[:, 0]
                ch.link(nc.vector.tensor_copy(pk[:, 0, :], b[:, 0, :]))
                for j in range(1, 4):
                    ch.link(nc.vector.scalar_tensor_tensor(out=pk[:, 0, :], in0=b[:, j, :], scalar=float(64 ** j),
                                                           in1=pk[:, 0, :], op0=ALU.mult, op1=ALU.add))
                ch.link(nc.vector.tensor_copy(packed[:], pk[:, 0, :]))

    def pair_blocks(eng, k):
        r = eng.value_load(packed[0:1, bass.ds(k, 1)], min_val=0, max_val=64 ** 4 - 1)
        why = "make_steps numbers the blocks from 0 to NB"
        b = [eng.snap((r >> (6 * j)) & 63) if j else r & 63 for j in range(4)]
        b = [nc.s_assert_within(v, 0, NB, skip_runtime_bounds_check_because=why) for v in b]
        return b


    full_iters, left = K // NBUF, K % NBUF
    slot_full = [nc.alloc_semaphore(name=f"slot_full{j}") for j in range(NBUF * U)]
    used = [0] * NBUF

    def nxt(i, u):
        return (i, u + 1) if u + 1 < NBUF else (i + 1, 0)

    def each_batch(eng, body):
        with eng.Fori(0, full_iters) as i:
            for u in range(NBUF):
                body(i, u)
        for u in range(left):
            body(full_iters, u)

    def ahead(eng, early, late):
        early(0, 0)
        with eng.Fori(0, full_iters) as i:
            for u in range(NBUF):
                early(*nxt(i, u))
                late(i, u)
        for u in range(left):
            if u + 1 < left:
                early(full_iters, u + 1)
            late(full_iters, u)

    def gather_batches(pool, rows, width, table, stage, staged, pair_done, base, order=range(U // 2)):
        def batch(i, u):
            k = i * NBUF + u
            pool.wait_ge(staged[u], i * 16 + 16)
            for q, pair in enumerate(order):
                wait_apart(pool, pair_done, k * (U // 2) + (q + 1), waits_met)
                for j in (2 * pair, 2 * pair + 1):
                    nc.gpsimd.indirect_dma_start(
                        out=rows[:, u, j, 0:width], out_offset=None, in_=table,
                        in_offset=bass.IndirectOffsetOnAxis(ap=stage[:, u, j:j + 1], axis=0),
                    ).then_inc(slot_full[u * U + j], 16)
        each_batch(pool, batch)

    def stage_indices(sp, index, stage, staged, base):
        def batch(i, u, reused=True):
            k = i * NBUF + u
            if reused:
                for j in range(U):
                    sp.wait_ge(slot_full[u * U + j], i * 16 + 16 * base[u])
            sp.dma_start(stage[:, u, :], index[:, bass.ds(k * U, U)]).then_inc(staged[u], 16)
        for u in range(NBUF):
            batch(0, u, reused=False)
        with sp.Fori(1, full_iters) as i:
            for u in range(NBUF):
                batch(i, u)
        for u in range(left):
            batch(full_iters, u)

    def aggregate(name, table, index, with_deg):
        c = ExitStack()
        width = D + 1 if with_deg else D
        rows = sb(f"rows_{name}", [P, NBUF, U, width], FP, c)
        hot = sb(f"hot_{name}", [P, NBUF, U, P], FP, c)
        stage = sb(f"stage_{name}", [P, NBUF, U], I32, c)
        hot_ready, pair_done, added = sem(f"hot_{name}"), sem(f"pair_{name}"), sem(f"added_{name}")
        staged, ones_set = [sem(f"staged_{name}{u}") for u in range(NBUF)], sem(f"ones_{name}")
        base = list(used)
        for u in range(NBUF):
            used[u] += full_iters + (u < left)
        credit = NBUF * U // 2
        with nc.Block() as block:
            @block.gpsimd
            def _(pool):
                if with_deg:
                    nc.gpsimd.memset(rows[:, :, :, D:D + 1], 1.0).then_inc(ones_set, 1)
                nc.gpsimd.memset(hot[:], 0.0).then_inc(pair_done, credit)
                gather_batches(pool, rows, D, table, stage, staged, pair_done, base)

            @block.sync
            def _(sp):
                stage_indices(sp, index, stage, staged, base)

            @block.vector
            def _(dve):
                nc.vector.memset(agg[:], 0.0).then_inc(added, U // 2)
                dve.wait_ge(pair_done, credit)

                def early(i, u):
                    k = i * NBUF + u
                    dve.wait_ge(pair_done, (k + 1) * (U // 2))
                    nc.vector.tensor_tensor(
                        hot[:, u, :, :], iota_f[:].unsqueeze(1).to_broadcast([P, U, P]),
                        dloc[:, bass.ds(k * U, U)].unsqueeze(2).to_broadcast([P, U, P]),
                        ALU.is_equal).then_inc(hot_ready, 1)

                def late(i, u):
                    k = i * NBUF + u
                    blocks = pair_blocks(dve, k)
                    for j in range(U // 2):
                        dve.wait_ge(pair_done, k * (U // 2) + (credit + j + 1))
                        dve.wait_ge(added, k * (U // 2) + (U // 2 + j))
                        acc = agg[:, bass.ds(blocks[j], 1), 0:width].rearrange("p o w -> p (o w)")
                        nc.vector.tensor_tensor(acc, acc, ps[j][:, 0:width], ALU.add).then_inc(added, 1)
                ahead(dve, early, late)

            @block.tensor
            def _(pe):
                if with_deg:
                    pe.wait_ge(ones_set, 1)
                def batch(i, u):
                    k = i * NBUF + u
                    pe.wait_ge(hot_ready, k + 1)
                    for j in range(U // 2):
                        pe.wait_ge(added, k * (U // 2) + (j + 1))
                        for s in (2 * j, 2 * j + 1):
                            pe.wait_ge(slot_full[u * U + s], i * 16 + 16 * (base[u] + 1))
                            mm = nc.tensor.matmul(ps[j][:, 0:width], hot[:, u, s, :], rows[:, u, s, :],
                                                  start=s % 2 == 0, stop=s % 2 == 1)
                        mm.then_inc(pair_done, 1)
                each_batch(pe, batch)
        c.close()

    G = 5

    def load(name, pairs):
        s = sem(f"load_{name}")
        with nc.Block() as block:
            @block.sync
            def _(sp):
                for out_, in_ in pairs:
                    sp.dma_start(out_, in_).then_inc(s, 16)
                sp.wait_ge(s, 16 * len(pairs))

    def two_ahead(eng, early, late):
        early(0, 0)
        with eng.Fori(0, NBA // 2 - 1) as i:
            early(i * 2 + 1, 1)
            late(i * 2, 0)
            early(i * 2 + 2, 0)
            late(i * 2 + 1, 1)
        early(NBA - 1, 1)
        late(NBA - 2, 0)
        late(NBA - 1, 1)

    def project(name, weights, widths, fill, fill_links, on_act, on_dve, dve_links=0, ob=None, table=None, keep=False):
        c = ExitStack()
        nb = sb(f"nb_{name}", [P, 2, D], FP, c)
        xt = sb(f"xt_{name}", [P, 2, 2, P], FP, c)
        filled, turned, xt_ready, mm_done = (sem(f"{q}_{name}") for q in ("filled", "turned", "xt", "mm"))
        taken_a, taken_d, kept, ob_free = (sem(f"{q}_{name}") for q in ("takena", "takend", "kept", "obfree"))
        fch, dch = sem(f"fillchain_{name}"), sem(f"takechain_{name}")
        stored = [sem(f"stored_{name}{u}") for u in range(2)]
        nt, la, ld = len(widths), len(on_act), len(on_dve)
        sets = 2 if nt <= 3 else 1
        pst = [ps[6], ps[7]]
        start = [sum(widths[:n]) for n in range(nt)]

        def bank(u, n):
            return ps[(u % sets) * nt + n]

        def take(eng, i, u, tiles, taken, links=0):
            if not tiles:
                return
            if ob is not None:
                eng.wait_ge(ob_free, i + 1)
            ch = Chain(eng, dch, i * links)
            for n, f in tiles.items():
                eng.wait_ge(mm_done, i * nt + (2 * nt + n + 1))
                f(ch, i, u, bank(u, n)[:, 0:widths[n]]).then_inc(taken, 1)
            assert ch.n == links

        with nc.Block() as block:
            @block.vector
            def _(dve):
                def early(i, u):
                    dve.wait_ge(turned, i + 1)
                    if keep:
                        dve.wait_ge(kept, i + 1)
                    ch = Chain(dve, fch, i * fill_links)
                    fill(ch, i, nb[:, u, :]).then_inc(filled, 1)
                    assert ch.n == fill_links
                two_ahead(dve, early, lambda i, u: take(dve, i, u, on_dve, taken_d, dve_links))

            @block.scalar
            def _(act):
                act.sem_inc(turned, 2)
                act.sem_inc(xt_ready, 2)
                act.sem_inc(mm_done, 2 * nt)
                if keep:
                    act.sem_inc(kept, 2)
                if la:
                    act.sem_inc(taken_a, sets * la)
                if ld:
                    act.sem_inc(taken_d, sets * ld)
                if ob is not None:
                    act.sem_inc(ob_free, 2)

                def early(i, u):
                    act.wait_ge(turned, i + 3)
                    act.wait_ge(mm_done, i * nt + nt)
                    nc.scalar.copy(xt[:, u, :, :].rearrange("p h e -> p (h e)"),
                                   pst[u][:, 0:2 * P]).then_inc(xt_ready, 1)
                    if keep:
                        nc.scalar.copy(cur[:, bass.ds(i, 1), :].rearrange("p o w -> p (o w)"),
                                       nb[:, u, :]).then_inc(kept, 1)
                two_ahead(act, early, lambda i, u: take(act, i, u, on_act, taken_a))

            @block.tensor
            def _(pe):
                def early(i, u):
                    pe.wait_ge(filled, i + 1)
                    pe.wait_ge(xt_ready, i + 1)
                    nc.tensor.transpose(pst[u][:, 0:P], nb[:, u, 0:P], ident[:])
                    nc.tensor.transpose(pst[u][:, P:2 * P], nb[:, u, P:D], ident[:]).then_inc(turned, 1)

                def late(i, u):
                    pe.wait_ge(xt_ready, i + 3)
                    for n in range(nt):
                        if n in on_act:
                            pe.wait_ge(taken_a, i * la + (list(on_act).index(n) + 1))
                        else:
                            pe.wait_ge(taken_d, i * ld + (list(on_dve).index(n) + 1))
                        for h in range(2):
                            mm = nc.tensor.matmul(bank(u, n)[:, 0:widths[n]], xt[:, u, h, :],
                                                  weights[:, h, start[n]:start[n] + widths[n]],
                                                  start=h == 0, stop=h == 1)
                        mm.then_inc(mm_done, 1)
                two_ahead(pe, early, late)

            @block.sync
            def _(sp):
                if ob is None:
                    return
                with sp.Fori(0, NBA // 2) as it:
                    for u in range(2):
                        i = it * 2 + u
                        if la:
                            sp.wait_ge(taken_a, i * la + (sets + 1) * la)
                        if ld:
                            sp.wait_ge(taken_d, i * ld + (sets + 1) * ld)
                        sp.dma_start(table(i), ob[:, u]).then_inc(stored[u], 16)
                        sp.wait_ge(stored[u], it * 16 + 16)
                        sp.sem_inc(ob_free, 1)
        c.close()

    def blk1(a, i):
        return a[:, bass.ds(i, 1), 0:D].rearrange("p o w -> p (o w)")

    def grp(a, g):
        return a[:, bass.ds(g * G, G), 0:D]

    def each_group(name, links, body, per=1):
        s = sem(f"groups_{name}")
        with nc.Block() as block:
            @block.vector
            def _(dve):
                with dve.Fori(0, NBA // G) as g:
                    ch = Chain(dve, s, g * links, waits_met)
                    body(ch, g)
                    assert ch.n == links, (name, ch.n)

    mv = sb("mv", [P, NBA, 2], FP)
    rstd = sb("rstd", [P, NBA], FP)

    def row_stats(name, combine, links):
        c = ExitStack()
        st6 = sb(f"st6_{name}", [P, G, 6], FP, c)
        mv5 = sb(f"mv5_{name}", [P, G, 2], FP, c)

        def body(ch, g):
            combine(ch, g)
            for j in range(G):
                ins = nc.vector.bn_stats(st6[:, j, :], blk1(cur, g * G + j))
            ch.link(ins, plain=True)
            for j in range(G):
                ins = nc.vector.bn_aggr(mv5[:, j, :], st6[:, j, :])
            ch.link(ins)
            ch.link(nc.vector.tensor_copy(mv[:, bass.ds(g * G, G), :], mv5[:]))
        each_group(name, links + 3, body)
        root, done = sem(f"root_{name}"), sem(f"rstd_{name}")
        with nc.Block() as block:
            @block.scalar
            def _(act):
                nc.scalar.activation(rstd[:], mv[:, :, 1:2].rearrange("p b o -> p (b o)"), ACT.Sqrt, bias=eps[:]).then_inc(root, 1)

            @block.vector
            def _(dve):
                dve.wait_ge(root, 1)
                nc.vector.reciprocal(rstd[:], rstd[:]).then_inc(done, 1)
        c.close()

    def normalised(ch, i, nb):
        return nc.vector.tensor_scalar(nb, blk1(cur, i), mv[:, bass.ds(i, 1), 0:1].rearrange("p o w -> p (o w)"),
                                       rstd[:, bass.ds(i, 1)], ALU.subtract, ALU.mult)

    def copied(ch, i, nb):
        return nc.vector.tensor_copy(nb, blk1(cur, i))

    def w_view(w):
        return w.rearrange("(h p) n -> p h n", p=P)

    def rows_of(t):
        return lambda i: t[bass.ds(i * P, P), :]

    def layer0():
        c = ExitStack()
        w = sb("w0", [P, 2, (R + 1) * D], FP, c)
        bias = sb("bias0", [P, D], FP, c)
        ob = sb("ob0", [P, 2, R * D], FP, c)
        zero = sem("cur_cleared")
        with nc.Block() as block:
            @block.gpsimd
            def _(pool):
                nc.gpsimd.memset(cur[:, NB - 1:NBA, :], 0.0).then_inc(zero, 1)
        load("x", [(cur[:, 0:NB - 1, :], x[0:(NB - 1) * P, :].rearrange("(b p) d -> p b d", p=P)),
                   (cur[0:LAST, NB - 1, :], x[(NB - 1) * P:N, :]),
                   (bias[:], h_bias.partition_broadcast(P)),
                   (w[:, :, R * D:], w_view(w_loop))] +
             [(w[:, :, r * D:(r + 1) * D], w_view(w_rel[r])) for r in range(R)])

        def to_ob(eng_copy, n):
            return lambda ch, i, u, b: eng_copy(ob[:, u, n * 512:(n + 1) * 512], b)

        def self_part(ch, i, u, b):
            ch.link(nc.vector.scalar_tensor_tensor(out=blk1(cur, i), in0=b, scalar=HALF, in1=blk1(cur, i),
                                                   op0=ALU.mult, op1=ALU.add))
            return nc.vector.tensor_tensor(blk1(cur, i), blk1(cur, i), bias[:], ALU.add)
        t0 = table0.rearrange("(r n) d -> n r d", r=R)
        project("l0", w, [512] * 4 + [D], copied, 0,
                {0: to_ob(nc.scalar.copy, 0), 1: to_ob(nc.scalar.copy, 1), 2: to_ob(nc.scalar.copy, 2)},
                {3: to_ob(nc.vector.tensor_copy, 3), 4: self_part}, dve_links=1,
                ob=ob, table=lambda i: t0[bass.ds(i * P, P), :, :])
        c.close()

    def degrees():
        s = sem("degrees")
        c = ExitStack()
        root = sb("deg_root", [P, NBA], FP, c)
        has = sb("deg_has", [P, NBA], FP, c)
        r = sem("deg_rooted")
        with nc.Block() as block:
            @block.vector
            def _(dve):
                ch = Chain(dve, s)
                ch.link(nc.vector.tensor_copy(deg[:], agg[:, :, D:D + 1].rearrange("p b o -> p (b o)")))
                nc.vector.tensor_scalar(has[:], deg[:], 0.0, None, ALU.is_gt)
                ch.link(nc.vector.tensor_scalar(deg[:], deg[:], 1.0, None, ALU.max))
                ch.link(nc.vector.reciprocal(rdeg[:], deg[:]))
                dve.wait_ge(r, 1)
                ch.link(nc.vector.reciprocal(dinv[:], root[:]))
                ch.link(nc.vector.tensor_tensor(dinv[:], dinv[:], has[:], ALU.mult))

            @block.scalar
            def _(act):
                act.wait_ge(s, 2)
                nc.scalar.sqrt(root[:], deg[:]).then_inc(r, 1)
        c.close()

    def layer1_table():
        c = ExitStack()
        w = sb("wl", [P, 2, D], FP, c)
        ob = sb("ob1", [P, 2, D], FP, c)
        load("wl", [(w[:], w_view(w_l))])

        def combine(ch, g):
            ch.link(nc.vector.scalar_tensor_tensor(out=grp(cur, g), in0=grp(agg, g), scalar=HALF, in1=grp(cur, g),
                                                   op0=ALU.mult, op1=ALU.add), plain=True)
        row_stats("x1", combine, 1)
        project("l1", w, [D], normalised, 0, {0: lambda ch, i, u, b: nc.scalar.copy(ob[:, u, :], b)}, {},
                ob=ob, table=rows_of(tables[0]), keep=True)
        c.close()

    def layer1_end():
        c = ExitStack()
        w = sb("wr", [P, 2, D], FP, c)
        bl = sb("bl", [P, D], FP, c)
        gam = sb("gam", [P, D], FP, c)
        bet = sb("bet", [P, D], FP, c)
        tmp = sb("tmp1", [P, 2, G, D], FP, c)
        ss = sb("ss", [P, NBA], FP, c)
        mask = sb("row_mask", [P, P], FP, c)
        mu = sb("mu", [P, D], FP, c)
        load("wr", [(w[:], w_view(w_r)), (bl[:], b_l.partition_broadcast(P)), (gam[:], gamma.partition_broadcast(P)),
                    (bet[:], beta.partition_broadcast(P))])

        def mean_part(ch, i, u, b):
            a = blk1(agg, i)
            ch.link(nc.vector.scalar_tensor_tensor(out=a, in0=a, scalar=rdeg[:, bass.ds(i, 1)], in1=b,
                                                   op0=ALU.mult, op1=ALU.add))
            return nc.vector.tensor_tensor(a, a, bl[:], ALU.add)
        project("l1r", w, [D], copied, 0, {}, {0: mean_part}, dve_links=1)

        def squares(ch, g):
            ch.link(nc.vector.tensor_tensor(tmp[:, 0], grp(agg, g), grp(agg, g), ALU.mult))
            ch.link(nc.vector.tensor_reduce(ss[:, bass.ds(g * G, G)], tmp[:, 0], op=ALU.add, axis=AX.X))
        each_group("squares", 2, squares)
        root, s, mk = sem("len_root"), sem("len_chain"), sem("mask_made")
        with nc.Block() as block:
            @block.scalar
            def _(act):
                nc.scalar.sqrt(ss[:], ss[:]).then_inc(root, 1)

            @block.gpsimd
            def _(pool):
                nc.gpsimd.affine_select(out=mask[:], in_=ones[:], compare_op=ALU.is_gt, fill=0.0, base=LAST,
                                        pattern=[[0, P]], channel_multiplier=-1).then_inc(mk, 1)

            @block.vector
            def _(dve):
                ch = Chain(dve, s)
                dve.wait_ge(root, 1)
                ch.link(nc.vector.tensor_scalar(ss[:], ss[:], L2_EPS, None, ALU.max))
                ch.link(nc.vector.reciprocal(ss[:], ss[:]))
                dve.wait_ge(mk, 1)
                ch.link(nc.vector.tensor_tensor(ss[:, NB - 1:NB], ss[:, NB - 1:NB], mask[:, 0:1], ALU.mult))
                ch.link(nc.vector.memset(ss[:, NB:NBA], 0.0))

        ngr = NBA // G
        scaled, summed, mean_s = sem("rows_scaled"), sem("mean_summed"), sem("mean_chain")
        with nc.Block() as block:
            @block.vector
            def _(dve):
                with dve.Fori(0, ngr) as g:
                    nc.vector.tensor_tensor(grp(agg, g), grp(agg, g),
                                            ss[:, bass.ds(g * G, G)].unsqueeze(2).to_broadcast([P, G, D]),
                                            ALU.mult).then_inc(scaled, 1)
                dve.wait_ge(summed, 1)
                nc.vector.tensor_scalar(mu[:], ps[0][:, 0:D], 1.0 / N, None, ALU.mult).then_inc(mean_s, 1)

            @block.tensor
            def _(pe):
                def one(i, first, last):
                    return nc.tensor.matmul(ps[0][:, 0:D], ones[:], blk1(agg, i), start=first, stop=last)
                pe.wait_ge(scaled, 1)
                for j in range(G):
                    one(j, j == 0, False)
                with pe.Fori(1, ngr - 1) as g:
                    pe.wait_ge(scaled, g + 1)
                    for j in range(G):
                        one(g * G + j, False, False)
                pe.wait_ge(scaled, ngr)
                for j in range(G):
                    mm = one((ngr - 1) * G + j, False, j == G - 1)
                mm.then_inc(summed, 1)

        cent, sq, sqd, var_s, rt, vch = (sem(q) for q in ("centred", "squared", "sq_summed", "var_summed", "var_root", "var_chain"))
        with nc.Block() as block:
            @block.vector
            def _(dve):
                with dve.Fori(0, ngr) as g:
                    nc.vector.tensor_tensor(grp(agg, g), grp(agg, g), mu[:].unsqueeze(1).to_broadcast([P, G, D]),
                                            ALU.subtract).then_inc(cent, 1)
                ch = Chain(dve, vch)
                dve.wait_ge(var_s, 1)
                ch.link(nc.vector.tensor_scalar(mu[:], ps[0][:, 0:D], 1.0 / N, None, ALU.mult))
                dve.wait_ge(rt, 1)
                ch.link(nc.vector.reciprocal(mu[:], mu[:]))
                ch.link(nc.vector.tensor_tensor(gam[:], gam[:], mu[:], ALU.mult))

            @block.scalar
            def _(act):
                act.sem_inc(sqd, 2)
                with act.Fori(0, ngr // 2) as gg:
                    for u in range(2):
                        g = gg * 2 + u
                        act.wait_ge(cent, g + 1)
                        act.wait_ge(sqd, g + 1)
                        nc.scalar.square(tmp[:, u], grp(agg, g)).then_inc(sq, 1)
                act.wait_ge(vch, 1)
                nc.scalar.activation(mu[:], mu[:], ACT.Sqrt, bias=eps[:]).then_inc(rt, 1)

            @block.tensor
            def _(pe):
                def group(g, u, first=False, final=False):
                    pe.wait_ge(sq, g + 1)
                    for j in range(G - final):
                        last = final and j == G - 2
                        mm = nc.tensor.matmul(ps[0][:, 0:D], mask[:] if last else ones[:], tmp[:, u, j, :],
                                              start=first and j == 0, stop=last)
                    mm.then_inc(sqd, 1)
                    return mm
                group(0, 0, first=True)
                group(1, 1)
                with pe.Fori(1, ngr // 2 - 1) as gg:
                    group(gg * 2, 0)
                    group(gg * 2 + 1, 1)
                group(ngr - 2, 0)
                group(ngr - 1, 1, final=True)
                pe.wait_ge(sqd, 2 + ngr)
                pe.sem_inc(var_s, 1)

        def combine(ch, g):
            t = tmp[:, 0]
            ch.link(nc.vector.tensor_tensor(t, grp(agg, g), gam[:].unsqueeze(1).to_broadcast([P, G, D]), ALU.mult))
            ch.link(nc.vector.tensor_tensor(t, t, bet[:].unsqueeze(1).to_broadcast([P, G, D]), ALU.add))
            ch.link(nc.vector.scalar_tensor_tensor(out=grp(cur, g), in0=t, scalar=0.0, in1=grp(cur, g),
                                                   op0=ALU.max, op1=ALU.add), plain=True)
        row_stats("x2", combine, 3)
        c.close()

    er_all = sb("er_all", [P, NBA, H], FP)
    er3 = sb("er3", [P, NBA, H, 3], BF)
    rden = sb("rden", [P, NBA, H], FP)

    def heads(a):
        return a.rearrange("p (h w) -> p h w", h=H)

    def gat_weights(c, n):
        w = sb(f"wg{n}", [P, 2, D + 2 * H], FP, c)
        av = sb(f"av{n}", [P, 2, D], FP, c)
        t = sb(f"avt{n}", [P, 2, D], FP, c)
        load(f"wg{n}", [(w[:, :, 0:D], w_view(gat_w[n])),
                        (av[:, 0, :], gat_al[n].rearrange("h d -> (h d)").partition_broadcast(P)),
                        (av[:, 1, :], gat_ar[n].rearrange("h d -> (h d)").partition_broadcast(P))])
        s = sem(f"wgchain{n}")
        with nc.Block() as block:
            @block.vector
            def _(dve):
                ch = Chain(dve, s)
                for q in range(2):
                    ch.link(nc.vector.tensor_tensor(t[:], w[:, :, 0:D], av[:, q:q + 1, :].to_broadcast([P, 2, D]), ALU.mult))
                    for k in range(2):
                        ch.link(nc.vector.tensor_reduce(w[:, k, D + q * H:D + (q + 1) * H], heads(t[:, k, :]),
                                                        op=ALU.add, axis=AX.X))
        return w

    def gat_table(c, n, fill, fill_links, table):
        w = gat_weights(c, n)
        ob = sb(f"obg{n}", [P, 2, W4], FP, c)

        def head_rows(ch, i, u, b):
            nc.scalar.copy(heads(ob[:, u, :])[:, :, 0:DH], heads(b[:, 0:D]))
            nc.scalar.copy(heads(ob[:, u, :])[:, :, DH:DH + 1].rearrange("p h o -> p (h o)"), b[:, D:D + H])
            return nc.scalar.copy(er_all[:, bass.ds(i, 1), :].rearrange("p o h -> p (o h)"), b[:, D + H:D + 2 * H])
        project(f"g{n}", w, [D + 2 * H], fill, fill_links, {0: head_rows}, {}, ob=ob, table=rows_of(table), keep=True)
        r = sb(f"er_rest{n}", [P, NBA, H], FP, c)
        s = sem(f"er_chain{n}")
        with nc.Block() as block:
            @block.vector
            def _(dve):
                ch = Chain(dve, s)
                part = lambda q: er3[:, :, :, q:q + 1].rearrange("p b h o -> p b (h o)")
                ch.link(nc.vector.tensor_copy(part(0), er_all[:]))
                ch.link(nc.vector.tensor_tensor(r[:], er_all[:], part(0), ALU.subtract))
                ch.link(nc.vector.tensor_copy(part(1), r[:]))
                ch.link(nc.vector.tensor_tensor(r[:], r[:], part(1), ALU.subtract))
                ch.link(nc.vector.tensor_copy(part(2), r[:]))

    def aggregate_gat(name, table):
        c = ExitStack()
        rows = sb(f"rows_{name}", [P, NBUF, U, W4], FP, c)
        hot = sb(f"hot_{name}", [P, 2, U, P], FP, c)
        hot_t = sb(f"hott_{name}", [P, 2, U * P], BF, c)
        dst_t = sb(f"dstt_{name}", [P, 2, U * P], BF, c)
        starts = sb(f"starts_{name}", [H, 2, U * P], BF, c)
        ends = sb(f"ends_{name}", [H, 2, U * P], BF, c)
        fwd = sb(f"fwd_{name}", [H, 2, U * P], FP, c)
        back = sb(f"back_{name}", [H, U * P], FP, c)
        el = sb(f"el_{name}", [P, 2, U, H], FP, c)
        er = sb(f"er_{name}", [P, U + 1, H], FP, c)
        z = sb(f"z_{name}", [P, 2, U + 1, H], FP, c)
        ex = sb(f"ex_{name}", [P, NBUF, U + 1, H], FP, c)
        am = sb(f"am_{name}", [1, H], FP, c)
        fac = sb(f"fac_{name}", [P, H], FP, c)
        stage = sb(f"stage_{name}", [P, NBUF, U], I32, c)
        names = ("pair", "added", "hot", "hott", "el", "elt", "er", "fwd", "back", "backt", "zr", "ex", "am", "fac",
                 "rescaled", "scaled", "scaledd", "erread", "zchain", "half", "weightsin", "facread")
        (pair_done, added, hot_ready, hott_ready, el_ready, elt_done, er_done, fwd_done, back_done, backt_done, z_ready,
         ex_ready, am_ready, fac_done, rescaled, scaled, scaled_d, er_read, zch, half, weights_in, fac_read) = (sem(f"{q}_{name}") for q in names)
        staged = [sem(f"staged_{name}{u}") for u in range(NBUF)]
        flags = [sem(f"flags_{name}{u}") for u in range(2)]
        base = list(used)
        for u in range(NBUF):
            used[u] += full_iters + (u < left)
        credit = NBUF * U // 2
        el_t = [ps[4], ps[5]]
        er_bank, misc = ps[6], ps[7]
        HU = U // 2
        back_t = misc[:, 0:(U + 2) * H].rearrange("p (s h) -> p s h", h=H)
        AP = 3
        order = [*range(AP, HU), *range(AP)]
        FACQ = 2
        fac_bank = ps[order[FACQ]][:, 512 - H:512]

        def three_batches(eng, first, step):
            assert left >= 2
            first(0, 0)
            step((0, 1), (0, 0), None)
            with eng.Fori(0, full_iters) as i:
                for u in range(NBUF):
                    step(nxt(*nxt(i, u)), nxt(i, u), (i, u))
            for u in range(left):
                step(*((full_iters, u + d) if u + d < left else None for d in (2, 1, 0)))

        with nc.Block() as block:
            @block.gpsimd
            def _(pool):
                nc.gpsimd.memset(hot[:], 0.0).then_inc(pair_done, credit)
                gather_batches(pool, rows, W4, table, stage, staged, pair_done, base, order)

            @block.sync
            def _(sp):
                sp.sem_inc(back_done, 2)
                sp.sem_inc(hott_ready, 2)

                def batch(i, u, reused=True):
                    k = i * NBUF + u
                    if reused:
                        for j in range(U):
                            sp.wait_ge(slot_full[u * U + j], i * 16 + 16 * base[u])
                    sp.dma_start(stage[:, u, :], rows_src[:, bass.ds(k * U, U)]).then_inc(staged[u], 16)
                    sp.wait_ge(hott_ready, k + 1)
                    sp.wait_ge(back_done, k + 1)
                    for to, of, n in ((dst_t, dloc_dram, P), (starts, starts_dram, H), (ends, ends_dram, H)):
                        sp.dma_start(to[:, u % 2, :], of[bass.ds(k * U, U), :].rearrange("s e -> (s e)")
                                     .partition_broadcast(n)).then_inc(flags[u % 2], 16)
                for u in range(NBUF):
                    batch(0, u, reused=False)
                with sp.Fori(1, full_iters) as i:
                    for u in range(NBUF):
                        batch(i, u)
                for u in range(left):
                    batch(full_iters, u)

            @block.vector
            def _(dve):
                nc.vector.memset(agg[:], 0.0).then_inc(added, credit + 1)
                dve.sem_inc(zch, credit)
                nc.vector.memset(fwd[:], -BIG).then_inc(fwd_done, 1)
                dve.wait_ge(pair_done, credit)
                dve.sem_inc(elt_done, 1)
                dve.sem_inc(er_done, 2)
                dve.sem_inc(backt_done, 2)
                dve.sem_inc(ex_ready, 1)
                dve.sem_inc(fac_done, 1)

                def logit_parts(i, u):
                    k = i * NBUF + u
                    for j in range(U):
                        dve.wait_ge(slot_full[u * U + j], i * 16 + 16 * (base[u] + 1))
                    dve.wait_ge(elt_done, k + 1)
                    nc.vector.tensor_tensor(
                        el[:, u % 2], rows[:, u, :, :].rearrange("p s (h w) -> p s h w", h=H)[:, :, :, DH:DH + 1]
                        .rearrange("p s h o -> p s (h o)"),
                        mneg[:, bass.ds(k * U, U)].unsqueeze(2).to_broadcast([P, U, H]), ALU.add).then_inc(el_ready, 1)
                    dve.wait_ge(flags[u % 2], i * (48 * NBUF // 2) + 48 * (u // 2 + 1))
                    dve.wait_ge(er_done, k + 1)
                    nc.vector.tensor_scalar(hot_t[:, u % 2, :], dst_t[:, u % 2, :], iota_p[:], None,
                                            ALU.is_equal).then_inc(hott_ready, 1)

                def one_hots(i, u):
                    k = i * NBUF + u
                    dve.wait_ge(pair_done, k * HU + (credit - HU))
                    nc.vector.tensor_tensor(
                        hot[:, u % 2, :, :], iota_f[:].unsqueeze(1).to_broadcast([P, U, P]),
                        dloc[:, bass.ds(k * U, U)].unsqueeze(2).to_broadcast([P, U, P]),
                        ALU.is_equal).then_inc(hot_ready, 1)

                def forward(i, u):
                    k, v = i * NBUF + u, u % 2
                    dve.wait_ge(elt_done, k + 2)
                    dve.wait_ge(fwd_done, k + 1)
                    dve.wait_ge(backt_done, k + 2)
                    nc.vector.tensor_tensor_scan(fwd[:, v, 0:HU * P], starts[:, v, 0:HU * P], el_t[0][0:H, 0:HU * P],
                                                 fwd[:, 1 - v, U * P - 1:U * P], ALU.add, ALU.max).then_inc(half, 1)
                    dve.wait_ge(half, k + 1)
                    nc.vector.tensor_tensor_scan(fwd[:, v, HU * P:], starts[:, v, HU * P:], el_t[1][0:H, 0:HU * P],
                                                 fwd[:, v, HU * P - 1:HU * P], ALU.add, ALU.max).then_inc(fwd_done, 1)

                def backward(i, u):
                    k, v = i * NBUF + u, u % 2
                    dve.wait_ge(fwd_done, k + 2)
                    dve.wait_ge(backt_done, k + 2)
                    nc.vector.tensor_tensor_scan(back[:, ::-1], ends[:, v, ::-1], fwd[:, v, ::-1], -BIG,
                                                 ALU.add, ALU.max).then_inc(back_done, 1)

                def logits(i, u):
                    k = i * NBUF + u
                    ch = Chain(dve, zch, k * 4 + credit)
                    dve.wait_ge(er_done, k + 3)
                    ch.link(nc.vector.tensor_reduce(er[:], er_bank[:, 0:(U + 1) * H * 3]
                                                    .rearrange("p (s h q) -> p s h q", h=H, q=3), op=ALU.add, axis=AX.X))
                    yield
                    dve.wait_ge(ex_ready, k + 1)
                    nc.vector.tensor_tensor(z[:, 0, 0:U, :], el[:, u % 2], er[:, 0:U, :], ALU.add).then_inc(er_read, 1)
                    dve.wait_ge(backt_done, k + 3)
                    nc.vector.tensor_tensor(z[:, 1, :, :], back_t[:, 0:U + 1, :], er[:], ALU.add)
                    nc.vector.tensor_tensor(z[:, 0, U, :], back_t[:, U + 1, :], er[:, U, :], ALU.add).then_inc(zch, 1)
                    ch.n += 1
                    yield
                    dve.wait_ge(zch, ch.at + 2)
                    flat = z[:].rearrange("p a s h -> p (a s h)")
                    nc.vector.scalar_tensor_tensor(out=flat, in0=flat, scalar=0.2, in1=flat, op0=ALU.mult,
                                                   op1=ALU.max).then_inc(zch, 1)
                    yield
                    dve.wait_ge(zch, ch.at + 3)
                    nc.vector.tensor_tensor(z[:, 0], z[:, 0], z[:, 1], ALU.subtract).then_inc(zch, 1)
                    yield
                    dve.wait_ge(zch, ch.at + 4)
                    nc.vector.tensor_scalar(z[:, 0], z[:, 0], 0.0, None, ALU.min).then_inc(z_ready, 1)

                def growth(i, u):
                    k = i * NBUF + u
                    dve.wait_ge(ex_ready, k + 2)
                    dve.wait_ge(fac_done, k + 1)
                    nc.vector.tensor_scalar(am[:], ex[0:1, u, U, :], -1.0, cont[:, bass.ds(k, 1)],
                                            ALU.add, ALU.mult).then_inc(am_ready, 1)

                def weigh(i, u):
                    for j in range(AP, HU):
                        a = rows[:, u, 2 * j:2 * j + 2, :].rearrange("p s (h w) -> p (s h) w", h=H)[:, :, 0:DH]
                        w = ex[:, u, 2 * j:2 * j + 2, :].rearrange("p s h -> p (s h)")
                        nc.vector.tensor_tensor(a, a, w.unsqueeze(2).to_broadcast([P, 2 * H, DH]),
                                                ALU.mult).then_inc(scaled_d, 1)

                def factors(i, u):
                    dve.wait_ge(fac_done, i * NBUF + (u + 2))
                    nc.vector.tensor_scalar(fac[:], fac_bank, 1.0, None, ALU.add).then_inc(fac_read, 1)

                def rescale(i, u, blocks):
                    k = i * NBUF + u
                    dve.wait_ge(added, k * HU + (credit + 1))
                    dve.wait_ge(fac_read, k + 2)
                    acc = agg[:, bass.ds(blocks[0], 1), :].rearrange("p o (h w) -> p (o h) w", h=H)
                    nc.vector.tensor_tensor(acc, acc, fac[:].unsqueeze(2).to_broadcast([P, H, W4 // H]),
                                            ALU.mult).then_inc(rescaled, 1)

                def accumulate(i, u, blocks, q):
                    k = i * NBUF + u
                    j = order[q]
                    if q == 0:
                        dve.wait_ge(rescaled, k + 1)
                    dve.wait_ge(pair_done, k * HU + (credit + q + 1))
                    dve.wait_ge(added, k * HU + (credit + q + 1))
                    acc = agg[:, bass.ds(blocks[j], 1), :].rearrange("p o w -> p (o w)")
                    nc.vector.tensor_tensor(acc, acc, ps[j][:, 0:W4], ALU.add).then_inc(added, 1)

                def step(after, nx, this):
                    if this:
                        growth(*this)
                        weigh(*this)
                    if nx:
                        forward(*nx)
                    if this:
                        factors(*this)
                    if nx:
                        backward(*nx)
                    if after:
                        logit_parts(*after)
                    if this:
                        blocks = pair_blocks(dve, this[0] * NBUF + this[1])
                        rescale(*this, blocks)
                    if nx:
                        one_hots(*nx)
                    links = logits(*nx) if nx else iter(())
                    for q in range(HU - 1):
                        next(links, None)
                        if this:
                            accumulate(*this, blocks, q)
                    next(links, None)
                    next(links, None)
                    if this:
                        accumulate(*this, blocks, HU - 1)
                dve.sem_inc(fac_read, 1)
                three_batches(dve, logit_parts, step)

            @block.scalar
            def _(act):
                act.sem_inc(er_read, 1)
                act.sem_inc(z_ready, 1)
                act.sem_inc(am_ready, NBUF)

                def batch(i, u):
                    k = i * NBUF + u
                    act.wait_ge(z_ready, k + 2)
                    act.wait_ge(am_ready, k + 1)
                    nc.scalar.activation(ex[:, u], z[:, 0], ACT.Exp).then_inc(ex_ready, 1)
                    act.wait_ge(ex_ready, k + 2)
                    by_head = rows[:, u, :, :].rearrange("p s (h w) -> p s h w", h=H)
                    nc.scalar.copy(by_head[:, :, :, DH:DH + 1].rearrange("p s h o -> p s (h o)"),
                                   ex[:, u, 0:U, :]).then_inc(weights_in, 1)
                    for s in range(2 * AP):
                        for h in range(H):
                            a = by_head[:, s, h, 0:DH]
                            ins = nc.scalar.mul(a, a, ex[:, u, s, h:h + 1])
                        if s % 2:
                            ins.then_inc(scaled, 1)
                each_batch(act, batch)

            @block.tensor
            def _(pe):
                def turn(i, u):
                    k = i * NBUF + u
                    pe.wait_ge(el_ready, k + 1)
                    pe.wait_ge(fwd_done, k + 1)
                    for s in range(U):
                        ins = nc.tensor.transpose(el_t[s // HU][0:H, (s % HU) * P:(s % HU + 1) * P], el[:, u % 2, s, :], ident[:])
                    ins.then_inc(elt_done, 1)

                def er_of_edges(i, u, blocks):
                    k = i * NBUF + u
                    pe.wait_ge(hott_ready, k + 3)
                    pe.wait_ge(er_read, k + 1)
                    for place, s in enumerate([*range(U), 0]):
                        ins = nc.tensor.matmul(er_bank[:, place * 3 * H:(place + 1) * 3 * H],
                                               hot_t[:, u % 2, s * P:(s + 1) * P],
                                               er3[:, bass.ds(blocks[s // 2], 1), :, :].rearrange("p o h q -> p (o h q)"),
                                               start=True, stop=True)
                    ins.then_inc(er_done, 1)

                def factor(i, u):
                    k = i * NBUF + u
                    pe.wait_ge(am_ready, k + (NBUF + 1))
                    pe.wait_ge(hot_ready, k + 1)
                    pe.wait_ge(fac_read, k + 1)
                    pe.wait_ge(added, k * HU + (credit - HU + 1 + FACQ + 1))
                    nc.tensor.matmul(fac_bank, hot[0:1, u % 2, 0, :], am[:], start=True, stop=True).then_inc(fac_done, 1)

                def turn_back(i, u):
                    k = i * NBUF + u
                    pe.wait_ge(back_done, k + 3)
                    wait_apart(pe, z_ready, k + 1, waits_met)
                    for place, s in enumerate([*range(U), 0]):
                        nc.tensor.transpose(back_t[:, place, :], back[:, s * P:(s + 1) * P], ident[0:H, 0:H])
                    prev = fwd[:, (u - 1) % 2, U * P - 1:U * P]
                    nc.tensor.matmul(back_t[:, U + 1, :], prev.to_broadcast([H, P]), ident[0:H, 0:H],
                                     start=True, stop=True).then_inc(backt_done, 1)

                def sums(i, u, places):
                    k = i * NBUF + u
                    for q in places:
                        j = order[q]
                        if j < AP:
                            pe.wait_ge(scaled, k * AP + (j + 1))
                        else:
                            pe.wait_ge(weights_in, k + 1)
                            pe.wait_ge(scaled_d, k * (HU - AP) + (j + 1 - AP))
                        pe.wait_ge(added, k * HU + (credit - HU + 2 + q))
                        if q == FACQ:
                            pe.wait_ge(fac_read, k + 2)
                        for s in (2 * j, 2 * j + 1):
                            mm = nc.tensor.matmul(ps[j][:, 0:W4], hot[:, u % 2, s, :], rows[:, u, s, :],
                                                  start=s % 2 == 0, stop=s % 2 == 1)
                        mm.then_inc(pair_done, 1)

                def first(i, u):
                    turn(i, u)
                    er_of_edges(i, u, pair_blocks(pe, i * NBUF + u))

                def step(after, nx, this):
                    if this:
                        factor(*this)
                        sums(*this, (0, 1))
                    if nx:
                        turn_back(*nx)
                    if after:
                        turn(*after)
                        blocks = pair_blocks(pe, after[0] * NBUF + after[1])
                    if this:
                        sums(*this, (2, 3))
                    if after:
                        er_of_edges(*after, blocks)
                three_batches(pe, first, step)
        c.close()

    def gat_fill(ch, i, nb):
        a = agg[:, bass.ds(i, 1), :].rearrange("p o (h w) -> p (o h) w", h=H)[:, :, 0:DH]
        ch.link(nc.vector.tensor_tensor(heads(nb), a, rden[:, bass.ds(i, 1), :].rearrange("p o h -> p (o h)")
                                        .unsqueeze(2).to_broadcast([P, H, DH]), ALU.mult))
        ch.link(nc.vector.tensor_tensor(nb, nb, blk1(cur, i), ALU.add))
        return nc.vector.tensor_scalar(nb, nb, 0.0, None, ALU.max)

    def weight_sums(n):
        s = sem(f"rden{n}")
        with nc.Block() as block:
            @block.vector
            def _(dve):
                ch = Chain(dve, s)
                den = agg[:].rearrange("p b (h w) -> p b h w", h=H)[:, :, :, DH:DH + 1].rearrange("p b h o -> p b (h o)")
                ch.link(nc.vector.tensor_scalar(rden[:], den, 1e-9, None, ALU.max))
                ch.link(nc.vector.reciprocal(rden[:], rden[:]))

    def layer2():
        for n in range(3):
            c = ExitStack()
            if n:
                weight_sums(n)
                gat_table(c, n, gat_fill, 2, tables[1 + n])
            else:
                gat_table(c, n, normalised, 0, tables[1])
                load("keep_x2", [(x2_dram.rearrange("(b p) d -> p b d", p=P), cur[:])])
            c.close()
            clear_sems()
            aggregate_gat(f"a{2 + n}", tables[1 + n])
            clear_sems()
        weight_sums(3)
        load("x2_back", [(cur[:], x2_dram.rearrange("(b p) d -> p b d", p=P))])
        c = ExitStack()
        t = sb("h3", [P, D], FP, c)
        s = sem("h3_chain")

        def combine(ch, g):
            for j in range(G):
                i = g * G + j
                a = agg[:, bass.ds(i, 1), :].rearrange("p o (h w) -> p (o h) w", h=H)[:, :, 0:DH]
                ch.link(nc.vector.tensor_tensor(heads(t[:]), a, rden[:, bass.ds(i, 1), :].rearrange("p o h -> p (o h)")
                                                .unsqueeze(2).to_broadcast([P, H, DH]), ALU.mult))
                ch.link(nc.vector.scalar_tensor_tensor(out=blk1(cur, i), in0=t[:], scalar=0.0, in1=blk1(cur, i),
                                                       op0=ALU.max, op1=ALU.add), plain=True)
        row_stats("x3", combine, 2 * G)
        c.close()
        clear_sems()

    def layer3():
        c = ExitStack()
        w = sb("w3s", [P, 2, D], FP, c)
        ob = sb("ob5", [P, 2, D], FP, c)
        load("w3", [(w[:], w_view(w3))])
        project("l3", w, [D], normalised, 0,
                {0: lambda ch, i, u, b: nc.scalar.mul(ob[:, u, :], b, dinv[:, bass.ds(i, 1)])}, {},
                ob=ob, table=rows_of(tables[4]), keep=True)
        c.close()
        clear_sems()
        aggregate("a5", tables[4], rows_src, False)
        clear_sems()

        def combine(ch, g):
            ch.link(nc.vector.tensor_tensor(grp(agg, g), grp(agg, g), dinv[:, bass.ds(g * G, G)].unsqueeze(2)
                                            .to_broadcast([P, G, D]), ALU.mult))
            ch.link(nc.vector.tensor_tensor(grp(cur, g), grp(cur, g), grp(agg, g), ALU.add), plain=True)
        row_stats("x4", combine, 2)

    def store_out():
        ready, so = sem("out_ready"), sem("out_stored")
        with nc.Block() as block:
            @block.vector
            def _(dve):
                with dve.Fori(0, NB) as i:
                    normalised(None, i, blk1(cur, i)).then_inc(ready, 1)

            @block.sync
            def _(sp):
                with sp.Fori(0, NB - 1) as i:
                    sp.wait_ge(ready, i + 1)
                    sp.dma_start(out[bass.ds(i * P, P), :], blk1(cur, i)).then_inc(so, 16)
                sp.wait_ge(ready, NB)
                sp.dma_start(out[(NB - 1) * P:N, :], cur[0:LAST, NB - 1, :]).then_inc(so, 16)
                sp.wait_ge(so, 16 * NB)

    c = ExitStack()
    make_steps(c, raw_edges(c))
    c.close()
    clear_sems()
    layer0()
    clear_sems()
    aggregate("a0", table0, row0, True)
    clear_sems()
    degrees()
    layer1_table()
    clear_sems()
    aggregate("a1", tables[0], rows_src, False)
    clear_sems()
    layer1_end()
    clear_sems()
    layer2()
    layer3()
    store_out()
    ctx.close()


def kernel(x, src, dst, edge_type_8, L0_gnn_weight, L0_gnn_h_bias, L0_gnn_loop_weight, L1_gnn_W_l, L1_gnn_b_l,
           L1_gnn_W_r, L1_gnn_gamma, L1_gnn_beta, L2_gnn_W0, L2_gnn_al0, L2_gnn_ar0, L2_gnn_W1, L2_gnn_al1,
           L2_gnn_ar1, L2_gnn_W2, L2_gnn_al2, L2_gnn_ar2, L3_gnn_W):
    import numpy as np
    import concourse.bacc as bacc
    from concourse import mybir as mb
    from concourse.bass_utils import run_bass_kernel_spmd

    nc = bacc.Bacc("TRN2", target_bir_lowering=False, num_devices=1)
    arrays = {}

    def given(name, a):
        a = np.ascontiguousarray(a)
        arrays[name] = a
        return nc.dram_tensor(name, a.shape, mb.dt.from_np(a.dtype), kind="ExternalInput").ap()

    args = [given("in_x", x), given("in_src", src), given("in_dst", dst), given("in_type", edge_type_8),
            given("in_w_rel", L0_gnn_weight), given("in_h_bias", L0_gnn_h_bias), given("in_w_loop", L0_gnn_loop_weight),
            given("in_w_l", np.asarray(L1_gnn_W_l).T), given("in_b_l", L1_gnn_b_l), given("in_w_r", np.asarray(L1_gnn_W_r).T),
            given("in_gamma", L1_gnn_gamma), given("in_beta", L1_gnn_beta),
            [given(f"in_gat_w{i}", a) for i, a in enumerate((L2_gnn_W0, L2_gnn_W1, L2_gnn_W2))],
            [given(f"in_gat_al{i}", a) for i, a in enumerate((L2_gnn_al0, L2_gnn_al1, L2_gnn_al2))],
            [given(f"in_gat_ar{i}", a) for i, a in enumerate((L2_gnn_ar0, L2_gnn_ar1, L2_gnn_ar2))],
            given("in_w3", L3_gnn_W)]
    out = nc.dram_tensor("out_0_dram", (N, D), FP, kind="ExternalOutput").ap()
    build(nc, *args, out)
    r = run_bass_kernel_spmd(nc, [arrays], core_ids=[0])
    return r.results[0]["out_0_dram"]
```

```python
import concourse.bass as bass
from concourse import mybir
from contextlib import ExitStack

FP = mybir.dt.float32
BF = mybir.dt.bfloat16
I32 = mybir.dt.int32
ALU = mybir.AluOpType
ACT = mybir.ActivationFunctionType
AX = mybir.AxisListType

P = 128
N = 6250
E = 100000
D = 256
H = 4
DH = D // H
R = 8
NB = -(-N // P)
NBA = NB + 1
NP = NBA * P
LAST = N - (NB - 1) * P
T = -(-E // P)
TAIL = E - (T - 1) * P
CH = -(-T // P)
U = 8
NBUF = 4
S = -(-(T + NB - 1 + NB) // (2 * U)) * 2 * U
K = S // U
SC = -(-(S + U) // P)
SP_ = SC * P
RT = SC * P
NODST = 7000
NF = 5
BIG = 3.0e38
W4 = D + H
LN_EPS = 1e-5
BN_EPS = 1e-5
L2_EPS = 1e-12
HALF = 0.5 ** 0.5


class Chain:

    def __init__(self, eng, sem, at=0):
        self.eng, self.sem, self.at, self.n = eng, sem, at, 0

    def done(self, ins):
        self.n += 1
        ins.then_inc(self.sem, 1)

    def met(self):
        self.eng.wait_ge(self.sem, self.at + self.n)

    def link(self, ins):
        self.done(ins)
        self.met()


def wait_apart(eng, sem, value, passed):
    eng.wait_ge(sem, value)
    eng.sem_inc(passed, 1)


def build(nc, x, src, dst, etype, w_rel, h_bias, w_loop, w_l, b_l, w_r, gamma, beta,
          gat_w, gat_al, gat_ar, w3, out):
    ctx = ExitStack()
    sems = {}

    def sb(name, shape, dt, c=None):
        return (c or ctx).enter_context(nc.sbuf_tensor(name, shape, dt))

    def sem(name):
        if name not in sems:
            sems[name] = nc.alloc_semaphore(name=name)
        return sems[name]

    tiles_gathered = nc.alloc_semaphore(name="tiles_gathered")
    waits_met = nc.alloc_semaphore(name="waits_met")

    def clear_sems():
        numbers = sorted(s.num for s in sems.values())
        with nc.Block() as block:
            @block.gpsimd
            def _(pool):
                while numbers:
                    lo = hi = numbers.pop(0)
                    while numbers and numbers[0] == hi + 1:
                        hi = numbers.pop(0)
                    pool.sem_clear(range(lo, hi + 1))
        for s in sems.values():
            nc.release_semaphore(s)
        sems.clear()

    cur = sb("cur", [P, NBA, D], FP)
    agg = sb("agg", [P, NBA, W4], FP)
    row0 = sb("row0", [P, SP_], I32)
    rows_src = sb("rows_src", [P, SP_], I32)
    dloc = sb("dloc", [P, SP_], FP)
    mneg = sb("mneg", [P, SP_], FP)
    cont = sb("cont", [1, SP_ // U], FP)
    packed = sb("packed", [1, K], I32)
    deg = sb("deg", [P, NBA], FP)
    rdeg = sb("rdeg", [P, NBA], FP)
    dinv = sb("dinv", [P, NBA], FP)
    ident = sb("ident", [P, P], FP)
    iota_f = sb("iota_f", [P, P], FP)
    iota_p = sb("iota_p", [P, 1], FP)
    ones = sb("ones", [P, P], FP)
    eps = sb("eps", [P, 1], FP)
    ps = [ctx.enter_context(nc.psum_tensor(f"ps{i}", [P, 512], FP)) for i in range(8)]

    table0 = nc.dram_tensor("table0", (R * NP, D), FP, kind="Internal").ap()
    tables = [nc.dram_tensor(f"table{i}", (NP, W4 if i in (2, 3, 4) else D), FP, kind="Internal").ap()
              for i in range(1, 6)]
    tiles_dram = nc.dram_tensor("tiles_dram", (RT, NF * P), FP, kind="Internal").ap()
    dloc_dram = nc.dram_tensor("dloc_dram", (SP_, P), BF, kind="Internal").ap()
    starts_dram = nc.dram_tensor("starts_dram", (SP_, P), BF, kind="Internal").ap()
    ends_dram = nc.dram_tensor("ends_dram", (SP_, P), BF, kind="Internal").ap()
    x2_dram = nc.dram_tensor("x2_dram", (NBA * P, D), FP, kind="Internal").ap()

    def raw_edges(c):
        dst_i = sb("dst_i", [P, SC, P], I32, c)
        prev_i = sb("prev_i", [P, SC, P], I32, c)
        next_i = sb("next_i", [P, SC, P], I32, c)
        src_i = sb("src_i", [P, SC, P], I32, c)
        typ_i = sb("typ_i", [P, SC, P], I32, c)
        f = sb("fields", [P, SC, NF, P], FP, c)
        m, ld, st, ch_sem = sem("raw_memset"), sem("raw_loaded"), sem("raw_stored"), sem("raw_chain")
        full = CH - 1
        rest = T - 1 - full * P
        e0 = full * P * P

        with nc.Block() as block:
            @block.gpsimd
            def _(pool):
                nc.gpsimd.memset(dst_i[:, full, :], NODST)
                nc.gpsimd.memset(prev_i[:, full, :], NODST)
                nc.gpsimd.memset(prev_i[0:1, 0, 0:1], -1)
                nc.gpsimd.memset(next_i[:, full, :], NODST)
                nc.gpsimd.memset(src_i[:, full, :], 0)
                nc.gpsimd.memset(typ_i[:, full, :], 0)
                nc.gpsimd.memset(ident[:], 0.0)
                nc.gpsimd.memset(ones[:], 1.0)
                nc.gpsimd.memset(eps[:], LN_EPS).then_inc(m, 1)
                pool.wait_ge(m, 1)
                nc.gpsimd.affine_select(out=ident[:], in_=ident[:], compare_op=ALU.not_equal, fill=1.0,
                                        base=0, pattern=[[-1, P]], channel_multiplier=1)
                nc.gpsimd.iota(iota_f[:], [[1, P]], base=0, channel_multiplier=0,
                               allow_small_or_imprecise_dtypes=True)
                nc.gpsimd.iota(iota_p[:], [[0, 1]], base=0, channel_multiplier=1,
                               allow_small_or_imprecise_dtypes=True)

            @block.sync
            def _(sp):
                sp.wait_ge(m, 1)
                n = 0
                for tile, a in ((dst_i, dst), (src_i, src), (typ_i, etype)):
                    sp.dma_start(tile[:, 0:full, :], a[0:e0].rearrange("(c p e) -> p c e", p=P, e=P)).then_inc(ld, 16)
                    sp.dma_start(tile[0:rest, full, :], a[e0:e0 + rest * P].rearrange("(p e) -> p e", e=P)).then_inc(ld, 16)
                    sp.dma_start(tile[rest:rest + 1, full, 0:TAIL],
                                 a[E - TAIL:E].rearrange("(p e) -> p e", p=1)).then_inc(ld, 16)
                    n += 48
                sp.dma_start(prev_i[:, 1:full, :], dst[P * P - 1:e0 - 1].rearrange("(c p e) -> p c e", p=P, e=P)).then_inc(ld, 16)
                sp.dma_start(prev_i[1:P, 0, :], dst[P - 1:P * P - 1].rearrange("(p e) -> p e", e=P)).then_inc(ld, 16)
                sp.dma_start(prev_i[0:1, 0, 1:P], dst[0:P - 1].rearrange("(p e) -> p e", p=1)).then_inc(ld, 16)
                sp.dma_start(prev_i[0:rest, full, :], dst[e0 - 1:e0 - 1 + rest * P].rearrange("(p e) -> p e", e=P)).then_inc(ld, 16)
                sp.dma_start(prev_i[rest:rest + 1, full, 0:TAIL],
                             dst[E - TAIL - 1:E - 1].rearrange("(p e) -> p e", p=1)).then_inc(ld, 16)
                sp.dma_start(next_i[:, 0:full, :], dst[1:e0 + 1].rearrange("(c p e) -> p c e", p=P, e=P)).then_inc(ld, 16)
                sp.dma_start(next_i[0:rest, full, :], dst[e0 + 1:e0 + 1 + rest * P].rearrange("(p e) -> p e", e=P)).then_inc(ld, 16)
                sp.dma_start(next_i[rest:rest + 1, full, 0:TAIL - 1],
                             dst[E - TAIL + 1:E].rearrange("(p e) -> p e", p=1)).then_inc(ld, 16)
                n += 16 * 8
                sp.wait_ge(ld, n)

        assert SC == CH
        with nc.Block() as block:
            @block.vector
            def _(dve):
                ch = Chain(dve, ch_sem)
                nc.vector.tensor_copy(f[:, :, 0, :], dst_i[:])
                nc.vector.tensor_copy(f[:, :, 1, :], src_i[:])
                ch.link(nc.vector.tensor_copy(f[:, :, 2, :], typ_i[:]))
                ch.link(nc.vector.scalar_tensor_tensor(out=f[:, :, 2, :], in0=f[:, :, 2, :], scalar=float(NP),
                                                       in1=f[:, :, 1, :], op0=ALU.mult, op1=ALU.add))
                nc.vector.tensor_tensor(f[:, :, 3, :], dst_i[:], prev_i[:], ALU.not_equal)
                ch.link(nc.vector.tensor_tensor(f[:, :, 4, :], dst_i[:], next_i[:], ALU.not_equal))

        with nc.Block() as block:
            @block.sync
            def _(sp):
                sp.dma_start(tiles_dram.rearrange("(c p) w -> p c w", p=P),
                             f[:].rearrange("p c f e -> p c (f e)")).then_inc(st, 16)
                sp.wait_ge(st, 16)
        return f

    def make_steps(c, f):
        thr = sb("thr", [P, NB], FP, c)
        cmp_lo = sb("cmp_lo", [P, NB, CH], FP, c)
        cmp_hi = sb("cmp_hi", [P, NB, CH], FP, c)
        cnt = sb("cnt", [P, 2 * NB], FP, c)
        first = sb("first", [P, NB], FP, c)
        num = sb("num", [P, NB], FP, c)
        odd_i = sb("odd_i", [P, NB], I32, c)
        odd = sb("odd", [P, NB], FP, c)
        zero = sb("zero", [P, NB], FP, c)
        cum = sb("cum", [P, NB], FP, c)
        cum0 = sb("cum0", [P, NB], FP, c)
        shift = sb("shift", [P, NB], FP, c)
        step = sb("step", [P, SC], FP, c)
        ind = sb("ind", [P, SC, NB], FP, c)
        ind0 = sb("ind0", [P, SC, NB], FP, c)
        blk = sb("blk", [P, SC], FP, c)
        til = sb("til", [P, SC], FP, c)
        til_i = sb("til_i", [P, SC], I32, c)
        blk128 = sb("blk128", [P, SC], FP, c)
        brow = sb("brow", [1, SP_], FP, c)
        crow = sb("crow", [1, SP_], FP, c)
        pk = sb("pk", [1, 4, K], FP, c)
        a_s, b_s, g_s, t_s = sem("steps_thr"), sem("steps_cmp"), sem("steps_sum"), sem("steps_tiles")
        ch_sem = sem("steps_chain")

        with nc.Block() as block:
            @block.gpsimd
            def _(pool):
                nc.gpsimd.iota(thr[:], [[P, NB]], base=0, channel_multiplier=0,
                               allow_small_or_imprecise_dtypes=True)
                nc.gpsimd.iota(step[:], [[P, SC]], base=0, channel_multiplier=1,
                               allow_small_or_imprecise_dtypes=True)
                nc.gpsimd.memset(zero[:], 0.0).then_inc(a_s, 1)

            @block.vector
            def _(dve):
                ch = Chain(dve, ch_sem)
                dve.wait_ge(a_s, 1)
                nc.vector.tensor_tensor(cmp_hi[:], f[:, 0:CH, 0, P - 1:P].rearrange("p c o -> p o c").to_broadcast([P, NB, CH]),
                                        thr[:].unsqueeze(2).to_broadcast([P, NB, CH]), ALU.is_lt)
                ch.link(nc.vector.tensor_scalar(num[:], thr[:], float(P), None, ALU.add))
                ch.link(nc.vector.tensor_tensor(cmp_lo[:], f[:, 0:CH, 0, 0:1].rearrange("p c o -> p o c").to_broadcast([P, NB, CH]),
                                                num[:].unsqueeze(2).to_broadcast([P, NB, CH]), ALU.is_lt))
                nc.vector.tensor_reduce(cnt[:, 0:NB], cmp_hi[:], op=ALU.add, axis=AX.X)
                ch.link(nc.vector.tensor_reduce(cnt[:, NB:2 * NB], cmp_lo[:], op=ALU.add, axis=AX.X))
                nc.vector.tensor_copy(first[:], zero[:]).then_inc(b_s, 1)
                dve.wait_ge(g_s, 1)
                ch.link(nc.vector.tensor_copy(cnt[:], ps[0][:, 0:2 * NB]))
                ch.link(nc.vector.tensor_copy(first[:], cnt[:, 0:NB]))
                ch.link(nc.vector.tensor_tensor(num[:], cnt[:, NB:2 * NB], first[:], ALU.subtract))
                ch.link(nc.vector.tensor_scalar(num[:], num[:], 1.0, None, ALU.max))
                ch.link(nc.vector.tensor_copy(odd_i[:], num[:]))
                ch.link(nc.vector.tensor_scalar(odd_i[:], odd_i[:], 1, None, ALU.bitwise_and))
                ch.link(nc.vector.tensor_copy(odd[:], odd_i[:]))
                ch.link(nc.vector.tensor_tensor(num[:], num[:], odd[:], ALU.add))
                ch.link(nc.vector.tensor_tensor_scan(cum[:], num[:], zero[:], 0.0, ALU.add, ALU.add))
                ch.link(nc.vector.tensor_tensor(cum0[:], cum[:], num[:], ALU.subtract))
                ch.link(nc.vector.tensor_tensor(shift[:], first[:], cum0[:], ALU.subtract))
                nc.vector.tensor_tensor(ind[:], cum[:].unsqueeze(1).to_broadcast([P, SC, NB]),
                                        step[:].unsqueeze(2).to_broadcast([P, SC, NB]), ALU.is_le)
                ch.link(nc.vector.tensor_tensor(ind0[:], cum0[:].unsqueeze(1).to_broadcast([P, SC, NB]),
                                                step[:].unsqueeze(2).to_broadcast([P, SC, NB]), ALU.is_le))
                nc.vector.tensor_reduce(blk[:], ind[:], op=ALU.add, axis=AX.X)
                ch.link(nc.vector.tensor_tensor(ind0[:], ind0[:], ind[:], ALU.subtract))
                ch.link(nc.vector.tensor_tensor(ind0[:], ind0[:], shift[:].unsqueeze(1).to_broadcast([P, SC, NB]), ALU.mult))
                ch.link(nc.vector.tensor_reduce(til[:], ind0[:], op=ALU.add, axis=AX.X))
                ch.link(nc.vector.tensor_tensor(til[:], til[:], step[:], ALU.add))
                nc.vector.tensor_scalar(blk128[:], blk[:], float(P), None, ALU.mult)
                nc.vector.tensor_copy(til_i[:], til[:]).then_inc(t_s, 1)

            @block.tensor
            def _(pe):
                pe.wait_ge(b_s, 1)
                nc.tensor.matmul(ps[0][:, 0:2 * NB], ones[:], cnt[:], start=True, stop=True).then_inc(g_s, 1)

        sf = f
        ok = sb("ok", [P, SC, P], FP, c)
        d16 = sb("d16", [P, SC, P], BF, c)
        mrow = sb("mrow", [P, SC, P], FP, c)
        starts16 = sb("starts16", [P, SC, P], BF, c)
        ends16 = sb("ends16", [P, SC, P], BF, c)
        gth, cal, st = tiles_gathered, sem("steps_rows"), sem("steps_stored")
        with nc.Block() as block:
            @block.gpsimd
            def _(pool):
                for k in range(SC):
                    nc.gpsimd.indirect_dma_start(
                        out=sf[:, k, :, :].rearrange("p f e -> p (f e)"), out_offset=None, in_=tiles_dram,
                        in_offset=bass.IndirectOffsetOnAxis(ap=til_i[:, k:k + 1], axis=0)).then_inc(gth, 16)
                pool.wait_ge(gth, 16 * SC)
        ch2 = sem("rows_chain")
        with nc.Block() as block:
            @block.vector
            def _(dve):
                ch = Chain(dve, ch2)
                d = sf[:, :, 0, :]
                ch.link(nc.vector.tensor_tensor(d, d, blk128[:].unsqueeze(2).to_broadcast([P, SC, P]), ALU.subtract))
                ch.link(nc.vector.tensor_scalar(ok[:], d, 0.0, None, ALU.is_ge))
                ch.link(nc.vector.scalar_tensor_tensor(out=ok[:], in0=d, scalar=float(P), in1=ok[:],
                                                       op0=ALU.is_lt, op1=ALU.mult))
                ch.link(nc.vector.scalar_tensor_tensor(out=d, in0=d, scalar=1.0, in1=ok[:], op0=ALU.add, op1=ALU.mult))
                ch.link(nc.vector.tensor_scalar(d, d, -1.0, None, ALU.add))
                nc.vector.tensor_copy(d16[:], d)
                nc.vector.tensor_scalar(mrow[:], ok[:], BIG, -BIG, ALU.mult, ALU.add)
                ch.link(nc.vector.tensor_tensor(sf[:, :, 3, :], sf[:, :, 3, :], ok[:], ALU.mult))
                nc.vector.tensor_tensor(sf[:, :, 4, :], sf[:, :, 4, :], ok[:], ALU.mult)
                ch.link(nc.vector.tensor_tensor(ok[:], ok[:], sf[:, :, 3, :], ALU.subtract))
                ch.link(nc.vector.tensor_scalar(starts16[:], sf[:, :, 3, :], -BIG, None, ALU.mult))
                nc.vector.tensor_scalar(ends16[:], sf[:, :, 4, :], -BIG, None, ALU.mult).then_inc(cal, 1)

            @block.sync
            def _(sp):
                sp.wait_ge(cal, 1)
                sp.dma_start(dloc_dram.rearrange("(c p) e -> p c e", p=P), d16[:]).then_inc(st, 16)
                sp.dma_start(starts_dram.rearrange("(c p) e -> p c e", p=P), starts16[:]).then_inc(st, 16)
                sp.dma_start(ends_dram.rearrange("(c p) e -> p c e", p=P), ends16[:]).then_inc(st, 16)
                sp.wait_ge(st, 48)

        tr, cp = sem("turned"), sem("turned_copied")
        with nc.Block() as block:
            @block.tensor
            def _(pe):
                for k in range(SC):
                    if k:
                        pe.wait_ge(cp, 2 * k)
                    for j, a in enumerate((sf[:, k, 0, :], mrow[:, k, :], sf[:, k, 1, :], sf[:, k, 2, :])):
                        nc.tensor.transpose(ps[j][:, 0:P], a, ident[:]).then_inc(tr, 1)
                    nc.tensor.transpose(ps[4][:, 0:P], ok[:, k, :], ident[:])
                    nc.tensor.transpose(ps[5][0:1, 0:P], blk[:, k:k + 1], ident[:]).then_inc(tr, 1)

            @block.vector
            def _(dve):
                for k in range(SC):
                    col = slice(k * P, (k + 1) * P)
                    dve.wait_ge(tr, 5 * k + 5)
                    nc.vector.tensor_copy(dloc[:, col], ps[0][:, 0:P])
                    nc.vector.tensor_copy(mneg[:, col], ps[1][:, 0:P])
                    nc.vector.tensor_copy(rows_src[:, col], ps[2][:, 0:P])
                    nc.vector.tensor_copy(row0[:, col], ps[3][:, 0:P])
                    nc.vector.tensor_copy(crow[:, col], ps[4][0:1, 0:P])
                    nc.vector.tensor_copy(brow[:, col], ps[5][0:1, 0:P]).then_inc(cp, 2)
        ch3 = sem("pack_chain")
        with nc.Block() as block:
            @block.vector
            def _(dve):
                ch = Chain(dve, ch3)
                nc.vector.tensor_copy(cont[:], crow[:].rearrange("o (k u) -> o u k", u=U)[:, 0])
                b = brow[:, 0:S].rearrange("o (k j u) -> o u j k", j=U // 2, u=2)[:, 0]
                ch.link(nc.vector.tensor_copy(pk[:, 0, :], b[:, 0, :]))
                for j in range(1, 4):
                    ch.link(nc.vector.scalar_tensor_tensor(out=pk[:, 0, :], in0=b[:, j, :], scalar=float(64 ** j),
                                                           in1=pk[:, 0, :], op0=ALU.mult, op1=ALU.add))
                ch.link(nc.vector.tensor_copy(packed[:], pk[:, 0, :]))

    def pair_blocks(eng, k):
        r = eng.value_load(packed[0:1, bass.ds(k, 1)], min_val=0, max_val=64 ** 4 - 1)
        why = "make_steps numbers the blocks from 0 to NB"
        b = [(r >> (6 * j)) & 63 if j else r & 63 for j in range(4)]
        b = [nc.s_assert_within(v, 0, NB, skip_runtime_bounds_check_because=why) for v in b]
        return b

    full_iters, left = K // NBUF, K % NBUF
    slot_full = [nc.alloc_semaphore(name=f"slot_full{j}") for j in range(NBUF * U)]
    used = [0] * NBUF

    def nxt(i, u):
        return (i, u + 1) if u + 1 < NBUF else (i + 1, 0)

    def each_batch(eng, body):
        with eng.Fori(0, full_iters) as i:
            for u in range(NBUF):
                body(i, u)
        for u in range(left):
            body(full_iters, u)

    def ahead(eng, early, late):
        early(0, 0)
        with eng.Fori(0, full_iters) as i:
            for u in range(NBUF):
                early(*nxt(i, u))
                late(i, u)
        for u in range(left):
            if u + 1 < left:
                early(full_iters, u + 1)
            late(full_iters, u)

    def gather_batches(pool, rows, width, table, stage, staged, pair_done, order=range(U // 2)):
        def batch(i, u):
            k = i * NBUF + u
            pool.wait_ge(staged[u], i * 16 + 16)
            for q, pair in enumerate(order):
                wait_apart(pool, pair_done, k * (U // 2) + (q + 1), waits_met)
                for j in (2 * pair, 2 * pair + 1):
                    nc.gpsimd.indirect_dma_start(
                        out=rows[:, u, j, 0:width], out_offset=None, in_=table,
                        in_offset=bass.IndirectOffsetOnAxis(ap=stage[:, u, j:j + 1], axis=0),
                    ).then_inc(slot_full[u * U + j], 16)
        each_batch(pool, batch)

    def stage_indices(sp, index, stage, staged, base):
        def batch(i, u, reused=True):
            k = i * NBUF + u
            if reused:
                for j in range(U):
                    sp.wait_ge(slot_full[u * U + j], i * 16 + 16 * base[u])
            sp.dma_start(stage[:, u, :], index[:, bass.ds(k * U, U)]).then_inc(staged[u], 16)
        for u in range(NBUF):
            batch(0, u, reused=False)
        with sp.Fori(1, full_iters) as i:
            for u in range(NBUF):
                batch(i, u)
        for u in range(left):
            batch(full_iters, u)

    def aggregate(name, table, index, with_deg):
        c = ExitStack()
        width = D + 1 if with_deg else D
        rows = sb(f"rows_{name}", [P, NBUF, U, width], FP, c)
        hot = sb(f"hot_{name}", [P, NBUF, U, P], FP, c)
        stage = sb(f"stage_{name}", [P, NBUF, U], I32, c)
        hot_ready, pair_done, added = sem(f"hot_{name}"), sem(f"pair_{name}"), sem(f"added_{name}")
        staged, ones_set = [sem(f"staged_{name}{u}") for u in range(NBUF)], sem(f"ones_{name}")
        base = list(used)
        for u in range(NBUF):
            used[u] += full_iters + (u < left)
        credit = NBUF * U // 2
        with nc.Block() as block:
            @block.gpsimd
            def _(pool):
                if with_deg:
                    nc.gpsimd.memset(rows[:, :, :, D:D + 1], 1.0).then_inc(ones_set, 1)
                nc.gpsimd.memset(hot[:], 0.0).then_inc(pair_done, credit)
                gather_batches(pool, rows, D, table, stage, staged, pair_done)

            @block.sync
            def _(sp):
                stage_indices(sp, index, stage, staged, base)

            @block.vector
            def _(dve):
                nc.vector.memset(agg[:], 0.0).then_inc(added, U // 2)
                dve.wait_ge(pair_done, credit)

                def early(i, u):
                    k = i * NBUF + u
                    dve.wait_ge(pair_done, (k + 1) * (U // 2))
                    nc.vector.tensor_tensor(
                        hot[:, u, :, :], iota_f[:].unsqueeze(1).to_broadcast([P, U, P]),
                        dloc[:, bass.ds(k * U, U)].unsqueeze(2).to_broadcast([P, U, P]),
                        ALU.is_equal).then_inc(hot_ready, 1)

                def late(i, u):
                    k = i * NBUF + u
                    blocks = pair_blocks(dve, k)
                    for j in range(U // 2):
                        dve.wait_ge(pair_done, k * (U // 2) + (credit + j + 1))
                        dve.wait_ge(added, k * (U // 2) + (U // 2 + j))
                        acc = agg[:, bass.ds(blocks[j], 1), 0:width].rearrange("p o w -> p (o w)")
                        nc.vector.tensor_tensor(acc, acc, ps[j][:, 0:width], ALU.add).then_inc(added, 1)
                ahead(dve, early, late)

            @block.tensor
            def _(pe):
                if with_deg:
                    pe.wait_ge(ones_set, 1)
                def batch(i, u):
                    k = i * NBUF + u
                    pe.wait_ge(hot_ready, k + 1)
                    for j in range(U // 2):
                        pe.wait_ge(added, k * (U // 2) + (j + 1))
                        for s in (2 * j, 2 * j + 1):
                            pe.wait_ge(slot_full[u * U + s], i * 16 + 16 * (base[u] + 1))
                            mm = nc.tensor.matmul(ps[j][:, 0:width], hot[:, u, s, :], rows[:, u, s, :],
                                                  start=s % 2 == 0, stop=s % 2 == 1)
                        mm.then_inc(pair_done, 1)
                each_batch(pe, batch)
        c.close()

    G = 5

    def load(name, pairs):
        s = sem(f"load_{name}")
        with nc.Block() as block:
            @block.sync
            def _(sp):
                for out_, in_ in pairs:
                    sp.dma_start(out_, in_).then_inc(s, 16)
                sp.wait_ge(s, 16 * len(pairs))

    B = 4

    def side_by_side(eng, early, late, ahead=2):
        whole = (NBA - ahead) // B
        for i in range(ahead):
            early(i, i % B)
        with eng.Fori(0, whole) as it:
            for u in range(B):
                early(it * B + (u + ahead), (u + ahead) % B)
                late(it * B + u, u)
        for i in range(whole * B, NBA):
            if i + ahead < NBA:
                early(i + ahead, (i + ahead) % B)
            late(i, i % B)

    def project(name, weights, widths, fill, fill_links, on_act, on_dve, dve_links=0, ob=None, table=None, keep=False,
                act_copy=None, act_after=None):
        c = ExitStack()
        act_copy = act_copy or nc.scalar.copy
        nb = sb(f"nb_{name}", [P, B, D], FP, c)
        xt = sb(f"xt_{name}", [P, B, 2, P], FP, c)
        filled, turned, xt_ready, mm_done = (sem(f"{q}_{name}") for q in ("filled", "turned", "xt", "mm"))
        taken_a, taken_d, kept, ob_free = (sem(f"{q}_{name}") for q in ("takena", "takend", "kept", "obfree"))
        fch, dch = sem(f"fillchain_{name}"), sem(f"takechain_{name}")
        after_done = sem(f"after_{name}")
        stored = [sem(f"stored_{name}{u}") for u in range(B)]
        nt, la, ld = len(widths), len(on_act), len(on_dve)
        sets = B if nt == 1 else 1
        pst = ps[nt * sets:][:B]
        if len(pst) < B:
            pst = pst[:2]
        start = [sum(widths[:n]) for n in range(nt)]

        def bank(u, n):
            return ps[(u % sets) * nt + n]

        def take(eng, i, u, tiles, taken, links=0):
            if not tiles:
                return
            if ob is not None:
                eng.wait_ge(ob_free, i + 1)
            ch = Chain(eng, dch, i * links)
            for n, f in tiles.items():
                eng.wait_ge(mm_done, i * nt + (B * nt + n + 1))
                f(ch, i, u, bank(u, n)[:, 0:widths[n]]).then_inc(taken, 1)
            assert ch.n == links

        with nc.Block() as block:
            @block.vector
            def _(dve):
                def early(i, u):
                    dve.wait_ge(turned, i + 1)
                    if keep:
                        dve.wait_ge(kept, i + 1)
                    ch = Chain(dve, fch, i * fill_links)
                    fill(ch, i, nb[:, u, :]).then_inc(filled, 1)
                    assert ch.n == fill_links
                side_by_side(dve, early, lambda i, u: take(dve, i, u, on_dve, taken_d, dve_links), ahead=3)

            @block.scalar
            def _(act):
                act.sem_inc(turned, B)
                act.sem_inc(xt_ready, B)
                act.sem_inc(mm_done, B * nt)
                if keep:
                    act.sem_inc(kept, B)
                if la:
                    act.sem_inc(taken_a, sets * la)
                if ld:
                    act.sem_inc(taken_d, sets * ld)
                if ob is not None:
                    act.sem_inc(ob_free, B)
                if act_after:
                    act.sem_inc(after_done, B)

                def early(i, u):
                    act.wait_ge(turned, i + (B + 1))
                    act.wait_ge(mm_done, i * nt + nt)
                    act_copy(xt[:, u, :, :].rearrange("p h e -> p (h e)"),
                             pst[u % len(pst)][:, 0:2 * P]).then_inc(xt_ready, 1)
                    if keep:
                        act_copy(cur[:, bass.ds(i, 1), :].rearrange("p o w -> p (o w)"),
                                 nb[:, u, :]).then_inc(kept, 1)

                def late(i, u):
                    take(act, i, u, on_act, taken_a)
                    if act_after:
                        act.wait_ge(taken_d, i * ld + (sets + 1) * ld)
                        act.wait_ge(after_done, i + 1)
                        act_after(i, u).then_inc(after_done, 1)
                side_by_side(act, early, late)

            @block.tensor
            def _(pe):
                def early(i, u):
                    to = pst[u % len(pst)]
                    pe.wait_ge(filled, i + 1)
                    pe.wait_ge(xt_ready, i + (B + 1 - len(pst)))
                    nc.tensor.transpose(to[:, 0:P], nb[:, u, 0:P], ident[:])
                    nc.tensor.transpose(to[:, P:2 * P], nb[:, u, P:D], ident[:]).then_inc(turned, 1)

                def late(i, u):
                    pe.wait_ge(xt_ready, i + (B + 1))
                    for n in range(nt):
                        if n in on_act:
                            pe.wait_ge(taken_a, i * la + (list(on_act).index(n) + 1))
                        else:
                            pe.wait_ge(taken_d, i * ld + (list(on_dve).index(n) + 1))
                        for h in range(2):
                            mm = nc.tensor.matmul(bank(u, n)[:, 0:widths[n]], xt[:, u, h, :],
                                                  weights[:, h, start[n]:start[n] + widths[n]],
                                                  start=h == 0, stop=h == 1)
                        mm.then_inc(mm_done, 1)
                side_by_side(pe, early, late)

            @block.sync
            def _(sp):
                if ob is None:
                    return

                def store(it, u):
                    i = it * B + u
                    if la:
                        sp.wait_ge(taken_a, i * la + (sets + 1) * la)
                    if ld:
                        sp.wait_ge(taken_d, i * ld + (sets + 1) * ld)
                    sp.dma_start(table(i), ob[:, u]).then_inc(stored[u], 16)

                def done(it, u):
                    sp.wait_ge(stored[u], it * 16 + 16)
                    sp.sem_inc(ob_free, 1)
                for u in range(B):
                    store(0, u)
                    if u >= 2:
                        done(0, u - 2)
                with sp.Fori(1, NBA // B) as it:
                    for u in range(B):
                        store(it, u)
                        if u >= 2:
                            done(it, u - 2)
                        else:
                            done(it - 1, u + 2)
                for u in range(NBA % B):
                    store(NBA // B, u)
                for u in range(B):
                    sp.wait_ge(stored[u], 16 * (NBA // B + (u < NBA % B)))
        c.close()

    def blk1(a, i):
        return a[:, bass.ds(i, 1), 0:D].rearrange("p o w -> p (o w)")

    def grp(a, g):
        return a[:, bass.ds(g * G, G), 0:D]

    mv = sb("mv", [P, NBA, 2], FP)
    rstd = sb("rstd", [P, NBA], FP)

    def row_stats(name, combine, links):
        c = ExitStack()
        st6 = sb(f"st6_{name}", [P, G, 6], FP, c)
        mv5 = sb(f"mv5_{name}", [P, G, 2], FP, c)

        combined, counted = sem(f"combined_{name}"), sem(f"counted_{name}")

        def parts(dve, g):
            ch = Chain(dve, combined, g * links)
            yield from combine(ch, g)
            assert ch.n == links
            yield

        def step(dve, after, g):
            later = parts(dve, after) if after is not None else iter(())
            wait_apart(dve, combined, g * links + links, waits_met)
            next(later, None)
            for j in range(G):
                ins = nc.vector.bn_stats(st6[:, j, :], blk1(cur, g * G + j))
            ins.then_inc(counted, 1)
            next(later, None)
            wait_apart(dve, counted, g * 3 + 1, waits_met)
            for j in range(G):
                ins = nc.vector.bn_aggr(mv5[:, j, :], st6[:, j, :])
            ins.then_inc(counted, 1)
            next(later, None)
            dve.wait_ge(counted, g * 3 + 2)
            nc.vector.tensor_copy(mv[:, bass.ds(g * G, G), :], mv5[:]).then_inc(counted, 1)
            for _ in later:
                pass
        with nc.Block() as block:
            @block.vector
            def _(dve):
                for _ in parts(dve, 0):
                    pass
                with dve.Fori(0, NBA // G - 1) as g:
                    step(dve, g + 1, g)
                step(dve, None, NBA // G - 1)
        root, done = sem(f"root_{name}"), sem(f"rstd_{name}")
        with nc.Block() as block:
            @block.scalar
            def _(act):
                nc.scalar.activation(rstd[:], mv[:, :, 1:2].rearrange("p b o -> p (b o)"), ACT.Sqrt, bias=eps[:]).then_inc(root, 1)

            @block.vector
            def _(dve):
                dve.wait_ge(root, 1)
                nc.vector.reciprocal(rstd[:], rstd[:]).then_inc(done, 1)
        c.close()

    def normalised(ch, i, nb):
        return nc.vector.tensor_scalar(nb, blk1(cur, i), mv[:, bass.ds(i, 1), 0:1].rearrange("p o w -> p (o w)"),
                                       rstd[:, bass.ds(i, 1)], ALU.subtract, ALU.mult)

    def copied(ch, i, nb):
        return nc.vector.tensor_copy(nb, blk1(cur, i))

    def w_view(w):
        return w.rearrange("(h p) n -> p h n", p=P)

    def rows_of(t):
        return lambda i: t[bass.ds(i * P, P), :]

    def layer0():
        ob = sb("ob0", [P, B, R * D], FP, c0)
        with nc.Block() as block:
            @block.sync
            def _(sp):
                sp.wait_ge(x_loaded, 16 * (4 + R))

        def to_ob(eng_copy, n):
            return lambda ch, i, u, b: eng_copy(ob[:, u, n * 512:(n + 1) * 512], b)

        def self_part(ch, i, u, b):
            ch.link(nc.vector.scalar_tensor_tensor(out=blk1(cur, i), in0=b, scalar=HALF, in1=blk1(cur, i),
                                                   op0=ALU.mult, op1=ALU.add))
            return nc.vector.tensor_tensor(blk1(cur, i), blk1(cur, i), bias0[:], ALU.add)
        t0 = table0.rearrange("(r n) d -> n r d", r=R)
        project("l0", w0, [512] * 4 + [D], copied, 0,
                {0: to_ob(nc.scalar.copy, 0), 1: to_ob(nc.scalar.copy, 1), 2: to_ob(nc.scalar.copy, 2)},
                {3: to_ob(nc.vector.tensor_copy, 3), 4: self_part}, dve_links=1,
                ob=ob, table=lambda i: t0[bass.ds(i * P, P), :, :])

    def degrees():
        s = sem("degrees")
        c = ExitStack()
        root = sb("deg_root", [P, NBA], FP, c)
        has = sb("deg_has", [P, NBA], FP, c)
        r = sem("deg_rooted")
        with nc.Block() as block:
            @block.vector
            def _(dve):
                ch = Chain(dve, s)
                ch.link(nc.vector.tensor_copy(deg[:], agg[:, :, D:D + 1].rearrange("p b o -> p (b o)")))
                nc.vector.tensor_scalar(has[:], deg[:], 0.0, None, ALU.is_gt)
                ch.link(nc.vector.tensor_scalar(deg[:], deg[:], 1.0, None, ALU.max))
                ch.link(nc.vector.reciprocal(rdeg[:], deg[:]))
                dve.wait_ge(r, 1)
                ch.link(nc.vector.reciprocal(dinv[:], root[:]))
                ch.link(nc.vector.tensor_tensor(dinv[:], dinv[:], has[:], ALU.mult))

            @block.scalar
            def _(act):
                act.wait_ge(s, 2)
                nc.scalar.sqrt(root[:], deg[:]).then_inc(r, 1)
        c.close()

    def layer1_table():
        c = ExitStack()
        w = sb("wl", [P, 2, D], FP, c)
        ob = sb("ob1", [P, B, D], FP, c)
        load("wl", [(w[:], w_view(w_l))])

        def combine(ch, g):
            ch.done(nc.vector.scalar_tensor_tensor(out=grp(cur, g), in0=grp(agg, g), scalar=HALF, in1=grp(cur, g),
                                                   op0=ALU.mult, op1=ALU.add))
            yield
        row_stats("x1", combine, 1)
        project("l1", w, [D], normalised, 0, {0: lambda ch, i, u, b: nc.scalar.copy(ob[:, u, :], b)}, {},
                ob=ob, table=rows_of(tables[0]), keep=True)
        c.close()

    def layer1_end():
        c = ExitStack()
        w = sb("wr", [P, 2, D], FP, c)
        bl = sb("bl", [P, D], FP, c)
        gam = sb("gam", [P, D], FP, c)
        bet = sb("bet", [P, D], FP, c)
        tmp = sb("tmp1", [P, 2, G, D], FP, c)
        ss = sb("ss", [P, NBA], FP, c)
        mask = sb("row_mask", [P, P], FP, c)
        mu = sb("mu", [P, D], FP, c)
        load("wr", [(w[:], w_view(w_r)), (bl[:], b_l.partition_broadcast(P)), (gam[:], gamma.partition_broadcast(P)),
                    (bet[:], beta.partition_broadcast(P))])

        def mean_part(ch, i, u, b):
            a = blk1(agg, i)
            ch.link(nc.vector.scalar_tensor_tensor(out=a, in0=a, scalar=rdeg[:, bass.ds(i, 1)], in1=b,
                                                   op0=ALU.mult, op1=ALU.add))
            return nc.vector.tensor_tensor(a, a, bl[:], ALU.add)

        def square_sum(i, u):
            return nc.scalar.activation(tmp[:, 0, u, :], blk1(agg, i), ACT.Square, accum_out=ss[:, bass.ds(i, 1)])
        project("l1r", w, [D], copied, 0, {}, {0: mean_part}, dve_links=1, act_after=square_sum)

        root, s, mk = sem("len_root"), sem("len_chain"), sem("mask_made")
        with nc.Block() as block:
            @block.scalar
            def _(act):
                nc.scalar.sqrt(ss[:], ss[:]).then_inc(root, 1)

            @block.gpsimd
            def _(pool):
                nc.gpsimd.affine_select(out=mask[:], in_=ones[:], compare_op=ALU.is_gt, fill=0.0, base=LAST,
                                        pattern=[[0, P]], channel_multiplier=-1).then_inc(mk, 1)

            @block.vector
            def _(dve):
                ch = Chain(dve, s)
                dve.wait_ge(root, 1)
                ch.link(nc.vector.tensor_scalar(ss[:], ss[:], L2_EPS, None, ALU.max))
                ch.link(nc.vector.reciprocal(ss[:], ss[:]))
                dve.wait_ge(mk, 1)
                ch.link(nc.vector.tensor_tensor(ss[:, NB - 1:NB], ss[:, NB - 1:NB], mask[:, 0:1], ALU.mult))
                ch.link(nc.vector.memset(ss[:, NB:NBA], 0.0))

        ngr = NBA // G
        scaled, summed, mean_s = sem("rows_scaled"), sem("mean_summed"), sem("mean_chain")
        with nc.Block() as block:
            @block.vector
            def _(dve):
                with dve.Fori(0, ngr) as g:
                    nc.vector.tensor_tensor(grp(agg, g), grp(agg, g),
                                            ss[:, bass.ds(g * G, G)].unsqueeze(2).to_broadcast([P, G, D]),
                                            ALU.mult).then_inc(scaled, 1)
                dve.wait_ge(summed, 1)
                nc.vector.tensor_scalar(mu[:], ps[0][:, 0:D], 1.0 / N, None, ALU.mult).then_inc(mean_s, 1)

            @block.tensor
            def _(pe):
                def one(i, first, last):
                    return nc.tensor.matmul(ps[0][:, 0:D], ones[:], blk1(agg, i), start=first, stop=last)
                pe.wait_ge(scaled, 1)
                for j in range(G):
                    one(j, j == 0, False)
                with pe.Fori(1, ngr - 1) as g:
                    pe.wait_ge(scaled, g + 1)
                    for j in range(G):
                        one(g * G + j, False, False)
                pe.wait_ge(scaled, ngr)
                for j in range(G):
                    mm = one((ngr - 1) * G + j, False, j == G - 1)
                mm.then_inc(summed, 1)

        cent, sq, sqd, var_s, rt, vch = (sem(q) for q in ("centred", "squared", "sq_summed", "var_summed", "var_root", "var_chain"))
        with nc.Block() as block:
            @block.vector
            def _(dve):
                with dve.Fori(0, ngr) as g:
                    nc.vector.tensor_tensor(grp(agg, g), grp(agg, g), mu[:].unsqueeze(1).to_broadcast([P, G, D]),
                                            ALU.subtract).then_inc(cent, 1)
                ch = Chain(dve, vch)
                dve.wait_ge(var_s, 1)
                ch.link(nc.vector.tensor_scalar(mu[:], ps[0][:, 0:D], 1.0 / N, None, ALU.mult))
                dve.wait_ge(rt, 1)
                ch.link(nc.vector.reciprocal(mu[:], mu[:]))
                ch.link(nc.vector.tensor_tensor(gam[:], gam[:], mu[:], ALU.mult))

            @block.scalar
            def _(act):
                act.sem_inc(sqd, 2)
                with act.Fori(0, ngr // 2) as gg:
                    for u in range(2):
                        g = gg * 2 + u
                        act.wait_ge(cent, g + 1)
                        act.wait_ge(sqd, g + 1)
                        nc.scalar.square(tmp[:, u], grp(agg, g)).then_inc(sq, 1)
                act.wait_ge(vch, 1)
                nc.scalar.activation(mu[:], mu[:], ACT.Sqrt, bias=eps[:]).then_inc(rt, 1)

            @block.tensor
            def _(pe):
                def group(g, u, first=False, final=False):
                    pe.wait_ge(sq, g + 1)
                    for j in range(G - final):
                        last = final and j == G - 2
                        mm = nc.tensor.matmul(ps[0][:, 0:D], mask[:] if last else ones[:], tmp[:, u, j, :],
                                              start=first and j == 0, stop=last)
                    mm.then_inc(sqd, 1)
                    return mm
                group(0, 0, first=True)
                group(1, 1)
                with pe.Fori(1, ngr // 2 - 1) as gg:
                    group(gg * 2, 0)
                    group(gg * 2 + 1, 1)
                group(ngr - 2, 0)
                group(ngr - 1, 1, final=True)
                pe.wait_ge(sqd, 2 + ngr)
                pe.sem_inc(var_s, 1)

        def combine(ch, g):
            t = tmp[:, 0]
            ch.done(nc.vector.tensor_tensor(t, grp(agg, g), gam[:].unsqueeze(1).to_broadcast([P, G, D]), ALU.mult))
            yield
            ch.met()
            ch.done(nc.vector.tensor_tensor(t, t, bet[:].unsqueeze(1).to_broadcast([P, G, D]), ALU.add))
            yield
            ch.met()
            ch.done(nc.vector.scalar_tensor_tensor(out=grp(cur, g), in0=t, scalar=0.0, in1=grp(cur, g),
                                                   op0=ALU.max, op1=ALU.add))
        row_stats("x2", combine, 3)
        c.close()

    er_all = sb("er_all", [P, NBA, H], FP)
    er3 = sb("er3", [P, NBA, H, 3], BF)
    rden = sb("rden", [P, NBA, H], FP)

    def heads(a):
        return a.rearrange("p (h w) -> p h w", h=H)

    def gat_weights(c, n):
        w = sb(f"wg{n}", [P, 2, D + 2 * H], FP, c)
        av = sb(f"av{n}", [P, 2, D], FP, c)
        t = sb(f"avt{n}", [P, 2, D], FP, c)
        load(f"wg{n}", [(w[:, :, 0:D], w_view(gat_w[n])),
                        (av[:, 0, :], gat_al[n].rearrange("h d -> (h d)").partition_broadcast(P)),
                        (av[:, 1, :], gat_ar[n].rearrange("h d -> (h d)").partition_broadcast(P))])
        s = sem(f"wgchain{n}")
        with nc.Block() as block:
            @block.vector
            def _(dve):
                ch = Chain(dve, s)
                for q in range(2):
                    ch.link(nc.vector.tensor_tensor(t[:], w[:, :, 0:D], av[:, q:q + 1, :].to_broadcast([P, 2, D]), ALU.mult))
                    for k in range(2):
                        ch.link(nc.vector.tensor_reduce(w[:, k, D + q * H:D + (q + 1) * H], heads(t[:, k, :]),
                                                        op=ALU.add, axis=AX.X))
        return w

    def gat_table(c, n, fill, fill_links, table, act_copy=None):
        w = gat_weights(c, n)
        ob = sb(f"obg{n}", [P, B, W4], FP, c)

        def head_rows(ch, i, u, b):
            nc.scalar.copy(heads(ob[:, u, :])[:, :, 0:DH], heads(b[:, 0:D]))
            nc.scalar.copy(heads(ob[:, u, :])[:, :, DH:DH + 1].rearrange("p h o -> p (h o)"), b[:, D:D + H])
            return nc.scalar.copy(er_all[:, bass.ds(i, 1), :].rearrange("p o h -> p (o h)"), b[:, D + H:D + 2 * H])
        project(f"g{n}", w, [D + 2 * H], fill, fill_links, {0: head_rows}, {}, ob=ob, table=rows_of(table), keep=True, act_copy=act_copy)
        r = sb(f"er_rest{n}", [P, NBA, H], FP, c)
        s = sem(f"er_chain{n}")
        with nc.Block() as block:
            @block.vector
            def _(dve):
                ch = Chain(dve, s)
                part = lambda q: er3[:, :, :, q:q + 1].rearrange("p b h o -> p b (h o)")
                ch.link(nc.vector.tensor_copy(part(0), er_all[:]))
                ch.link(nc.vector.tensor_tensor(r[:], er_all[:], part(0), ALU.subtract))
                ch.link(nc.vector.tensor_copy(part(1), r[:]))
                ch.link(nc.vector.tensor_tensor(r[:], r[:], part(1), ALU.subtract))
                ch.link(nc.vector.tensor_copy(part(2), r[:]))

    def aggregate_gat(name, table, beside=None):
        c = ExitStack()
        rows = sb(f"rows_{name}", [P, NBUF, U, W4], FP, c)
        hot = sb(f"hot_{name}", [P, 2, U, P], FP, c)
        hot_t = sb(f"hott_{name}", [P, 2, U * P], BF, c)
        dst_t = sb(f"dstt_{name}", [P, 2, U * P], BF, c)
        starts = sb(f"starts_{name}", [H, 2, U * P], BF, c)
        ends = sb(f"ends_{name}", [H, 2, U * P], BF, c)
        fwd = sb(f"fwd_{name}", [H, 2, U * P], FP, c)
        back = sb(f"back_{name}", [H, U * P], FP, c)
        el = sb(f"el_{name}", [P, 2, U, H], FP, c)
        er = sb(f"er_{name}", [P, U + 1, H], FP, c)
        z = sb(f"z_{name}", [P, 2, U + 1, H], FP, c)
        ex = sb(f"ex_{name}", [P, NBUF, U + 1, H], FP, c)
        am = sb(f"am_{name}", [1, H], FP, c)
        fac = sb(f"fac_{name}", [P, H], FP, c)
        stage = sb(f"stage_{name}", [P, NBUF, U], I32, c)
        moved = sem(f"moved_{name}")
        names = ("pair", "added", "hot", "hott", "el", "elt", "er", "fwd", "back", "backt", "zr", "ex", "am", "fac",
                 "rescaled", "scaled", "scaledd", "erread", "zchain", "half", "weightsin", "facread")
        (pair_done, added, hot_ready, hott_ready, el_ready, elt_done, er_done, fwd_done, back_done, backt_done, z_ready,
         ex_ready, am_ready, fac_done, rescaled, scaled, scaled_d, er_read, zch, half, weights_in, fac_read) = (sem(f"{q}_{name}") for q in names)
        staged = [sem(f"staged_{name}{u}") for u in range(NBUF)]
        flags = [sem(f"flags_{name}{u}") for u in range(2)]
        base = list(used)
        for u in range(NBUF):
            used[u] += full_iters + (u < left)
        credit = NBUF * U // 2
        el_t = [ps[4], ps[5]]
        er_bank, misc = ps[6], ps[7]
        HU = U // 2
        back_t = misc[:, 0:(U + 2) * H].rearrange("p (s h) -> p s h", h=H)
        by_act = 3
        order = [*range(by_act, HU), *range(by_act)]
        fac_place = 2
        fac_bank = ps[order[fac_place]][:, 512 - H:512]

        def three_batches(eng, first, step):
            assert left >= 2
            first(0, 0)
            step((0, 1), (0, 0), None)
            with eng.Fori(0, full_iters) as i:
                for u in range(NBUF):
                    step(nxt(*nxt(i, u)), nxt(i, u), (i, u))
            for u in range(left):
                step(*((full_iters, u + d) if u + d < left else None for d in (2, 1, 0)))

        with nc.Block() as block:
            @block.gpsimd
            def _(pool):
                nc.gpsimd.memset(hot[:], 0.0).then_inc(pair_done, credit)
                gather_batches(pool, rows, W4, table, stage, staged, pair_done, order)

            @block.sync
            def _(sp):
                sp.sem_inc(back_done, 2)
                sp.sem_inc(hott_ready, 2)

                def batch(i, u, reused=True):
                    k = i * NBUF + u
                    if reused:
                        for j in range(U):
                            sp.wait_ge(slot_full[u * U + j], i * 16 + 16 * base[u])
                    sp.dma_start(stage[:, u, :], rows_src[:, bass.ds(k * U, U)]).then_inc(staged[u], 16)
                    sp.wait_ge(hott_ready, k + 1)
                    sp.wait_ge(back_done, k + 1)
                    for to, of, n in ((dst_t, dloc_dram, P), (starts, starts_dram, H), (ends, ends_dram, H)):
                        sp.dma_start(to[:, u % 2, :], of[bass.ds(k * U, U), :].rearrange("s e -> (s e)")
                                     .partition_broadcast(n)).then_inc(flags[u % 2], 16)
                for u in range(NBUF):
                    batch(0, u, reused=False)
                with sp.Fori(1, full_iters) as i:
                    for u in range(NBUF):
                        batch(i, u)
                for u in range(left):
                    batch(full_iters, u)

            @block.vector
            def _(dve):
                nc.vector.memset(agg[:], 0.0).then_inc(added, credit + 1)
                dve.sem_inc(zch, credit)
                nc.vector.memset(fwd[:], -BIG).then_inc(fwd_done, 1)
                dve.wait_ge(pair_done, credit)
                dve.sem_inc(elt_done, 1)
                dve.sem_inc(er_done, 2)
                dve.sem_inc(backt_done, 2)
                dve.sem_inc(ex_ready, 1)
                dve.sem_inc(fac_done, 1)

                def logit_parts(i, u):
                    k = i * NBUF + u
                    for j in range(U):
                        dve.wait_ge(slot_full[u * U + j], i * 16 + 16 * (base[u] + 1))
                    dve.wait_ge(elt_done, k + 1)
                    nc.vector.tensor_tensor(
                        el[:, u % 2], rows[:, u, :, :].rearrange("p s (h w) -> p s h w", h=H)[:, :, :, DH:DH + 1]
                        .rearrange("p s h o -> p s (h o)"),
                        mneg[:, bass.ds(k * U, U)].unsqueeze(2).to_broadcast([P, U, H]), ALU.add).then_inc(el_ready, 1)
                    dve.wait_ge(flags[u % 2], i * (48 * NBUF // 2) + 48 * (u // 2 + 1))
                    dve.wait_ge(er_done, k + 1)
                    nc.vector.tensor_scalar(hot_t[:, u % 2, :], dst_t[:, u % 2, :], iota_p[:], None,
                                            ALU.is_equal).then_inc(hott_ready, 1)

                def one_hots(i, u):
                    k = i * NBUF + u
                    dve.wait_ge(pair_done, k * HU + (credit - HU))
                    nc.vector.tensor_tensor(
                        hot[:, u % 2, :, :], iota_f[:].unsqueeze(1).to_broadcast([P, U, P]),
                        dloc[:, bass.ds(k * U, U)].unsqueeze(2).to_broadcast([P, U, P]),
                        ALU.is_equal).then_inc(hot_ready, 1)

                def forward(i, u):
                    k, v = i * NBUF + u, u % 2
                    dve.wait_ge(elt_done, k + 2)
                    dve.wait_ge(fwd_done, k + 1)
                    dve.wait_ge(backt_done, k + 2)
                    nc.vector.tensor_tensor_scan(fwd[:, v, 0:HU * P], starts[:, v, 0:HU * P], el_t[0][0:H, 0:HU * P],
                                                 fwd[:, 1 - v, U * P - 1:U * P], ALU.add, ALU.max).then_inc(half, 1)
                    dve.wait_ge(half, k + 1)
                    nc.vector.tensor_tensor_scan(fwd[:, v, HU * P:], starts[:, v, HU * P:], el_t[1][0:H, 0:HU * P],
                                                 fwd[:, v, HU * P - 1:HU * P], ALU.add, ALU.max).then_inc(fwd_done, 1)

                def backward(i, u):
                    k, v = i * NBUF + u, u % 2
                    dve.wait_ge(fwd_done, k + 2)
                    dve.wait_ge(backt_done, k + 2)
                    nc.vector.tensor_tensor_scan(back[:, ::-1], ends[:, v, ::-1], fwd[:, v, ::-1], -BIG,
                                                 ALU.add, ALU.max).then_inc(back_done, 1)

                def logits(i, u):
                    k = i * NBUF + u
                    ch = Chain(dve, zch, k * 4 + credit)
                    dve.wait_ge(er_done, k + 3)
                    ch.link(nc.vector.tensor_reduce(er[:], er_bank[:, 0:(U + 1) * H * 3]
                                                    .rearrange("p (s h q) -> p s h q", h=H, q=3), op=ALU.add, axis=AX.X))
                    yield
                    dve.wait_ge(ex_ready, k + 1)
                    nc.vector.tensor_tensor(z[:, 0, 0:U, :], el[:, u % 2], er[:, 0:U, :], ALU.add).then_inc(er_read, 1)
                    dve.wait_ge(backt_done, k + 3)
                    nc.vector.tensor_tensor(z[:, 1, :, :], back_t[:, 0:U + 1, :], er[:], ALU.add)
                    nc.vector.tensor_tensor(z[:, 0, U, :], back_t[:, U + 1, :], er[:, U, :], ALU.add).then_inc(zch, 1)
                    ch.n += 1
                    yield
                    dve.wait_ge(zch, ch.at + 2)
                    flat = z[:].rearrange("p a s h -> p (a s h)")
                    nc.vector.scalar_tensor_tensor(out=flat, in0=flat, scalar=0.2, in1=flat, op0=ALU.mult,
                                                   op1=ALU.max).then_inc(zch, 1)
                    yield
                    dve.wait_ge(zch, ch.at + 3)
                    nc.vector.tensor_tensor(z[:, 0], z[:, 0], z[:, 1], ALU.subtract).then_inc(zch, 1)
                    yield
                    dve.wait_ge(zch, ch.at + 4)
                    nc.vector.tensor_scalar(z[:, 0], z[:, 0], 0.0, None, ALU.min).then_inc(z_ready, 1)

                def growth(i, u):
                    k = i * NBUF + u
                    dve.wait_ge(ex_ready, k + 2)
                    dve.wait_ge(fac_done, k + 1)
                    nc.vector.tensor_scalar(am[:], ex[0:1, u, U, :], -1.0, cont[:, bass.ds(k, 1)],
                                            ALU.add, ALU.mult).then_inc(am_ready, 1)

                def weigh(i, u):
                    for j in range(by_act, HU):
                        a = rows[:, u, 2 * j:2 * j + 2, :].rearrange("p s (h w) -> p (s h) w", h=H)[:, :, 0:DH]
                        w = ex[:, u, 2 * j:2 * j + 2, :].rearrange("p s h -> p (s h)")
                        nc.vector.tensor_tensor(a, a, w.unsqueeze(2).to_broadcast([P, 2 * H, DH]),
                                                ALU.mult).then_inc(scaled_d, 1)

                def factors(i, u):
                    dve.wait_ge(fac_done, i * NBUF + (u + 2))
                    nc.vector.tensor_scalar(fac[:], fac_bank, 1.0, None, ALU.add).then_inc(fac_read, 1)

                def rescale(i, u, blocks):
                    k = i * NBUF + u
                    dve.wait_ge(added, k * HU + (credit + 1))
                    dve.wait_ge(fac_read, k + 2)
                    acc = agg[:, bass.ds(blocks[0], 1), :].rearrange("p o (h w) -> p (o h) w", h=H)
                    nc.vector.tensor_tensor(acc, acc, fac[:].unsqueeze(2).to_broadcast([P, H, W4 // H]),
                                            ALU.mult).then_inc(rescaled, 1)

                def accumulate(i, u, blocks, q):
                    k = i * NBUF + u
                    j = order[q]
                    if q == 0:
                        dve.wait_ge(rescaled, k + 1)
                    dve.wait_ge(pair_done, k * HU + (credit + q + 1))
                    dve.wait_ge(added, k * HU + (credit + q + 1))
                    acc = agg[:, bass.ds(blocks[j], 1), :].rearrange("p o w -> p (o w)")
                    nc.vector.tensor_tensor(acc, acc, ps[j][:, 0:W4], ALU.add).then_inc(added, 1)

                def step(after, nx, this):
                    if this:
                        growth(*this)
                        weigh(*this)
                    if nx:
                        forward(*nx)
                    if this:
                        blocks = pair_blocks(dve, this[0] * NBUF + this[1])
                        factors(*this)
                    if nx:
                        backward(*nx)
                    if after:
                        logit_parts(*after)
                    if this:
                        rescale(*this, blocks)
                    if nx:
                        one_hots(*nx)
                    if this:
                        for b in blocks[::-1]:
                            dve.compute_val(b)
                    links = logits(*nx) if nx else iter(())
                    for q in range(HU - 1):
                        next(links, None)
                        if this:
                            accumulate(*this, blocks, q)
                    next(links, None)
                    next(links, None)
                    if this:
                        accumulate(*this, blocks, HU - 1)
                dve.sem_inc(fac_read, 1)
                three_batches(dve, logit_parts, step)

            @block.scalar
            def _(act):
                if beside:
                    act.dma_start(*beside).then_inc(moved, 16)
                act.sem_inc(er_read, 1)
                act.sem_inc(z_ready, 1)
                act.sem_inc(am_ready, NBUF)

                def batch(i, u):
                    k = i * NBUF + u
                    act.wait_ge(z_ready, k + 2)
                    act.wait_ge(am_ready, k + 1)
                    nc.scalar.activation(ex[:, u], z[:, 0], ACT.Exp).then_inc(ex_ready, 1)
                    act.wait_ge(ex_ready, k + 2)
                    by_head = rows[:, u, :, :].rearrange("p s (h w) -> p s h w", h=H)
                    nc.scalar.copy(by_head[:, :, :, DH:DH + 1].rearrange("p s h o -> p s (h o)"),
                                   ex[:, u, 0:U, :]).then_inc(weights_in, 1)
                    for s in range(2 * by_act):
                        for h in range(H):
                            a = by_head[:, s, h, 0:DH]
                            ins = nc.scalar.mul(a, a, ex[:, u, s, h:h + 1])
                        if s % 2:
                            ins.then_inc(scaled, 1)
                each_batch(act, batch)
                if beside:
                    act.wait_ge(moved, 16)

            @block.tensor
            def _(pe):
                def turn(i, u):
                    k = i * NBUF + u
                    pe.wait_ge(el_ready, k + 1)
                    pe.wait_ge(fwd_done, k + 1)
                    for s in range(U):
                        ins = nc.tensor.transpose(el_t[s // HU][0:H, (s % HU) * P:(s % HU + 1) * P], el[:, u % 2, s, :], ident[:])
                    ins.then_inc(elt_done, 1)

                def er_of_edges(i, u, blocks):
                    k = i * NBUF + u
                    pe.wait_ge(hott_ready, k + 3)
                    pe.wait_ge(er_read, k + 1)
                    for place, s in enumerate([*range(U), 0]):
                        ins = nc.tensor.matmul(er_bank[:, place * 3 * H:(place + 1) * 3 * H],
                                               hot_t[:, u % 2, s * P:(s + 1) * P],
                                               er3[:, bass.ds(blocks[s // 2], 1), :, :].rearrange("p o h q -> p (o h q)"),
                                               start=True, stop=True)
                    ins.then_inc(er_done, 1)

                def factor(i, u):
                    k = i * NBUF + u
                    pe.wait_ge(am_ready, k + (NBUF + 1))
                    pe.wait_ge(hot_ready, k + 1)
                    pe.wait_ge(fac_read, k + 1)
                    pe.wait_ge(added, k * HU + (credit - HU + 1 + fac_place + 1))
                    nc.tensor.matmul(fac_bank, hot[0:1, u % 2, 0, :], am[:], start=True, stop=True).then_inc(fac_done, 1)

                def turn_back(i, u):
                    k = i * NBUF + u
                    pe.wait_ge(back_done, k + 3)
                    wait_apart(pe, z_ready, k + 1, waits_met)
                    for place, s in enumerate([*range(U), 0]):
                        nc.tensor.transpose(back_t[:, place, :], back[:, s * P:(s + 1) * P], ident[0:H, 0:H])
                    prev = fwd[:, (u - 1) % 2, U * P - 1:U * P]
                    nc.tensor.matmul(back_t[:, U + 1, :], prev.to_broadcast([H, P]), ident[0:H, 0:H],
                                     start=True, stop=True).then_inc(backt_done, 1)

                def sums(i, u, places):
                    k = i * NBUF + u
                    for q in places:
                        j = order[q]
                        if j < by_act:
                            pe.wait_ge(scaled, k * by_act + (j + 1))
                        else:
                            pe.wait_ge(weights_in, k + 1)
                            pe.wait_ge(scaled_d, k * (HU - by_act) + (j + 1 - by_act))
                        pe.wait_ge(added, k * HU + (credit - HU + 2 + q))
                        if q == fac_place:
                            pe.wait_ge(fac_read, k + 2)
                        for s in (2 * j, 2 * j + 1):
                            mm = nc.tensor.matmul(ps[j][:, 0:W4], hot[:, u % 2, s, :], rows[:, u, s, :],
                                                  start=s % 2 == 0, stop=s % 2 == 1)
                        mm.then_inc(pair_done, 1)

                def first(i, u):
                    turn(i, u)
                    er_of_edges(i, u, pair_blocks(pe, i * NBUF + u))

                def step(after, nx, this):
                    if this:
                        factor(*this)
                        sums(*this, (0, 1))
                    if nx:
                        turn_back(*nx)
                    if after:
                        blocks = pair_blocks(pe, after[0] * NBUF + after[1])
                    if this:
                        sums(*this, (2, 3))
                    if after:
                        turn(*after)
                        er_of_edges(*after, blocks)
                three_batches(pe, first, step)
        c.close()

    def gat_fill(ch, i, nb):
        a = agg[:, bass.ds(i, 1), :].rearrange("p o (h w) -> p (o h) w", h=H)[:, :, 0:DH]
        ch.link(nc.vector.tensor_tensor(heads(nb), a, rden[:, bass.ds(i, 1), :].rearrange("p o h -> p (o h)")
                                        .unsqueeze(2).to_broadcast([P, H, DH]), ALU.mult))
        return nc.vector.tensor_tensor(nb, nb, blk1(cur, i), ALU.add)

    def relu(out_, in_):
        return nc.scalar.activation(out_, in_, ACT.Relu)

    def weight_sums(n):
        s = sem(f"rden{n}")
        with nc.Block() as block:
            @block.vector
            def _(dve):
                ch = Chain(dve, s)
                den = agg[:].rearrange("p b (h w) -> p b h w", h=H)[:, :, :, DH:DH + 1].rearrange("p b h o -> p b (h o)")
                ch.link(nc.vector.tensor_scalar(rden[:], den, 1e-9, None, ALU.max))
                ch.link(nc.vector.reciprocal(rden[:], rden[:]))

    def layer2():
        for n in range(3):
            c = ExitStack()
            if n:
                weight_sums(n)
                gat_table(c, n, gat_fill, 1, tables[1 + n], relu)
            else:
                gat_table(c, n, normalised, 0, tables[1])
            c.close()
            clear_sems()
            x2 = x2_dram.rearrange("(b p) d -> p b d", p=P)
            aggregate_gat(f"a{2 + n}", tables[1 + n], ((x2, cur[:]), None, (cur[:], x2))[n])
            clear_sems()
        weight_sums(3)
        c = ExitStack()
        t = sb("h3", [P, G, D], FP, c)

        def combine(ch, g):
            by_head = agg[:, bass.ds(g * G, G), :].rearrange("p b (h w) -> p (b h) w", h=H)[:, :, 0:DH]
            ch.done(nc.vector.tensor_tensor(t[:].rearrange("p b (h w) -> p (b h) w", h=H), by_head,
                                            rden[:, bass.ds(g * G, G), :].rearrange("p b h -> p (b h)").unsqueeze(2)
                                            .to_broadcast([P, G * H, DH]), ALU.mult))
            yield
            ch.met()
            ch.done(nc.vector.scalar_tensor_tensor(out=grp(cur, g), in0=t[:], scalar=0.0, in1=grp(cur, g),
                                                   op0=ALU.max, op1=ALU.add))
        row_stats("x3", combine, 2)
        c.close()
        clear_sems()

    def layer3():
        c = ExitStack()
        w = sb("w3s", [P, 2, D], FP, c)
        ob = sb("ob5", [P, B, D], FP, c)
        load("w3", [(w[:], w_view(w3))])
        project("l3", w, [D], normalised, 0,
                {0: lambda ch, i, u, b: nc.scalar.mul(ob[:, u, :], b, dinv[:, bass.ds(i, 1)])}, {},
                ob=ob, table=rows_of(tables[4]), keep=True)
        c.close()
        clear_sems()
        aggregate("a5", tables[4], rows_src, False)
        clear_sems()

        def combine(ch, g):
            ch.done(nc.vector.tensor_tensor(grp(agg, g), grp(agg, g), dinv[:, bass.ds(g * G, G)].unsqueeze(2)
                                            .to_broadcast([P, G, D]), ALU.mult))
            yield
            ch.met()
            ch.done(nc.vector.tensor_tensor(grp(cur, g), grp(cur, g), grp(agg, g), ALU.add))
        row_stats("x4", combine, 2)

    def store_out():
        ready, so = sem("out_ready"), sem("out_stored")
        with nc.Block() as block:
            @block.vector
            def _(dve):
                with dve.Fori(0, NB) as i:
                    normalised(None, i, blk1(cur, i)).then_inc(ready, 1)

            @block.sync
            def _(sp):
                with sp.Fori(0, NB - 1) as i:
                    sp.wait_ge(ready, i + 1)
                    sp.dma_start(out[bass.ds(i * P, P), :], blk1(cur, i)).then_inc(so, 16)
                sp.wait_ge(ready, NB)
                sp.dma_start(out[(NB - 1) * P:N, :], cur[0:LAST, NB - 1, :]).then_inc(so, 16)
                sp.wait_ge(so, 16 * NB)

    c0 = ExitStack()
    w0 = sb("w0", [P, 2, (R + 1) * D], FP, c0)
    bias0 = sb("bias0", [P, D], FP, c0)
    x_loaded = nc.alloc_semaphore(name="x_loaded")
    zero = sem("cur_cleared")
    with nc.Block() as block:
        @block.gpsimd
        def _(pool):
            nc.gpsimd.memset(cur[:, NB - 1:NBA, :], 0.0).then_inc(zero, 1)

        @block.scalar
        def _(act):
            act.wait_ge(zero, 1)
            for to, of in [(cur[:, 0:NB - 1, :], x[0:(NB - 1) * P, :].rearrange("(b p) d -> p b d", p=P)),
                           (cur[0:LAST, NB - 1, :], x[(NB - 1) * P:N, :]),
                           (bias0[:], h_bias.partition_broadcast(P)),
                           (w0[:, :, R * D:], w_view(w_loop))] + [
                               (w0[:, :, r * D:(r + 1) * D], w_view(w_rel[r])) for r in range(R)]:
                act.dma_start(to, of).then_inc(x_loaded, 16)
    c = ExitStack()
    make_steps(c, raw_edges(c))
    c.close()
    clear_sems()
    layer0()
    c0.close()
    clear_sems()
    aggregate("a0", table0, row0, True)
    clear_sems()
    degrees()
    layer1_table()
    clear_sems()
    aggregate("a1", tables[0], rows_src, False)
    clear_sems()
    layer1_end()
    clear_sems()
    layer2()
    layer3()
    store_out()
    ctx.close()


def kernel(x, src, dst, edge_type_8, L0_gnn_weight, L0_gnn_h_bias, L0_gnn_loop_weight, L1_gnn_W_l, L1_gnn_b_l,
           L1_gnn_W_r, L1_gnn_gamma, L1_gnn_beta, L2_gnn_W0, L2_gnn_al0, L2_gnn_ar0, L2_gnn_W1, L2_gnn_al1,
           L2_gnn_ar1, L2_gnn_W2, L2_gnn_al2, L2_gnn_ar2, L3_gnn_W):
    import numpy as np
    import concourse.bacc as bacc
    from concourse import mybir as mb
    from concourse.bass_utils import run_bass_kernel_spmd

    nc = bacc.Bacc("TRN2", target_bir_lowering=False, num_devices=1)
    arrays = {}

    def given(name, a):
        a = np.ascontiguousarray(a)
        arrays[name] = a
        return nc.dram_tensor(name, a.shape, mb.dt.from_np(a.dtype), kind="ExternalInput").ap()

    args = [given("in_x", x), given("in_src", src), given("in_dst", dst), given("in_type", edge_type_8),
            given("in_w_rel", L0_gnn_weight), given("in_h_bias", L0_gnn_h_bias), given("in_w_loop", L0_gnn_loop_weight),
            given("in_w_l", np.asarray(L1_gnn_W_l).T), given("in_b_l", L1_gnn_b_l), given("in_w_r", np.asarray(L1_gnn_W_r).T),
            given("in_gamma", L1_gnn_gamma), given("in_beta", L1_gnn_beta),
            [given(f"in_gat_w{i}", a) for i, a in enumerate((L2_gnn_W0, L2_gnn_W1, L2_gnn_W2))],
            [given(f"in_gat_al{i}", a) for i, a in enumerate((L2_gnn_al0, L2_gnn_al1, L2_gnn_al2))],
            [given(f"in_gat_ar{i}", a) for i, a in enumerate((L2_gnn_ar0, L2_gnn_ar1, L2_gnn_ar2))],
            given("in_w3", L3_gnn_W)]
    out = nc.dram_tensor("out_0_dram", (N, D), FP, kind="ExternalOutput").ap()
    build(nc, *args, out)
    r = run_bass_kernel_spmd(nc, [arrays], core_ids=[0])
    return r.results[0]["out_0_dram"]
```
